# Optimizing a Trainium2 kernel written in Bass

```python
import numpy as np
import jax
import jax.numpy as jnp

def _softmax(x, axis=-1):
    return jax.nn.softmax(x, axis=axis)

def _gelu(x):
    return jax.nn.gelu(x, approximate=True)

def _silu(x):
    return jax.nn.silu(x)

def _sigmoid(x):
    return jax.nn.sigmoid(x)

def _layernorm(x, axis=-1, eps=1e-05):
    m = jnp.mean(x, axis=axis, keepdims=True)
    v = jnp.var(x, axis=axis, keepdims=True)
    return (x - m) / jnp.sqrt(v + eps)

def _scatter_add(tgt, idx, src, axis=0):
    return tgt.at[idx].add(src)

def _segment_sum(src, seg, n):
    return jax.ops.segment_sum(src, seg, n)
kernel_name = 'mk_gnn_preln_d2_gnn_r64_76b543'

def setup_inputs(seed: int=0):
    np.random.seed(seed)
    _w = jnp.asarray

    def _rec_inputs():
        import jax
        import jax.numpy as jnp
        _gk = jax.random.key(seed)
        x = 0.0007357 + 1 * jax.random.normal(jax.random.fold_in(_gk, 1), (50000, 256), jnp.float32)
        src = jax.random.randint(jax.random.fold_in(_gk, 2), (12500,), 0, 50000, jnp.int32)
        dst = jnp.minimum((50000 * jax.random.uniform(jax.random.fold_in(_gk, 3), (12500,)) ** 2.0).astype(jnp.int32), 49999)
        _o = jnp.argsort(dst, stable=True)
        src = src[_o]
        dst = dst[_o]
        edge_attr_16 = -0.000153872 + 1.00011 * jax.random.normal(jax.random.fold_in(_gk, 12), (12500, 16), jnp.float32)
        edge_attr_4 = 0.0007022 + 0.999661 * jax.random.normal(jax.random.fold_in(_gk, 13), (12500, 4), jnp.float32)
        return (x, src, dst, edge_attr_16, edge_attr_4)
    x, src, dst, edge_attr_16, edge_attr_4 = _rec_inputs()

    def _L0_gnn_setup():
        import jax, jax.numpy as jnp
        import numpy as np
        N_NODES = 10000
        N_EDGES = 5000
        D_IN = 256
        D_OUT = 256
        key = jax.random.key(seed)
        k1, k2, k3, k4, k5 = jax.random.split(key, 5)
        row = jax.random.randint(k1, (N_EDGES,), 0, N_NODES, dtype=jnp.int32)
        col = jax.random.randint(k2, (N_EDGES,), 0, N_NODES, dtype=jnp.int32)
        X = jax.random.normal(k3, (N_NODES, D_IN), dtype=jnp.float32)
        W = jax.random.normal(k4, (D_IN, D_OUT), dtype=jnp.float32) * (1.0 / np.sqrt(D_IN))
        b = jax.random.normal(k5, (D_OUT,), dtype=jnp.float32) * 0.01
        return {'row': row, 'col': col, 'X': X, 'W': W, 'b': b}
    _L0_gnn_all = _L0_gnn_setup()
    _L0_gnn_in = {k: v for k, v in _L0_gnn_all.items() if k in ('W', 'b')}
    del _L0_gnn_all

    def _L1_gnn_setup():
        import jax, jax.numpy as jnp
        import numpy as np
        N, E, C, R, HID = (50000, 500000, 64, 16, 64)
        key = jax.random.key(seed)
        ks = jax.random.split(key, 24)
        g = lambda k, shape, s=1.0: jax.random.normal(k, shape, dtype=jnp.float32) * s
        cs = C ** (-0.5)
        inp = {'h': g(ks[0], (N, 4 * C)), 'edge_index': jax.random.randint(ks[1], (2, E), 0, N), 'edge_sh': g(ks[2], (E, 4)), 'edge_rbf': g(ks[3], (E, R)), 'W_up0': g(ks[4], (C, C), cs), 'W_up1': g(ks[5], (C, C), cs), 'M1': g(ks[6], (R, HID), R ** (-0.5)), 'M2': g(ks[7], (HID, HID), HID ** (-0.5)), 'M3': g(ks[8], (HID, HID), HID ** (-0.5)), 'M4': g(ks[9], (HID, 4 * C), HID ** (-0.5)), 'W_lin0': g(ks[10], (C, C), cs), 'W_lin1': g(ks[11], (C, C), cs), 'Wsc0': g(ks[12], (C, C), cs), 'Wsc1': g(ks[13], (C, C), cs), 'Wc0': g(ks[14], (C, 5)), 'Wc1': g(ks[15], (C, 4)), 'WB0': g(ks[16], (C, C), cs), 'WB1': g(ks[17], (C, C), cs), 'gamma0': jnp.ones((C,), jnp.float32), 'beta0': jnp.zeros((C,), jnp.float32), 'gamma1': jnp.ones((C,), jnp.float32)}
        return inp
    _L1_gnn_all = _L1_gnn_setup()
    _L1_gnn_in = {k: v for k, v in _L1_gnn_all.items() if k in ('W_up0', 'W_up1', 'M1', 'M2', 'M3', 'M4', 'W_lin0', 'W_lin1', 'Wsc0', 'Wsc1', 'Wc0', 'Wc1', 'WB0', 'WB1', 'gamma0', 'beta0', 'gamma1')}
    del _L1_gnn_all
    return {'x': x, 'src': src, 'dst': dst, 'edge_attr_16': edge_attr_16, 'edge_attr_4': edge_attr_4, 'L0_gnn_W': _L0_gnn_in['W'], 'L0_gnn_b': _L0_gnn_in['b'], 'L1_gnn_W_up0': _L1_gnn_in['W_up0'], 'L1_gnn_W_up1': _L1_gnn_in['W_up1'], 'L1_gnn_M1': _L1_gnn_in['M1'], 'L1_gnn_M2': _L1_gnn_in['M2'], 'L1_gnn_M3': _L1_gnn_in['M3'], 'L1_gnn_M4': _L1_gnn_in['M4'], 'L1_gnn_W_lin0': _L1_gnn_in['W_lin0'], 'L1_gnn_W_lin1': _L1_gnn_in['W_lin1'], 'L1_gnn_Wsc0': _L1_gnn_in['Wsc0'], 'L1_gnn_Wsc1': _L1_gnn_in['Wsc1'], 'L1_gnn_Wc0': _L1_gnn_in['Wc0'], 'L1_gnn_Wc1': _L1_gnn_in['Wc1'], 'L1_gnn_WB0': _L1_gnn_in['WB0'], 'L1_gnn_WB1': _L1_gnn_in['WB1'], 'L1_gnn_gamma0': _L1_gnn_in['gamma0'], 'L1_gnn_beta0': _L1_gnn_in['beta0'], 'L1_gnn_gamma1': _L1_gnn_in['gamma1']}

def reference(x, src, dst, edge_attr_16, edge_attr_4, L0_gnn_W, L0_gnn_b, L1_gnn_W_up0, L1_gnn_W_up1, L1_gnn_M1, L1_gnn_M2, L1_gnn_M3, L1_gnn_M4, L1_gnn_W_lin0, L1_gnn_W_lin1, L1_gnn_Wsc0, L1_gnn_Wsc1, L1_gnn_Wc0, L1_gnn_Wc1, L1_gnn_WB0, L1_gnn_WB1, L1_gnn_gamma0, L1_gnn_beta0, L1_gnn_gamma1):
    import jax
    import jax.numpy as jnp

    def _L0_gnn_ref(row, col, X, W, b):
        import jax, jax.numpy as jnp
        import numpy as np
        N_NODES = 10000
        N_EDGES = 5000
        D_IN = 256
        D_OUT = 256
        N = X.shape[0]
        E = row.shape[0]
        deg = 1.0 + jax.ops.segment_sum(jnp.ones((E,), X.dtype), col, num_segments=N)
        dinv = jax.lax.rsqrt(deg)
        XW = X @ W + b
        scaled = XW * dinv[:, None]
        msg = jax.ops.segment_sum(scaled[col], row, num_segments=N)
        out = (msg + scaled) * dinv[:, None]
        return out

    def _L1_gnn_ref(h, edge_index, edge_sh, edge_rbf, W_up0, W_up1, M1, M2, M3, M4, W_lin0, W_lin1, Wsc0, Wsc1, Wc0, Wc1, WB0, WB1, gamma0, beta0, gamma1):
        import jax, jax.numpy as jnp
        import numpy as np
        N, E, C, R, HID = (50000, 500000, 64, 16, 64)
        n = h.shape[0]
        h0 = h[:, :C]
        h1 = h[:, C:].reshape(n, C, 3)
        up0 = h0 @ W_up0
        up1 = jnp.einsum('ncx,cd->ndx', h1, W_up1)
        r = jax.nn.silu(edge_rbf @ M1)
        r = jax.nn.silu(r @ M2)
        r = jax.nn.silu(r @ M3)
        tpw = (r @ M4).reshape(-1, 4, C)
        snd, rcv = (edge_index[0], edge_index[1])
        x0 = up0[snd]
        x1 = up1[snd]
        sh0 = edge_sh[:, 0]
        sh1 = edge_sh[:, 1:]
        inv3 = 1.0 / jnp.sqrt(jnp.float32(3.0))
        m0e = tpw[:, 0] * x0 * sh0[:, None] + tpw[:, 3] * jnp.einsum('ecx,ex->ec', x1, sh1) * inv3
        m1e = tpw[:, 1][:, :, None] * x0[:, :, None] * sh1[:, None, :] + tpw[:, 2][:, :, None] * x1 * sh0[:, None, None]
        msg0 = jax.ops.segment_sum(m0e, rcv, num_segments=n)
        msg1 = jax.ops.segment_sum(m1e, rcv, num_segments=n)
        A0 = msg0 @ W_lin0
        A1 = jnp.einsum('ncx,cd->ndx', msg1, W_lin1)
        sc0 = h0 @ Wsc0
        sc1 = jnp.einsum('ncx,cd->ndx', h1, Wsc1)
        vv = jnp.sum(A1 * A1, -1)
        B0 = Wc0[:, 0] * A0 + Wc0[:, 1] * A0 * A0 + Wc0[:, 2] * vv + Wc0[:, 3] * A0 ** 3 + Wc0[:, 4] * A0 * vv
        B1 = (Wc1[:, 0] + Wc1[:, 1] * A0 + Wc1[:, 2] * A0 * A0 + Wc1[:, 3] * vv)[..., None] * A1
        o0 = B0 @ WB0 + sc0
        o1 = jnp.einsum('ncx,cd->ndx', B1, WB1) + sc1
        eps = jnp.float32(1e-05)
        mu = jnp.mean(o0, 0)
        xc = o0 - mu
        var = jnp.mean(xc * xc, 0)
        n0 = xc * jax.lax.rsqrt(var + eps) * gamma0 + beta0
        nrm1 = jnp.mean(jnp.sum(o1 * o1, -1) / 3.0, 0)
        n1 = o1 * (jax.lax.rsqrt(nrm1 + eps) * gamma1)[None, :, None]
        return jnp.concatenate([n0, n1.reshape(n, 3 * C)], -1)
    edge_index = jnp.stack([src, dst])
    h = jnp.maximum(_layernorm(x, axis=-1), 0.0)
    x = x + _L0_gnn_ref(src, dst, h, L0_gnn_W, L0_gnn_b)
    h = jnp.maximum(_layernorm(x, axis=-1), 0.0)
    x = x + _L1_gnn_ref(h, edge_index, edge_attr_4, edge_attr_16, L1_gnn_W_up0, L1_gnn_W_up1, L1_gnn_M1, L1_gnn_M2, L1_gnn_M3, L1_gnn_M4, L1_gnn_W_lin0, L1_gnn_W_lin1, L1_gnn_Wsc0, L1_gnn_Wsc1, L1_gnn_Wc0, L1_gnn_Wc1, L1_gnn_WB0, L1_gnn_WB1, L1_gnn_gamma0, L1_gnn_beta0, L1_gnn_gamma1)
    return x

_drawn_inputs = setup_inputs


def setup_inputs(seed=0):
    import zlib

    import numpy as np

    out = dict(_drawn_inputs(seed))
    spreads = {'L1_gnn_gamma0': (1.0, 0.2), 'L1_gnn_beta0': (0.0, 0.1), 'L1_gnn_gamma1': (1.0, 0.2)}
    factors = {'L0_gnn_b': 6.216}
    for name, (base, spread) in spreads.items():
        noise = np.random.default_rng([zlib.crc32(name.encode()), seed]).standard_normal(out[name].shape)
        drawn = base * np.exp(spread * noise) if base else spread * noise
        out[name] = jnp.asarray(drawn.astype(out[name].dtype))
    for name, factor in factors.items():
        out[name] = (out[name] * factor).astype(out[name].dtype)
    return out
```

```python
from contextlib import ExitStack

import concourse.bass as bass
from concourse import mybir

ALU = mybir.AluOpType
ACT = mybir.ActivationFunctionType
F32 = mybir.dt.float32
BF16 = mybir.dt.bfloat16
F16 = mybir.dt.float16
I32 = mybir.dt.int32

P = 128
N = 50000
E = 12500
D = 256
C = 64
R = 16
J = 4
NG = P * J
G = -(-N // NG)
TAIL = N - (G - 1) * NG
TAILP = TAIL // J
T = -(-E // P)
T += T % 2
S = T // 2
LASTP = E - (P - 1) * T
PAD = T - LASTP
ROW = D + 1
TRASH = N
MSG_ROWS = -(-(N + 2 * P) // P)
ZERO_ROWS = 8
EPS = 1e-5
INV3 = 3.0 ** -0.5
U = 4
NOWHERE = 1 << 20
assert TAIL == TAILP * J and 0 < LASTP < T


class Step:

    def __init__(self, b, u, k, n, looped=False):
        self.b, self.u, self.k, self.n, self.looped = b, u, k, n, looped

    def at(self, d=0):
        return self.b * U + (self.u - d)

    def live(self, d=0):
        assert not self.looped or self.k >= d, "more steps have to come before the loop"
        return 0 <= self.k - d < self.n

    def slot(self, d, m):
        return (self.u - d) % m

    def uses(self, d, m):
        return self.b * (U // m) + (self.u - d) // m + 1


def run(eng, n, skew, body, first=1):
    hi = n // U - (1 if n % U == 0 else 0)
    for s in range(first * U):
        body(Step(s // U, s % U, s, n))
    with eng.Fori(first, hi, 1) as b:
        for u in range(U):
            body(Step(b, u, first * U + u, n, looped=True))
    for s in range(hi * U, n + skew):
        body(Step(s // U, s % U, s, n))


class Signal:

    def __init__(self, sem, base=0):
        self.sem, self.base = sem, base


def done(eng, sem, s, d=0, per=1):
    if s.live(d):
        eng.wait_ge(sem.sem, s.at(d) * per + (per + sem.base))


def landed(eng, slots, s, d=0, dmas=1):
    if s.live(d):
        eng.wait_ge(slots[s.slot(d, len(slots))], s.uses(d, len(slots)) * (16 * dmas))


def all_landed(eng, slots, n, dmas=1):
    for i, one in enumerate(slots):
        eng.wait_ge(one, 16 * dmas * len(range(i, n, len(slots))))


class Chain:

    def __init__(self, eng, sem, per=0, i=0):
        self.eng, self.sem, self.base, self.per, self.k = eng, sem.sem, i * per + sem.base, per, 0

    def __call__(self, instruction):
        self.k += 1
        instruction.then_inc(self.sem, 1)
        self.eng.wait_ge(self.sem, self.base + self.k)

    def end(self):
        assert self.k == self.per, self.k


def build(nc, x, src, dst, ea16, ea4, W, b, Wup0, Wup1, M1, M2, M3, M4, Wlin0, Wlin1, Wsc0, Wsc1,
          Wc0, Wc1, WB0, WB1, gamma0, beta0, gamma1, out):
    with ExitStack() as ctx:
        def sb(name, shape, dt=F32):
            return ctx.enter_context(nc.sbuf_tensor(name, shape, dt))

        def sem(name):
            return ctx.enter_context(nc.semaphore(name))

        def sems(name, n):
            return [sem(f"{name}{i}") for i in range(n)]

        def named(prefix, names):
            return {n: Signal(sem(f"{prefix}_{n}")) for n in names.split()}

        def after(signals, names):
            return {n: Signal(signals[n].sem, signals[n].base + S) for n in names.split()}

        def dram(name, shape, dt=F32):
            return nc.dram_tensor(name, shape, dt, kind="Internal").ap()

        x1_tab = dram("x1_tab", [N + 2 * P, ROW])
        msg_tab = dram("msg_tab", [P * MSG_ROWS, ROW])
        dinv_tab = dram("dinv_tab", [G * NG, 1])
        tpw_tab = dram("tpw_tab", [S, P, 2 * D])
        edge_o = dram("edge_o", [S, P, 2 * D])
        edge_x = dram("edge_x", [S, P, 2 * ROW])

        ident = sb("ident", [P, P])
        later = sb("later", [P, 2, 2 * P])
        ones = sb("ones", [P, P])
        ones_bf = sb("ones_bf", [3, P], BF16)
        eps_col = sb("eps_col", [P, 1])
        iota_h = sb("iota_h", [P, G * J], F16)
        trash_i = sb("trash_i", [P, 2], I32)
        trash = sb("trash", [P, 2])
        pair_i = sb("pair_i", [P, T], I32)
        pair_no = sb("pair_no", [P, T])
        valid = sb("valid", [P, T])
        vm1 = sb("vm1", [P, T])
        node_ok = sb("node_ok", [P, G * J])
        zeros = sb("zeros", [P, ZERO_ROWS * ROW])
        w_sb = sb("w_sb", [P, 2, D])
        b_f = sb("b_f", [1, 3, D])
        b_bf = sb("b_bf", [1, 3, D], BF16)
        b3 = sb("b3", [3, D], BF16)
        up_w = sb("up_w", [P, 2, P])
        lin_w = sb("lin_w", [P, 2, P])
        sc_w = sb("sc_w", [P, 2, P])
        wb_w = sb("wb_w", [P, 2, P])
        fin_w = sb("fin_w", [P, 2, P])
        m_sb = [sb("m1_sb", [R, C]), sb("m2_sb", [C, C]), sb("m3_sb", [C, C])]
        m4_sb = sb("m4_sb", [C, 4 * C])
        sc64 = sb("sc64", [C, 2, C])
        cw = sb("cw", [P, 9 * C])
        poly = sb("poly", [P, 4, 2, C])
        poly_vv = sb("poly_vv", [P, 1, C])
        g_b = sb("g_b", [P, 3, C])

        idx3 = sb("idx3", [P, T, 3], I32)
        src_c = sb("src_c", [P, T])
        dst_c = sb("dst_c", [P, T])
        src_f = sb("src_f", [P, T])
        dst_f = sb("dst_f", [P, T])
        src_delta = sb("src_delta", [P, T])
        dst_delta = sb("dst_delta", [P, T])
        int_a = sb("int_a", [P, T], I32)
        int_b = sb("int_b", [P, T], I32)
        lo_d, hi_d, lo_s, hi_s = (sb(n, [P, T]) for n in ("lo_d", "hi_d", "lo_s", "hi_s"))
        first_in_pair = sb("first_in_pair", [P, T])
        dinv_edge = sb("dinv_edge", [P, T, 2])
        final_idx = sb("final_idx", [P, T], I32)
        ea16_sb = sb("ea16_sb", [P, T * R])
        ea4_sb = sb("ea4_sb", [P, T * 4])
        deg = sb("deg", [P, G * J])
        dinv = sb("dinv", [P, G * J])
        dinv2 = sb("dinv2", [P, G * J])
        alone = sb("alone", [P, G * J])
        no_dst = sb("no_dst", [P, G * J])
        w_src = sb("w_src", [P, G * J])

        onehot = sb("onehot", [P, 2, 2, 2, P + G * J], BF16)
        rbf = sb("rbf", [P, 2, 2 * R])
        mlp_t = sb("mlp_t", [C, 4, 2 * P])
        tpb = sb("tpb", [P, 2, 2, 4, C])
        big = sb("big", [P, 4, J * ROW])
        hb = sb("hb", [P, 2, J, D])
        ht = sb("ht", [P, 2, 4 * P])
        x1b = sb("x1b", [P, 2, J * ROW])
        h2b = sb("h2b", [P, 2, J, ROW])
        st = sb("st", [P, 2, J, 6])
        mv = sb("mv", [P, 2, 2, J, 2])
        sd = sb("sd", [P, 2, 2, J])
        rs = sb("rs", [P, 2, 2, 3, J])
        idx = sb("idx", [P, 2, 3], I32)
        idx_e = sb("idx_e", [P, 2, 2], I32)
        got = sb("got", [P, 2, 2])
        claim = sb("claim", [P, 2, ROW])
        xg = sb("xg", [P, 4, 2, ROW])
        msg_in = sb("msg_in", [P, 4, 2, ROW])
        hg = sb("hg", [P, 2, 2, D])
        h2 = sb("h2", [P, 2, 2, ROW])
        hw = sb("hw", [P, 2, 2, D])
        vb = sb("vb", [P, 2, 2, D])
        own = sb("own", [P, 2, 2])
        sidx_f = sb("sidx_f", [P, 2])
        sidx = sb("sidx", [P, 4, 2], I32)
        eq = sb("eq", [P, 4, 2, 2 * P])
        eq_junk = sb("eq_junk", [P, 2, 2 * P])
        n_later = sb("n_later", [P, 2])
        coef = sb("coef", [P, 2, 2])
        addb = sb("addb", [P, 2, 2, ROW])
        dot = sb("dot", [P, 2, C])
        scaled_w = sb("scaled_w", [P, 2, 2, C])
        tmp_a = sb("tmp_a", [P, 2, C])
        tmp_b = sb("tmp_b", [P, 2, C])
        mt = sb("mt", [P, 4 * P])
        bt = sb("bt", [P, 4 * P])
        asb = sb("asb", [P, 2, 2, 4, C])
        asq = sb("asq", [P, 2, 2, 4, C])
        vv = sb("vv", [P, 2, C])
        term = sb("term", [P, 3, 2, 2, C])
        bsb = sb("bsb", [P, 2, 2, 4, C])
        osb = sb("osb", [P, 2, 2, 2 * D])
        lead_f = sb("lead_f", [P, 2])
        lead = sb("lead", [P, 4, 2])
        g_sb = sb("g_sb", [C, 2, C + 1])
        z_sb = sb("z_sb", [C, 3, C])
        row_sb = sb("row_sb", [1, 5 * C])
        slot_sum = sb("slot_sum", [P, 5 * C])
        fin = sb("fin", [P, 8, C])
        scale = sb("scale", [P, 4, C])
        bias = sb("bias", [P, C])

        bank = [ctx.enter_context(nc.psum_tensor(f"bank{i}", [P, 512], F32)) for i in range(8)]
        gram0, gram1 = bank[4], bank[5]

        def xj(t, slot, width):
            return t[:, slot, 0:J * width].rearrange("p (j d) -> p j d", j=J)

        def by_component(rows):
            return rows.rearrange("p (c x) -> p x c", x=3)

        def groups(table):
            return (table[0:(G - 1) * NG, :].rearrange("(g p j) d -> g p (j d)", p=P, j=J),
                    table[(G - 1) * NG:N, :].rearrange("(p j) d -> p (j d)", j=J))

        x_groups, out_groups, x1_groups = groups(x), groups(out), groups(x1_tab)

        def group(table, s, d=0):
            return (table[1], TAILP) if s.k - d == G - 1 else (table[0][s.at(d)], P)

        def pair(t, s, d=0):
            return t[:, bass.ds(s.at(d) * 2, 2)]

        def rows_of(index):
            return bass.IndirectOffsetOnAxis(ap=index, axis=0)
        loads = []
        for col, e in ((1, dst), (2, src)):
            loads += [(idx3[0:P - 16, :, col], e[0:(P - 16) * T].rearrange("(p t) -> p t", t=T)),
                      (idx3[P - 16:P - 1, :, col], e[(P - 16) * T:(P - 1) * T].rearrange("(p t) -> p t", t=T)),
                      (idx3[P - 1:P, 0:LASTP, col], e[(P - 1) * T:E].rearrange("(p t) -> p t", p=1)),
                      (idx3[P - 1:P, LASTP:T, col], e[E - PAD:E].rearrange("(p t) -> p t", p=1))]
        for to, e, w in ((ea16_sb, ea16, R), (ea4_sb, ea4, 4)):
            loads += [(to[0:P - 16, :], e[0:(P - 16) * T, :].rearrange("(p t) r -> p (t r)", t=T)),
                      (to[P - 16:P - 1, :], e[(P - 16) * T:(P - 1) * T, :].rearrange("(p t) r -> p (t r)", t=T)),
                      (to[P - 1:P, 0:LASTP * w], e[(P - 1) * T:E, :].rearrange("(p t) r -> p (t r)", p=1)),
                      (to[P - 1:P, LASTP * w:T * w], e[E - PAD:E, :].rearrange("(p t) r -> p (t r)", p=1))]
        loads += [(w_sb[:, i, :], W[i * P:(i + 1) * P, :]) for i in range(2)]
        loads += [(b_f[:, 0, :], b.rearrange("(a d) -> a d", a=1))]
        for to, w0, w1 in ((up_w, Wup0, Wup1), (lin_w, Wlin0, Wlin1), (sc_w, Wsc0, Wsc1), (wb_w, WB0, WB1)):
            loads += [(to[0:C, 0, 0:C], w0), (to[C:P, 0, C:P], w1), (to[0:C, 1, 0:C], w1), (to[C:P, 1, C:P], w1)]
        loads += [(sc64[:, 0, :], Wsc0), (sc64[:, 1, :], Wsc1)]
        loads += list(zip((m_sb[0][:], m_sb[1][:], m_sb[2][:], m4_sb[:]), (M1, M2, M3, M4)))
        loads += [(cw[:, 0:5 * C], Wc0.rearrange("c k -> (c k)").partition_broadcast(P)),
                  (cw[:, 5 * C:9 * C], Wc1.rearrange("c k -> (c k)").partition_broadcast(P))]
        loads += [(g_b[:, i, :], w.partition_broadcast(P)) for i, w in enumerate((gamma0, beta0, gamma1))]
        LOADED = 16 * len(loads)
        CLEARED = 16 * (-(-MSG_ROWS // ZERO_ROWS) + 1)

        pre = named("pre", "pool_chain dve_chain consts inputs prepared b_split b3 cleared deg root dinv dinv_out")
        cnt = named("cnt", "rbf onehot counted turned0 act0 layer1 act1 layer2 act2 layer3 act3 layer4 weights")
        tpw_out = sems("tpw_out", 2)
        p1 = named("p1", "chain_a chain_b chain_m chain_n stats1 root1 norm1 relu1 turned ht xw x1 stats2 root2 norm2 "
                         "relu2 gram idx dinv_got")
        x_in, x1_out, claim_out, dinv_in = sems("x_in", 4), sems("x1_out", 2), sems("claim_out", 1), sems("dinv_in", 2)
        e1 = named("e1", "idx own others chain_a chain_b chain_c eq sidx coef stats root norm relu turned ht xw v "
                         "merged add")
        e1_got, e1_out = sems("e1_got", 4), sems("e1_out", 1)
        e2 = named("e2", "chain_m weighted up gram message")
        e2 |= after(e1, "idx own others eq sidx stats root norm relu turned ht merged add")
        e2_got, e2_out, tp_in = sems("e2_got", 4), sems("e2_out", 1), sems("tp_in", 2)
        e3 = named("e3", "chain_p lead m_turned mt a_done a b b_turned bt o_done o summed")
        e3 |= after(e2, "idx stats root norm relu turned ht")
        e3_got, eo_out, ex_out = sems("e3_got", 4), sems("eo_out", 2), sems("ex_out", 4)
        fs = named("fs", "chain grams products z sums var root rsqrt weights")
        p2 = named("p2", "chain_a chain_b stats root norm relu turned ht y out")
        y_in, y_out = sems("y_in", 4), sems("y_out", 2)
        f = named("f", "chain idx rows")
        f_in, f_out = sems("f_in", 2), sems("f_out", 2)

        for chain, per in (("chain_a", 1), ("chain_b", 1), ("chain_c", 3)):
            e2[chain] = Signal(e1[chain].sem, S * per)
            e3[chain] = Signal(e1[chain].sem, 2 * S * per)
        n_consts = []

        waited = {nc.gpsimd.engine: sem("waited_pool"), nc.tensor.engine: sem("waited_pe"),
                  nc.vector.engine: sem("waited_dve")}

        def settle(eng):
            eng.sem_inc(waited[eng.engine], 1)

        block = ctx.enter_context(nc.Block())

        @block.gpsimd
        def _(pool):
            g = nc.gpsimd
            n = [0]

            def const(instruction, wait=False):
                n[0] += 1
                instruction.then_inc(pre["consts"].sem, 1)
                if wait:
                    pool.wait_ge(pre["consts"].sem, n[0])

            const(g.memset(ident[:], 0.0), wait=True)
            const(g.affine_select(out=ident[:], in_=ident[:], compare_op=ALU.not_equal, fill=1.0, base=0,
                                  pattern=[[-1, P]], channel_multiplier=1))
            const(g.memset(later[:, 0, :], 1.0))
            const(g.memset(later[:, 1, 0:P], 0.0))
            const(g.memset(later[:, 1, P:2 * P], 1.0), wait=True)
            for a in range(2):
                v = later[:, a, a * P:(a + 1) * P]
                const(g.affine_select(out=v, in_=v, compare_op=ALU.is_gt, fill=0.0, base=0, pattern=[[1, P]],
                                      channel_multiplier=-1))
            const(g.memset(valid[:], 1.0))
            const(g.memset(node_ok[:], 1.0), wait=True)
            const(g.affine_select(out=valid[:], in_=valid[:], compare_op=ALU.is_gt, fill=0.0, base=E,
                                  pattern=[[-1, T]], channel_multiplier=-T))
            v = node_ok[:].rearrange("p (g j) -> p g j", j=J)
            const(g.affine_select(out=v, in_=v, compare_op=ALU.is_gt, fill=0.0, base=N, pattern=[[-NG, G], [-1, J]],
                                  channel_multiplier=-J))
            const(g.memset(ones[:], 1.0))
            const(g.memset(ones_bf[:], 1.0))
            const(g.memset(eps_col[:], EPS))
            const(g.memset(zeros[:], 0.0))
            for t in (claim, addb, up_w, lin_w, sc_w, wb_w):
                const(g.memset(t[:], 0.0))
            const(g.memset(h2b[:, :, :, 0:1], 1.0))
            const(g.memset(h2[:, :, :, 0:1], 1.0))
            const(g.iota(iota_h[:], pattern=[[1, G * J]], base=0, channel_multiplier=0,
                         allow_small_or_imprecise_dtypes=True))
            const(g.iota(trash_i[:], pattern=[[P, 2]], base=TRASH, channel_multiplier=1))
            const(g.iota(pair_i[:], pattern=[[1, S], [0, 2]], base=0, channel_multiplier=0))
            n_consts.append(n[0])

            def rbf_step(s):
                if s.live():
                    if s.k == 0:
                        pool.wait_ge(pre["inputs"].sem, LOADED)
                    done(pool, cnt["turned0"], s, 2)
                    settle(pool)
                    g.tensor_copy(rbf[:, s.slot(0, 2), :],
                                  ea16_sb[:, bass.ds(s.at() * (2 * R), 2 * R)]).then_inc(cnt["rbf"].sem, 1)

            run(pool, S, 0, rbf_step)

            def claim_step(s):
                if s.live():
                    a = s.slot(0, 2)
                    if s.k == 0:
                        pool.wait_ge(pre["prepared"].sem, 1)
                        pool.wait_ge(pre["cleared"].sem, CLEARED)
                        pool.wait_ge(pre["dinv_out"].sem, 16)
                    landed(pool, claim_out, s, 2)
                    landed(pool, dinv_in, s, 2, dmas=2)
                    settle(pool)
                    g.tensor_copy(idx[:, a, :], idx3[:, bass.ds(s.at(), 1), :]).then_inc(p1["idx"].sem, 1)
                    g.tensor_copy(claim[:, a, D:ROW], pair_no[:, bass.ds(s.at(), 1)]).then_inc(p1["idx"].sem, 1)
                    done(pool, p1["idx"], s, 0, per=2)
                    done(pool, p1["dinv_got"], s, 2)
                    landed(pool, claim_out, s, 1)
                    settle(pool)
                    pool.indirect_dma_start(msg_tab, rows_of(idx[:, a, 0:1]), claim[:, a, :],
                                            None).then_inc(claim_out[0], 16)
                    for i in range(2):
                        pool.indirect_dma_start(got[:, a, i:i + 1], None, dinv_tab,
                                                rows_of(idx[:, a, i + 1:i + 2])).then_inc(dinv_in[a], 16)
                if s.live(1):
                    landed(pool, dinv_in, s, 1, dmas=2)
                    settle(pool)
                    g.tensor_copy(dinv_edge[:, bass.ds(s.at(1), 1), :],
                                  got[:, s.slot(1, 2), :].unsqueeze(1)).then_inc(p1["dinv_got"].sem, 1)

            run(pool, T, 1, claim_step)

            def gather(sm, got_sems, s, which, sources, free):
                a = s.slot(0, 2)
                landed(pool, got_sems, s, 2, dmas=2 * len(sources))
                settle(pool)
                g.tensor_copy(idx_e[:, a, :], idx3[:, bass.ds(s.at() * 2, 2), which]).then_inc(sm["idx"].sem, 1)
                free(s)
                settle(pool)
                done(pool, sm["idx"], s, 0)
                settle(pool)
                for i in range(2):
                    for to, table in sources:
                        pool.indirect_dma_start(to[:, s.slot(0, 4), i, 0:table.shape[1]], None, table,
                                                rows_of(idx_e[:, a, i:i + 1])).then_inc(got_sems[s.slot(0, 4)], 16)

            def scatter_add(sm, out_sems, s, d, table):
                if s.live(d):
                    done(pool, sm["add"], s, d)
                    done(pool, sm["sidx"], s, d)
                    landed(pool, out_sems, s, d + 1, dmas=2)
                    settle(pool)
                    for i in range(2):
                        pool.indirect_dma_start(table, rows_of(sidx[:, s.slot(d, 4), i:i + 1]),
                                                addb[:, s.slot(d, 2), i, :], None,
                                                compute_op=ALU.add).then_inc(out_sems[0], 16)

            def e1_step(s):
                if s.live():
                    gather(e1, e1_got, s, 1, [(xg, x)], lambda s: done(pool, e1["relu"], s, 4))
                if s.k == 2:
                    all_landed(pool, x1_out, G)
                scatter_add(e1, e1_out, s, 2, x1_tab)

            run(pool, S, 2, e1_step)
            all_landed(pool, e1_out, S, dmas=2)

            def e2_step(s):
                if s.live():
                    gather(e2, e2_got, s, 2, [(xg, x1_tab)], lambda s: done(pool, e2["weighted"], s, 4))
                if s.k == 3:
                    all_landed(pool, claim_out, T)
                scatter_add(e2, e2_out, s, 3, msg_tab)

            run(pool, S, 3, e2_step)
            all_landed(pool, e2_out, S, dmas=2)

            def e3_free(s):
                done(pool, e3["relu"], s, 4)
                landed(pool, ex_out, s, 4)
                done(pool, e3["lead"], s, 4)
                done(pool, e3["m_turned"], s, 4)
                settle(pool)

            def e3_step(s):
                if s.live():
                    gather(e3, e3_got, s, 1, [(xg, x1_tab), (msg_in, msg_tab)], e3_free)

            run(pool, S, 0, e3_step)

            def f_step(s):
                if s.live():
                    a = s.slot(0, 2)
                    landed(pool, f_out, s, 2, dmas=2)
                    settle(pool)
                    g.tensor_copy(idx_e[:, a, :], pair(final_idx, s)).then_inc(f["idx"].sem, 1)
                    done(pool, f["idx"], s, 0)
                    done(pool, f["rows"], s, 0)
                    settle(pool)
                    if s.k == 0:
                        all_landed(pool, y_out, G)
                    for i in range(2):
                        pool.indirect_dma_start(out, rows_of(idx_e[:, a, i:i + 1]), hg[:, a, i, :], None,
                                                bounds_check=N - 1, oob_is_err=False).then_inc(f_out[a], 16)

            pool.wait_ge(e3["lead"].sem, S)
            run(pool, S, 0, f_step)
            all_landed(pool, f_out, S, dmas=2)

        @block.sync
        def _(sp):
            sp.wait_ge(pre["consts"].sem, n_consts[0])
            with nc.allow_non_contiguous_dma(reason="each edge's index lies beside its others"):
                for to, what in loads:
                    sp.dma_start(to, what).then_inc(pre["inputs"].sem, 16)
            m = msg_tab.rearrange("(p r) d -> p (r d)", p=P)
            for r in range(0, MSG_ROWS, ZERO_ROWS):
                n = min(ZERO_ROWS, MSG_ROWS - r)
                sp.dma_start(m[:, r * ROW:(r + n) * ROW], zeros[:, 0:n * ROW]).then_inc(pre["cleared"].sem, 16)
            sp.dma_start(x1_tab[N:N + 2 * P, :].rearrange("(p a) d -> p (a d)", p=P),
                         zeros[:, 0:2 * ROW]).then_inc(pre["cleared"].sem, 16)
            sp.wait_ge(pre["b_split"].sem, 1)
            for i in range(3):
                sp.dma_start(b3[i:i + 1, :], b_bf[:, i, :]).then_inc(pre["b3"].sem, 16)
            def tpw_step(s):
                if s.live(4):
                    done(sp, cnt["weights"], s, 4)
                    sp.dma_start(tpw_tab[s.at(4)], tpb[:, s.slot(4, 2)].rearrange("p a k c -> p (a k c)")
                                 ).then_inc(tpw_out[s.slot(4, 2)], 16)

            run(sp, S, 4, tpw_step)
            sp.wait_ge(pre["dinv"].sem, 1)
            sp.dma_start(dinv_tab.rearrange("(g p j) a -> p g (j a)", p=P, j=J),
                         dinv[:].rearrange("p (g j) -> p g j", j=J)).then_inc(pre["dinv_out"].sem, 16)

            def p1_step(s):
                done(sp, p1["x1"], s, 4)
                if s.live():
                    rows, n = group(x_groups, s)
                    sp.dma_start(big[0:n, s.slot(0, 4), 0:J * D], rows).then_inc(x_in[s.slot(0, 4)], 16)
                if s.live(4):
                    rows, n = group(x1_groups, s, 4)
                    sp.dma_start(rows, x1b[0:n, s.slot(4, 2), :]).then_inc(x1_out[s.slot(4, 2)], 16)

            run(sp, G, 4, p1_step)

            all_landed(sp, tpw_out, S)
            def tp_step(s):
                if s.live():
                    done(sp, e2["message"], s, 2)
                    sp.dma_start(tpb[:, s.slot(0, 2)].rearrange("p a k c -> p (a k c)"),
                                 tpw_tab[s.at()]).then_inc(tp_in[s.slot(0, 2)], 16)

            run(sp, S, 0, tp_step)

            def e3_step(s):
                if s.live():
                    landed(sp, e3_got, s, 0, dmas=4)
                    sp.dma_start(edge_x[s.at()], xg[:, s.slot(0, 4)].rearrange("p a d -> p (a d)")
                                 ).then_inc(ex_out[s.slot(0, 4)], 16)
                if s.live(2):
                    done(sp, e3["o"], s, 2)
                    sp.dma_start(edge_o[s.at(2)].rearrange("p (a d) -> p a d", a=2),
                                 osb[:, s.slot(2, 2), :, D:2 * D]).then_inc(eo_out[s.slot(2, 2)], 16)

            run(sp, S, 2, e3_step)

            def p2_step(s):
                if s.k == 0:
                    all_landed(sp, ex_out, S)
                done(sp, p2["out"], s, 4)
                if s.live():
                    rows, n = group(x1_groups, s)
                    sp.dma_start(big[0:n, s.slot(0, 4), :], rows).then_inc(y_in[s.slot(0, 4)], 16)
                if s.live(3):
                    done(sp, p2["out"], s, 3)
                    rows, n = group(out_groups, s, 3)
                    sp.dma_start(rows, x1b[0:n, s.slot(3, 2), 0:J * D]).then_inc(y_out[s.slot(3, 2)], 16)

            run(sp, G, 3, p2_step)

            all_landed(sp, eo_out, S)
            def f_step(s):
                if s.live():
                    a = s.slot(0, 2)
                    done(sp, f["rows"], s, 2)
                    sp.dma_start(vb[:, a].rearrange("p a d -> p (a d)"), edge_o[s.at()]).then_inc(f_in[a], 16)
                    sp.dma_start(xg[:, a].rearrange("p a d -> p (a d)"), edge_x[s.at()]).then_inc(f_in[a], 16)

            run(sp, S, 0, f_step)
            all_landed(sp, y_out, G)

        @block.tensor
        def _(pe):
            mm = nc.tensor.matmul

            layers = ((cnt["turned0"], bank[2]), (cnt["layer1"], bank[3]), (cnt["layer2"], bank[6]),
                      (cnt["layer3"], bank[7]))

            def count_step(s):
                if s.k == 0:
                    pe.wait_ge(pre["consts"].sem, n_consts[0])
                    pe.wait_ge(pre["inputs"].sem, LOADED)
                if s.live():
                    a = s.slot(0, 2)
                    done(pe, cnt["onehot"], s, 0)
                    for i in range(2):
                        for which in range(2):
                            o = onehot[:, a, i, which, :]
                            last = mm(bank[which][:, 0:G * J], o[:, 0:P], o[:, P:P + G * J],
                                      start=(s.k == 0 and i == 0), stop=(s.k == S - 1 and i == 1))
                    last.then_inc(cnt["counted"].sem, 1)
                    done(pe, cnt["rbf"], s, 0)
                    done(pe, cnt["act0"], s, 1)
                    for i in range(2):
                        last = nc.tensor.transpose(bank[2][0:R, i * P:(i + 1) * P], rbf[:, a, i * R:(i + 1) * R],
                                                   ident[:])
                    last.then_inc(cnt["turned0"].sem, 1)
                for i in range(3):
                    if s.live(i + 1):
                        done(pe, cnt[f"act{i}"], s, i + 1)
                        done(pe, cnt[f"act{i + 1}"], s, i + 2)
                        k = R if i == 0 else C
                        settle(pe)
                        mm(layers[i + 1][1][0:C, 0:2 * P], m_sb[i][:], mlp_t[0:k, i, :], start=True,
                           stop=True).then_inc(cnt[f"layer{i + 1}"].sem, 1)
                if s.live(4):
                    done(pe, cnt["act3"], s, 4)
                    done(pe, cnt["weights"], s, 5)
                    for i in range(2):
                        last = mm(bank[4][:, i * D:(i + 1) * D], mlp_t[:, 3, i * P:(i + 1) * P], m4_sb[:],
                                  start=True, stop=True)
                    last.then_inc(cnt["layer4"].sem, 1)

            run(pe, S, 4, count_step, first=2)

            pe.wait_ge(pre["b3"].sem, 48)

            def p1_step(s):
                if s.live(1):
                    done(pe, p1["relu1"], s, 1)
                    for q in range(2):
                        if s.live(2):
                            pe.wait_ge(p1["ht"].sem, s.at(2) * 2 + q + 1)
                        for j in range(2):
                            for k in range(2):
                                last = nc.tensor.transpose(bank[q][:, (2 * j + k) * P:(2 * j + k + 1) * P],
                                                           hb[:, s.slot(1, 2), 2 * q + j, k * P:(k + 1) * P], ident[:])
                        last.then_inc(p1["turned"].sem, 1)
                    done(pe, p1["x1"], s, 2)
                    for q in range(2):
                        pe.wait_ge(p1["ht"].sem, s.at(1) * 2 + q + 1)
                        for j in range(2):
                            y = bank[2 + q][:, j * D:(j + 1) * D]
                            for k in range(2):
                                mm(y, ht[:, q, (2 * j + k) * P:(2 * j + k + 1) * P], w_sb[:, k, :], start=(k == 0),
                                   stop=False)
                            last = mm(y, ones_bf[:], b3[:], start=False, stop=True)
                        last.then_inc(p1["xw"].sem, 1)
                if s.live(2):
                    done(pe, p1["relu2"], s, 2)
                    settle(pe)
                    for j in range(J):
                        h = h2b[:, s.slot(2, 2), j, :]
                        mm(gram0[0:C, 0:C + 1], h[:, 1:C + 1], h[:, 0:C + 1], start=(s.k == 2 and j == 0), stop=False)
                        for c in range(3):
                            v = by_component(h[:, C + 1:ROW])[:, c, :]
                            last = mm(gram1[0:C, 0:C], v, v, start=(s.k == 2 and j == 0 and c == 0), stop=False)
                    last.then_inc(p1["gram"].sem, 1)

            run(pe, G, 2, p1_step)

            def spread_own(sm, s, to):
                done(pe, sm["own"], s, 0)
                done(pe, sm["eq"], s, 1)
                for i in range(2):
                    last = mm(to[:, i * P:(i + 1) * P], own[:, s.slot(0, 2), i:i + 1].to_broadcast([P, P]), ident[:],
                              start=True, stop=True)
                last.then_inc(sm["others"].sem, 1)

            def turn(h, to, ready):
                for i in range(2):
                    for k in range(2):
                        last = nc.tensor.transpose(to[:, (2 * i + k) * P:(2 * i + k + 1) * P],
                                                   h[:, i, k * P:(k + 1) * P], ident[:])
                last.then_inc(ready.sem, 1)

            def merge(sm, s, d, rows, to):
                for i in range(2):
                    for k in range(2):
                        last = mm(to[:, i * D:(i + 1) * D], eq[:, s.slot(d, 4), k, i * P:(i + 1) * P],
                                  rows[:, k, 0:D], start=(k == 0), stop=(k == 1))
                last.then_inc(sm["merged"].sem, 1)

            def e1_step(s):
                if s.live():
                    spread_own(e1, s, bank[6])
                    done(pe, e1["relu"], s, 0)
                    done(pe, e1["ht"], s, 1)
                    turn(hg[:, s.slot(0, 2)], bank[0], e1["turned"])
                if s.live(1):
                    done(pe, e1["v"], s, 1)
                    done(pe, e1["eq"], s, 1)
                    done(pe, e1["add"], s, 2)
                    merge(e1, s, 1, vb[:, s.slot(1, 2)], bank[3])
                if s.live():
                    done(pe, e1["ht"], s, 0)
                    done(pe, e1["v"], s, 1)
                    for i in range(2):
                        y = bank[2][:, i * D:(i + 1) * D]
                        for k in range(2):
                            mm(y, ht[:, 0, (2 * i + k) * P:(2 * i + k + 1) * P], w_sb[:, k, :], start=(k == 0),
                               stop=False)
                        last = mm(y, ones_bf[:], b3[:], start=False, stop=True)
                    last.then_inc(e1["xw"].sem, 1)

            run(pe, S, 1, e1_step)

            def e2_step(s):
                if s.live():
                    spread_own(e2, s, bank[6])
                    done(pe, e2["relu"], s, 0)
                    done(pe, e2["ht"], s, 1)
                    turn(h2[:, s.slot(0, 2), :, 1:ROW], bank[0], e2["turned"])
                if s.live(2):
                    done(pe, e2["message"], s, 2)
                    done(pe, e2["add"], s, 3)
                    merge(e2, s, 2, msg_in[:, s.slot(2, 4)], bank[7])
                if s.live():
                    done(pe, e2["ht"], s, 0)
                    done(pe, e2["message"], s, 2)
                    for i in range(2):
                        for k in range(2):
                            last = mm(bank[2 + s.slot(0, 2)][:, i * D + k * P:i * D + (k + 1) * P],
                                      ht[:, 0, (2 * i + k) * P:(2 * i + k + 1) * P], up_w[:, k, :], start=True,
                                      stop=True)
                    last.then_inc(e2["up"].sem, 1)
                    done(pe, e2["weighted"], s, 0)
                    settle(pe)
                    for i in range(2):
                        h, w = h2[:, s.slot(0, 2), i, :], hw[:, s.slot(0, 2), i, :]
                        end = s.k == S - 1 and i == 1
                        mm(gram0[0:C, 0:C + 1], w[:, 0:C], h[:, 0:C + 1], start=False, stop=end)
                        for c in range(1, 4):
                            last = mm(gram1[0:C, 0:C], w[:, c * C:(c + 1) * C], h[:, 1 + c * C:1 + (c + 1) * C],
                                      start=False, stop=(end and c == 3))
                    last.then_inc(e2["gram"].sem, 1)

            run(pe, S, 2, e2_step)

            def e3_step(s):
                if s.live():
                    landed(pe, e3_got, s, 0, dmas=4)
                    done(pe, e3["mt"], s, 1)
                    turn(msg_in[:, s.slot(0, 4)], bank[1], e3["m_turned"])
                    done(pe, e3["relu"], s, 0)
                    done(pe, e3["ht"], s, 1)
                    turn(h2[:, s.slot(0, 2), :, 1:ROW], bank[0], e3["turned"])
                    done(pe, e3["mt"], s, 0)
                    done(pe, e3["a"], s, 1)
                    for i in range(2):
                        for k in range(2):
                            last = mm(bank[2][:, i * D + k * P:i * D + (k + 1) * P],
                                      mt[:, (2 * i + k) * P:(2 * i + k + 1) * P], lin_w[:, k, :], start=True, stop=True)
                    last.then_inc(e3["a_done"].sem, 1)
                if s.live(1):
                    done(pe, e3["b"], s, 1)
                    done(pe, e3["bt"], s, 2)
                    turn(bsb[:, s.slot(1, 2)].rearrange("p a k c -> p a (k c)"), bank[3], e3["b_turned"])
                    done(pe, e3["bt"], s, 1)
                    done(pe, e3["o"], s, 2)
                    for i in range(2):
                        for k in range(2):
                            y = bank[6][:, i * D + k * P:i * D + (k + 1) * P]
                            at = slice((2 * i + k) * P, (2 * i + k + 1) * P)
                            mm(y, bt[:, at], wb_w[:, k, :], start=True, stop=False)
                            last = mm(y, ht[:, s.slot(1, 2), at], sc_w[:, k, :], start=False, stop=True)
                    last.then_inc(e3["o_done"].sem, 1)
                if s.live(2):
                    done(pe, e3["o"], s, 2)
                    done(pe, e3["lead"], s, 2)
                    for i in range(2):
                        last = mm(bank[7][0:1, 0:5 * C], lead[:, s.slot(2, 4), i:i + 1],
                                  osb[:, s.slot(2, 2), i, 0:5 * C], start=(s.k == 2 and i == 0),
                                  stop=(s.k == S + 1 and i == 1))
                    last.then_inc(e3["summed"].sem, 1)

            run(pe, S, 2, e3_step)

            pe.wait_ge(fs["grams"].sem, 1)
            for i in range(2):
                mm(bank[i][0:C, 0:C], g_sb[:, i, 1 - i:1 - i + C], sc64[:, i, :], start=True,
                   stop=True).then_inc(fs["products"].sem, 1)
            pe.wait_ge(fs["z"].sem, 1)
            mm(bank[2][:, 0:3 * C], ones[0:C, :], z_sb[:].rearrange("p a c -> p (a c)"), start=True, stop=True)
            mm(bank[3][:, 0:5 * C], ones[0:1, :], row_sb[:], start=True, stop=True).then_inc(fs["sums"].sem, 1)

            pe.wait_ge(fs["weights"].sem, 1)

            def p2_step(s):
                if s.live(1):
                    done(pe, p2["relu"], s, 1)
                    for q in range(2):
                        if s.live(2):
                            pe.wait_ge(p2["ht"].sem, s.at(2) * 2 + q + 1)
                        for j in range(2):
                            for k in range(2):
                                last = nc.tensor.transpose(bank[q][:, (2 * j + k) * P:(2 * j + k + 1) * P],
                                                           hb[:, s.slot(1, 2), 2 * q + j, k * P:(k + 1) * P], ident[:])
                        last.then_inc(p2["turned"].sem, 1)
                    done(pe, p2["out"], s, 2)
                    for q in range(2):
                        pe.wait_ge(p2["ht"].sem, s.at(1) * 2 + q + 1)
                        for j in range(2):
                            for k in range(2):
                                y = bank[2 + q][:, j * D + k * P:j * D + (k + 1) * P]
                                last = mm(y, ht[:, q, (2 * j + k) * P:(2 * j + k + 1) * P], fin_w[:, k, :], start=True,
                                          stop=(k == 1))
                                if k == 0:
                                    mm(y[:, 0:C], ones[0:1, :], bias[0:1, :], start=False, stop=True)
                        last.then_inc(p2["y"].sem, 1)

            run(pe, G, 1, p2_step)

        @block.scalar
        def _(act):
            s_act = nc.scalar.activation

            def count_step(s):
                if s.live():
                    done(act, cnt["turned0"], s, 0)
                    done(act, cnt["layer1"], s, 1)
                    nc.scalar.copy(mlp_t[0:R, 0, :], bank[2][0:R, 0:2 * P]).then_inc(cnt["act0"].sem, 1)
                for i, from_ in ((1, bank[3]), (2, bank[6]), (3, bank[7])):
                    if s.live(i):
                        done(act, cnt[f"layer{i}"], s, i)
                        done(act, cnt[f"layer{i + 1}"], s, i + 1)
                        s_act(mlp_t[:, i, :], from_[0:C, 0:2 * P], ACT.Silu).then_inc(cnt[f"act{i}"].sem, 1)
                if s.live(4):
                    done(act, cnt["layer4"], s, 4)
                    landed(act, tpw_out, s, 6)
                    nc.scalar.copy(tpb[:, s.slot(4, 2)].rearrange("p a k c -> p (a k c)"), bank[4][:]
                                   ).then_inc(cnt["weights"].sem, 1)

            run(act, S, 4, count_step, first=2)
            act.wait_ge(pre["deg"].sem, 1)
            s_act(deg[:], deg[:], ACT.Sqrt).then_inc(pre["root"].sem, 1)

            def root(sm, which, k, a, n, s, d=0):
                done(act, sm[f"stats{which}"], s, d)
                s_act(sd[:, k, a, 0:n], mv[:, k, a, 0:n, 1], ACT.Sqrt, bias=eps_col[:]).then_inc(sm[f"root{which}"].sem, 1)

            def p1_step(s):
                if s.live(1):
                    for q in range(2):
                        pe_turned = s.at(1) * 2 + q + 1
                        act.wait_ge(p1["turned"].sem, pe_turned)
                        if s.live(2):
                            act.wait_ge(p1["xw"].sem, s.at(2) * 2 + q + 1)
                        nc.scalar.copy(ht[:, q, :], bank[q][:]).then_inc(p1["ht"].sem, 1)
                if s.live():
                    root(p1, "1", 0, s.slot(0, 2), J, s)
                if s.live(2):
                    a = s.slot(2, 2)
                    done(act, p1["norm2"], s, 2)
                    done(act, p1["gram"], s, 4)
                    for j in range(J):
                        last = s_act(h2b[:, a, j, 1:ROW], xj(x1b, a, ROW)[:, j, 0:D], ACT.Relu,
                                     bias=rs[:, 1, a, 2, j:j + 1], scale=rs[:, 1, a, 1, j:j + 1])
                    last.then_inc(p1["relu2"].sem, 1)
                if s.live():
                    a = s.slot(0, 2)
                    done(act, p1["norm1"], s, 0)
                    done(act, p1["turned"], s, 2, per=2)
                    for j in range(J):
                        last = s_act(hb[:, a, j, :], xj(big, s.slot(0, 4), D)[:, j, :], ACT.Relu,
                                     bias=rs[:, 0, a, 1, j:j + 1], scale=rs[:, 0, a, 0, j:j + 1])
                    last.then_inc(p1["relu1"].sem, 1)
                if s.live(1):
                    root(p1, "2", 1, s.slot(1, 2), J, s, 1)

            run(act, G, 2, p1_step)

            def relu_by_component(h, rows, r, j):
                s_act(h[:, 0:C], rows[:, 0:C], ACT.Relu, bias=r[:, 1, j:j + 1], scale=r[:, 0, j:j + 1])
                return s_act(by_component_out(h[:, C:D]), by_component(rows[:, C:D]), ACT.Relu,
                             bias=r[:, 1, j:j + 1], scale=r[:, 0, j:j + 1])

            def by_component_out(h):
                return h.rearrange("p (x c) -> p x c", x=3)

            def e1_step(s):
                if s.live():
                    root(e1, "", 0, s.slot(0, 2), 2, s)
                    done(act, e1["norm"], s, 0)
                    done(act, e1["turned"], s, 2)
                    for i in range(2):
                        last = s_act(hg[:, s.slot(0, 2), i, :], xg[:, s.slot(0, 4), i, 0:D], ACT.Relu,
                                     bias=rs[:, 0, s.slot(0, 2), 1, i:i + 1], scale=rs[:, 0, s.slot(0, 2), 0, i:i + 1])
                    last.then_inc(e1["relu"].sem, 1)
                if s.live(1):
                    done(act, e1["xw"], s, 1)
                    done(act, e1["coef"], s, 1)
                    done(act, e1["merged"], s, 3)
                    for i in range(2):
                        last = s_act(vb[:, s.slot(1, 2), i, :], bank[2][:, i * D:(i + 1) * D], ACT.Identity,
                                     scale=coef[:, s.slot(1, 2), i:i + 1])
                    last.then_inc(e1["v"].sem, 1)
                if s.live():
                    done(act, e1["turned"], s, 0)
                    done(act, e1["xw"], s, 1)
                    nc.scalar.copy(ht[:, 0, :], bank[0][:]).then_inc(e1["ht"].sem, 1)
                if s.live(1):
                    done(act, e1["merged"], s, 1)
                    landed(act, e1_out, s, 3, dmas=2)
                    nc.scalar.copy(addb[:, s.slot(1, 2), :, 0:D], bank[3][:].rearrange("p (a d) -> p a d", a=2)
                                   ).then_inc(e1["add"].sem, 1)

            run(act, S, 1, e1_step)

            def e2_step(s):
                if s.live():
                    a = s.slot(0, 2)
                    root(e2, "", 0, a, 2, s)
                    done(act, e2["norm"], s, 0)
                    done(act, e2["gram"], s, 2)
                    for i in range(2):
                        last = relu_by_component(h2[:, a, i, 1:ROW], xg[:, s.slot(0, 4), i, :], rs[:, 0, a], i)
                    last.then_inc(e2["relu"].sem, 1)
                    done(act, e2["relu"], s, 0)
                    for i in range(2):
                        last = s_act(hw[:, a, i, :], h2[:, a, i, 1:ROW], ACT.Identity,
                                     scale=xg[:, s.slot(0, 4), i, D:ROW])
                    last.then_inc(e2["weighted"].sem, 1)
                    done(act, e2["turned"], s, 0)
                    done(act, e2["up"], s, 1)
                    nc.scalar.copy(ht[:, 0, :], bank[0][:]).then_inc(e2["ht"].sem, 1)
                if s.live(2):
                    done(act, e2["merged"], s, 2)
                    landed(act, e2_out, s, 4, dmas=2)
                    nc.scalar.copy(addb[:, s.slot(2, 2), :, 0:D], bank[7][:].rearrange("p (a d) -> p a d", a=2)
                                   ).then_inc(e2["add"].sem, 1)

            run(act, S, 2, e2_step)

            def e3_step(s):
                if s.live():
                    a = s.slot(0, 2)
                    root(e3, "", 0, a, 2, s)
                    done(act, e3["m_turned"], s, 0)
                    done(act, e3["a_done"], s, 1)
                    nc.scalar.copy(mt[:], bank[1][:]).then_inc(e3["mt"].sem, 1)
                    done(act, e3["norm"], s, 0)
                    done(act, e3["turned"], s, 2)
                    for i in range(2):
                        last = relu_by_component(h2[:, a, i, 1:ROW], xg[:, s.slot(0, 4), i, :], rs[:, 0, a], i)
                    last.then_inc(e3["relu"].sem, 1)
                    done(act, e3["a_done"], s, 0)
                    done(act, e3["b"], s, 2)
                    nc.scalar.copy(asb[:, a].rearrange("p a k c -> p (a k c)"), bank[2][:])
                    s_act(asq[:, a].rearrange("p a k c -> p (a k c)"), bank[2][:], ACT.Square).then_inc(e3["a"].sem, 1)
                    done(act, e3["turned"], s, 0)
                    done(act, e3["o_done"], s, 2)
                    nc.scalar.copy(ht[:, a, :], bank[0][:]).then_inc(e3["ht"].sem, 1)
                if s.live(1):
                    a = s.slot(1, 2)
                    done(act, e3["b_turned"], s, 1)
                    done(act, e3["o_done"], s, 2)
                    nc.scalar.copy(bt[:], bank[3][:]).then_inc(e3["bt"].sem, 1)
                    done(act, e3["o_done"], s, 1)
                    done(act, e3["summed"], s, 3)
                    landed(act, eo_out, s, 3)
                    o = bank[6][:].rearrange("p (a d) -> p a d", a=2)
                    s_act(osb[:, a, :, 0:D], o, ACT.Square)
                    nc.scalar.copy(osb[:, a, :, D:2 * D], o).then_inc(e3["o"].sem, 1)

            run(act, S, 1, e3_step)

            for i in range(2):
                act.wait_ge(fs["var"].sem, i + 1)
                s_act(fin[:, 6 + i, :], fin[:, 4 + i, :], ACT.Sqrt, bias=eps_col[:]).then_inc(fs["root"].sem, 1)

            def p2_step(s):
                if s.live(1):
                    for q in range(2):
                        act.wait_ge(p2["turned"].sem, s.at(1) * 2 + q + 1)
                        if s.live(2):
                            act.wait_ge(p2["y"].sem, s.at(2) * 2 + q + 1)
                        nc.scalar.copy(ht[:, q, :], bank[q][:]).then_inc(p2["ht"].sem, 1)
                if s.live():
                    a = s.slot(0, 2)
                    root(p2, "", 0, a, J, s)
                    done(act, p2["norm"], s, 0)
                    done(act, p2["turned"], s, 2, per=2)
                    for j in range(J):
                        last = relu_by_component(hb[:, a, j, :], xj(big, s.slot(0, 4), ROW)[:, j, :], rs[:, 0, a], j)
                    last.then_inc(p2["relu"].sem, 1)

            run(act, G, 1, p2_step)

        @block.vector
        def _(dve):
            v = nc.vector
            link = Chain(dve, pre["dve_chain"])

            dve.wait_ge(pre["consts"].sem, n_consts[0])
            dve.wait_ge(pre["inputs"].sem, LOADED)
            v.tensor_copy(trash[:], trash_i[:])
            v.tensor_copy(pair_no[:], pair_i[:])
            v.tensor_scalar(vm1[:], valid[:], -1.0, None, ALU.add)
            v.tensor_copy(dst_f[:], idx3[:, :, 1])
            link(v.tensor_copy(src_f[:], idx3[:, :, 2]))
            v.tensor_tensor(dst_c[:], dst_f[:], valid[:], ALU.mult)
            link(v.tensor_tensor(src_c[:], src_f[:], valid[:], ALU.mult))
            link(v.scalar_tensor_tensor(out=idx3[:, :, 0], in0=vm1[:], scalar=-float(TRASH + P - 1), in1=dst_c[:],
                                        op0=ALU.mult, op1=ALU.add))
            v.tensor_tensor(dst_c[:], dst_c[:], vm1[:], ALU.add)
            v.tensor_tensor(src_c[:], src_c[:], vm1[:], ALU.add)
            for delta, index in ((dst_delta, dst_f), (src_delta, src_f)):
                for i in range(2):
                    v.tensor_scalar(delta[:].rearrange("p (s a) -> p a s", a=2)[:, i],
                                    index[:].rearrange("p (s a) -> p a s", a=2)[:, i], trash[:, i:i + 1], None,
                                    ALU.subtract)
            for col, lo, hi in ((1, lo_d, hi_d), (2, lo_s, hi_s)):
                link(v.tensor_scalar(int_a[:], idx3[:, :, col], 2, P - 1, ALU.logical_shift_right, ALU.bitwise_and))
                link(v.tensor_copy(lo[:], int_a[:]))
                link(v.tensor_tensor(lo[:], lo[:], valid[:], ALU.mult))
                v.tensor_tensor(lo[:], lo[:], vm1[:], ALU.add)
                v.tensor_scalar(int_a[:], idx3[:, :, col], 9, 2, ALU.logical_shift_right, ALU.logical_shift_left)
                link(v.tensor_scalar(int_b[:], idx3[:, :, col], J - 1, None, ALU.bitwise_and))
                link(v.tensor_tensor(int_a[:], int_a[:], int_b[:], ALU.bitwise_or))
                link(v.tensor_copy(hi[:], int_a[:]))
            v.tensor_copy(int_b[:], int_a[:]).then_inc(pre["prepared"].sem, 1)

            link(v.tensor_copy(b_bf[:, 0, :], b_f[:, 0, :]))
            link(v.tensor_tensor(b_f[:, 1, :], b_f[:, 0, :], b_bf[:, 0, :], ALU.subtract))
            link(v.tensor_copy(b_bf[:, 1, :], b_f[:, 1, :]))
            link(v.tensor_tensor(b_f[:, 2, :], b_f[:, 1, :], b_bf[:, 1, :], ALU.subtract))
            v.tensor_copy(b_bf[:, 2, :], b_f[:, 2, :]).then_inc(pre["b_split"].sem, 1)

            c0 = cw[:, 0:5 * C].rearrange("p (c k) -> p k c", k=5)
            c1 = cw[:, 5 * C:9 * C].rearrange("p (c k) -> p k c", k=4)
            for i, k in enumerate((0, 1, 3, 4)):
                v.tensor_copy(poly[:, i, 0, :], c0[:, k])
                v.tensor_copy(poly[:, i, 1, :], c1[:, i])
            link(v.tensor_copy(poly_vv[:, 0, :], c0[:, 2]))

            def onehot_step(s):
                if s.live():
                    done(dve, cnt["counted"], s, 2)
                    for i in range(2):
                        for which, lo, hi in ((0, lo_d, hi_d), (1, lo_s, hi_s)):
                            o = onehot[:, s.slot(0, 2), i, which, :]
                            v.tensor_scalar(o[:, 0:P], iota_h[:, 0:P], lo[:, bass.ds(s.at() * 2 + i, 1)], None,
                                            ALU.is_equal)
                            last = v.tensor_scalar(o[:, P:P + G * J], iota_h[:], hi[:, bass.ds(s.at() * 2 + i, 1)],
                                                   None, ALU.is_equal)
                    last.then_inc(cnt["onehot"].sem, 1)

            run(dve, S, 0, onehot_step)

            dve.wait_ge(cnt["counted"].sem, S)
            ends, starts = bank[0][:, 0:G * J], bank[1][:, 0:G * J]
            v.tensor_scalar(deg[:], ends, 1.0, None, ALU.add).then_inc(pre["deg"].sem, 1)
            v.tensor_scalar(no_dst[:], ends, 0.0, None, ALU.is_equal)
            v.tensor_scalar(w_src[:], starts, 1.0, None, ALU.max)
            link(v.scalar_tensor_tensor(out=alone[:], in0=starts, scalar=0.0, in1=node_ok[:], op0=ALU.is_equal,
                                        op1=ALU.mult))
            v.tensor_tensor(alone[:], alone[:], no_dst[:], ALU.mult)
            link(v.reciprocal(w_src[:], w_src[:]))
            link(v.tensor_tensor(w_src[:], w_src[:], no_dst[:], ALU.mult))
            dve.wait_ge(pre["root"].sem, 1)
            link(v.reciprocal(dinv[:], deg[:]))
            v.tensor_tensor(dinv2[:], dinv[:], dinv[:], ALU.mult).then_inc(pre["dinv"].sem, 1)
            dve.wait_ge(pre["dinv"].sem, 1)

            def stats(sm, chain, signal, k, a, rows, s, d=0):
                one = Chain(dve, sm[chain], 1, s.at(d))
                for j, row in enumerate(rows):
                    last = v.bn_stats(st[:, k, j, :], row)
                one(last)
                settle(dve)
                for j in range(len(rows)):
                    last = v.bn_aggr(mv[:, k, a, j, :], st[:, k, j, :])
                last.then_inc(sm[signal].sem, 1)
                one.end()

            def norm(sm, a, n, s):
                one = Chain(dve, sm["chain_b"], 1, s.at())
                done(dve, sm["root1" if sm is p1 else "root"], s, 0)
                one(v.reciprocal(rs[:, 0, a, 0, 0:n], sd[:, 0, a, 0:n]))
                v.scalar_tensor_tensor(out=rs[:, 0, a, 1, 0:n], in0=mv[:, 0, a, 0:n, 0], scalar=-1.0,
                                       in1=rs[:, 0, a, 0, 0:n], op0=ALU.mult, op1=ALU.mult
                                       ).then_inc(sm["norm1" if sm is p1 else "norm"].sem, 1)
                one.end()

            def p1_step(s):
                if s.live():
                    landed(dve, x_in, s)
                    stats(p1, "chain_a", "stats1", 0, s.slot(0, 2),
                          [xj(big, s.slot(0, 4), D)[:, j, :] for j in range(J)], s)
                if s.live(2):
                    a = s.slot(2, 2)
                    one = Chain(dve, p1["chain_n"], 2, s.at(2))
                    done(dve, p1["root2"], s, 2)
                    one(v.reciprocal(rs[:, 1, a, 0, :], sd[:, 1, a, :]))
                    one(v.tensor_tensor(rs[:, 1, a, 1, :], rs[:, 1, a, 0, :], alone[:, bass.ds(s.at(2) * J, J)],
                                        ALU.mult))
                    v.scalar_tensor_tensor(out=rs[:, 1, a, 2, :], in0=mv[:, 1, a, :, 0], scalar=-1.0,
                                           in1=rs[:, 1, a, 1, :], op0=ALU.mult, op1=ALU.mult
                                           ).then_inc(p1["norm2"].sem, 1)
                    one.end()
                if s.live():
                    norm(p1, s.slot(0, 2), J, s)
                if s.live(1):
                    a = s.slot(1, 2)
                    x1 = xj(x1b, a, ROW)
                    landed(dve, x1_out, s, 3)
                    done(dve, p1["relu2"], s, 3)
                    v.tensor_copy(x1[:, :, D], w_src[:, bass.ds(s.at(1) * J, J)])
                    for q in range(2):
                        dve.wait_ge(p1["xw"].sem, s.at(1) * 2 + q + 1)
                        for i in range(2):
                            j = 2 * q + i
                            last = v.scalar_tensor_tensor(
                                out=x1[:, j, 0:D], in0=bank[2 + q][:, i * D:(i + 1) * D],
                                scalar=dinv2[:, bass.ds(s.at(1) * J + j, 1)], in1=xj(big, s.slot(1, 4), D)[:, j, :],
                                op0=ALU.mult, op1=ALU.add)
                    last.then_inc(p1["x1"].sem, 1)
                    done(dve, p1["x1"], s, 1)
                    stats(p1, "chain_m", "stats2", 1, a, [x1[:, j, 0:D] for j in range(J)], s, 1)

            run(dve, G, 2, p1_step)

            def same_index(sm, s, index):
                done(dve, sm["others"], s, 0)
                done(dve, sm["merged"], s, 4)
                for i in range(2):
                    last = v.tensor_scalar(eq[:, s.slot(0, 4), i, :], bank[6][:, 0:2 * P],
                                           own[:, s.slot(0, 2), i:i + 1], None, ALU.is_equal)
                last.then_inc(sm["eq"].sem, 1)

            def scatter_to(sm, out_sems, s, delta):
                one = Chain(dve, sm["chain_c"], 3, s.at())
                done(dve, sm["eq"], s, 0)
                for i in range(2):
                    last = v.tensor_tensor_reduce(out=eq_junk[:, i, :], in0=eq[:, s.slot(0, 4), i, :],
                                                  in1=later[:, i, :], scale=1.0, scalar=0.0, op0=ALU.mult,
                                                  op1=ALU.add, accum_out=n_later[:, i:i + 1])
                one(last)
                one(v.scalar_tensor_tensor(out=pair(first_in_pair, s), in0=n_later[:], scalar=0.0,
                                           in1=pair(valid, s), op0=ALU.is_equal, op1=ALU.mult))
                one(v.tensor_tensor(sidx_f[:], pair(first_in_pair, s), pair(delta, s), ALU.mult))
                landed(dve, out_sems, s, 4, dmas=2)
                v.tensor_tensor(sidx[:, s.slot(0, 4), :], sidx_f[:], trash[:], ALU.add).then_inc(sm["sidx"].sem, 1)
                one.end()

            def take_own(sm, s, index):
                done(dve, sm["others"], s, 2)
                v.tensor_copy(own[:, s.slot(0, 2), :], pair(index, s)).then_inc(sm["own"].sem, 1)
                done(dve, sm["own"], s, 0)

            dve.wait_ge(p1["dinv_got"].sem, T)

            def e1_step(s):
                if s.live():
                    take_own(e1, s, src_c)
                    landed(dve, e1_got, s, 0, dmas=2)
                    stats(e1, "chain_a", "stats", 0, s.slot(0, 2),
                          [xg[:, s.slot(0, 4), i, 0:D] for i in range(2)], s)
                    same_index(e1, s, src_c)
                    norm(e1, s.slot(0, 2), 2, s)
                    done(dve, e1["v"], s, 2)
                    c = pair(dinv_edge, s)
                    v.tensor_tensor(coef[:, s.slot(0, 2), :], c[:, :, 0], c[:, :, 1], ALU.mult
                                    ).then_inc(e1["coef"].sem, 1)
                    scatter_to(e1, e1_out, s, src_delta)

            run(dve, S, 0, e1_step)

            def e2_step(s):
                if s.live():
                    take_own(e2, s, dst_c)
                    landed(dve, e2_got, s, 0, dmas=2)
                    stats(e2, "chain_a", "stats", 0, s.slot(0, 2),
                          [xg[:, s.slot(0, 4), i, 0:D] for i in range(2)], s)
                    same_index(e2, s, dst_c)
                    norm(e2, s.slot(0, 2), 2, s)
                    scatter_to(e2, e2_out, s, dst_delta)
                if s.live(1):
                    one = Chain(dve, e2["chain_m"], 4, s.at(1))
                    done(dve, e2["up"], s, 1)
                    landed(dve, tp_in, s, 1)
                    w = tpb[:, s.slot(1, 2)]
                    up = bank[2 + s.slot(1, 2)][:].rearrange("p (a k c) -> p a k c", a=2, k=4)
                    m = msg_in[:, s.slot(1, 4), :, 0:D].rearrange("p a (k c) -> p a k c", k=4)

                    def sh(i, k):
                        return ea4_sb[:, bass.ds((s.at(1) * 2 + i) * 4 + k, 1)]

                    for i in range(2):
                        v.tensor_scalar(dot[:, i, :], up[:, i, 1, :], sh(i, 1), None, ALU.mult)
                        v.tensor_scalar(scaled_w[:, i], w[:, i, 0:4:2, :], sh(i, 0), None, ALU.mult)
                    one(v.tensor_tensor(tmp_a[:], w[:, :, 1, :], up[:, :, 0, :], ALU.mult))
                    for i in range(2):
                        v.scalar_tensor_tensor(out=dot[:, i, :], in0=up[:, i, 2, :], scalar=sh(i, 2),
                                               in1=dot[:, i, :], op0=ALU.mult, op1=ALU.add)
                        v.tensor_tensor(m[:, i, 1:4, :], scaled_w[:, i, 1:2, :].to_broadcast([P, 3, C]),
                                        up[:, i, 1:4, :], ALU.mult)
                    one(v.tensor_tensor(m[:, :, 0, :], scaled_w[:, :, 0, :], up[:, :, 0, :], ALU.mult))
                    for i in range(2):
                        last = v.scalar_tensor_tensor(out=dot[:, i, :], in0=up[:, i, 3, :], scalar=sh(i, 3),
                                                      in1=dot[:, i, :], op0=ALU.mult, op1=ALU.add)
                    one(last)
                    for i in range(2):
                        for k in range(1, 4):
                            v.scalar_tensor_tensor(out=m[:, i, k, :], in0=tmp_a[:, i, :], scalar=sh(i, k),
                                                   in1=m[:, i, k, :], op0=ALU.mult, op1=ALU.add)
                    one(v.tensor_tensor(tmp_b[:], w[:, :, 3, :], dot[:], ALU.mult))
                    v.scalar_tensor_tensor(out=m[:, :, 0, :], in0=tmp_b[:], scalar=INV3, in1=m[:, :, 0, :],
                                           op0=ALU.mult, op1=ALU.add).then_inc(e2["message"].sem, 1)
                    one.end()

            run(dve, S, 1, e2_step)

            def e3_step(s):
                if s.live():
                    landed(dve, e3_got, s, 0, dmas=4)
                    stats(e3, "chain_a", "stats", 0, s.slot(0, 2),
                          [xg[:, s.slot(0, 4), i, 0:D] for i in range(2)], s)
                    one = Chain(dve, e3["chain_c"], 3, s.at())
                    one(v.tensor_tensor(lead_f[:], msg_in[:, s.slot(0, 4), :, D], pair(pair_no, s), ALU.is_equal))
                    done(dve, e3["summed"], s, 4)
                    one(v.tensor_tensor(lead[:, s.slot(0, 4), :], lead_f[:], pair(first_in_pair, s), ALU.mult))
                    one(v.scalar_tensor_tensor(out=sidx_f[:], in0=pair(dst_f, s), scalar=-float(NOWHERE),
                                               in1=lead[:, s.slot(0, 4), :], op0=ALU.add, op1=ALU.mult))
                    v.tensor_scalar(pair(final_idx, s), sidx_f[:], float(NOWHERE), None, ALU.add
                                    ).then_inc(e3["lead"].sem, 1)
                    one.end()
                    norm(e3, s.slot(0, 2), 2, s)
                if s.live(1):
                    a = s.slot(1, 2)
                    one = Chain(dve, e3["chain_p"], 6, s.at(1))
                    done(dve, e3["a"], s, 1)
                    done(dve, e3["b_turned"], s, 3)
                    A, Q, B = asb[:, a], asq[:, a], bsb[:, a]

                    def coefficients(i):
                        return poly[:, i].unsqueeze(1).to_broadcast([P, 2, 2, C])

                    def both(t):
                        return t.unsqueeze(2).to_broadcast([P, 2, 2, C])

                    one(v.tensor_tensor(vv[:], Q[:, :, 1, :], Q[:, :, 2, :], ALU.add))
                    v.tensor_tensor(term[:, 0], coefficients(1), both(A[:, :, 0, :]), ALU.mult)
                    v.tensor_tensor(term[:, 1], coefficients(2), both(Q[:, :, 0, :]), ALU.mult)
                    one(v.tensor_tensor(vv[:], vv[:], Q[:, :, 3, :], ALU.add))
                    v.tensor_tensor(tmp_a[:], poly_vv[:].to_broadcast([P, 2, C]), vv[:], ALU.mult)
                    v.tensor_tensor(term[:, 0], term[:, 0], coefficients(0), ALU.add)
                    one(v.tensor_tensor(term[:, 2], coefficients(3), both(vv[:]), ALU.mult))
                    one(v.tensor_tensor(term[:, 1], term[:, 1], term[:, 2], ALU.add))
                    one(v.tensor_tensor(term[:, 0], term[:, 0], term[:, 1], ALU.add))
                    for i in range(2):
                        v.tensor_tensor(B[:, i, 1:4, :], term[:, 0, i, 1:2, :].to_broadcast([P, 3, C]),
                                        A[:, i, 1:4, :], ALU.mult)
                    one(v.tensor_tensor(tmp_b[:], term[:, 0, :, 0, :], A[:, :, 0, :], ALU.mult))
                    v.tensor_tensor(B[:, :, 0, :], tmp_a[:], tmp_b[:], ALU.add).then_inc(e3["b"].sem, 1)
                    one.end()

            run(dve, S, 1, e3_step)

            one = Chain(dve, fs["chain"])
            dve.wait_ge(e2["gram"].sem, S)
            dve.wait_ge(e3["summed"].sem, S)
            v.tensor_copy(g_sb[:, 0, :], gram0[0:C, 0:C + 1])
            v.tensor_copy(row_sb[:], bank[7][0:1, 0:5 * C])
            v.tensor_copy(g_sb[:, 1, 0:C], gram1[0:C, 0:C]).then_inc(fs["grams"].sem, 1)
            dve.wait_ge(fs["grams"].sem, 1)
            dve.wait_ge(fs["products"].sem, 2)
            for i in range(2):
                v.tensor_tensor(z_sb[:, i, :], sc64[:, i, :], bank[i][0:C, 0:C], ALU.mult)
            v.tensor_scalar(z_sb[:, 2, :], sc64[:, 0, :], g_sb[:, 0, 0:1], None, ALU.mult).then_inc(fs["z"].sem, 1)
            dve.wait_ge(fs["sums"].sem, 1)
            one(v.tensor_copy(slot_sum[:], bank[3][:, 0:5 * C]))
            whole = bank[2]
            v.tensor_tensor(fin[:, 0, :], whole[:, 2 * C:3 * C], slot_sum[:, 4 * C:5 * C], ALU.add)
            v.tensor_tensor(fin[:, 1, :], whole[:, 0:C], slot_sum[:, 0:C], ALU.add)
            v.tensor_tensor(fin[:, 2, :], whole[:, C:2 * C], slot_sum[:, C:2 * C], ALU.add)
            one(v.tensor_tensor(fin[:, 3, :], slot_sum[:, 2 * C:3 * C], slot_sum[:, 3 * C:4 * C], ALU.add))
            v.tensor_scalar(fin[:, 0, :], fin[:, 0, :], 1.0 / N, None, ALU.mult)
            v.tensor_scalar(fin[:, 1, :], fin[:, 1, :], 1.0 / N, None, ALU.mult)
            one(v.tensor_tensor(fin[:, 2, :], fin[:, 2, :], fin[:, 3, :], ALU.add))
            v.tensor_scalar(fin[:, 5, :], fin[:, 2, :], 1.0 / (3 * N), None, ALU.mult)
            one(v.tensor_tensor(fin[:, 4, :], fin[:, 0, :], fin[:, 0, :], ALU.mult))
            v.tensor_tensor(fin[:, 4, :], fin[:, 1, :], fin[:, 4, :], ALU.subtract).then_inc(fs["var"].sem, 2)
            dve.wait_ge(fs["root"].sem, 2)
            one(v.reciprocal(fin[:, 6:8, :], fin[:, 6:8, :]))
            v.tensor_tensor(scale[:, 0, :], fin[:, 6, :], g_b[:, 0, :], ALU.mult)
            for k in range(1, 4):
                last = v.tensor_tensor(scale[:, k, :], fin[:, 7, :], g_b[:, 2, :], ALU.mult)
            one(last)
            one(v.tensor_tensor(bias[:], fin[:, 0, :], scale[:, 0, :], ALU.mult))
            v.tensor_tensor(fin_w[:].rearrange("p a c -> p (a c)"), sc_w[:].rearrange("p a c -> p (a c)"),
                            scale[:].rearrange("p a c -> p (a c)"), ALU.mult)
            v.tensor_tensor(bias[:], g_b[:, 1, :], bias[:], ALU.subtract).then_inc(fs["weights"].sem, 1)
            dve.wait_ge(fs["weights"].sem, 1)

            def p2_step(s):
                if s.live():
                    landed(dve, y_in, s)
                    stats(p2, "chain_a", "stats", 0, s.slot(0, 2),
                          [xj(big, s.slot(0, 4), ROW)[:, j, 0:D] for j in range(J)], s)
                    norm(p2, s.slot(0, 2), J, s)
                if s.live(1):
                    landed(dve, y_out, s, 3)
                    o, x1 = xj(x1b, s.slot(1, 2), D), xj(big, s.slot(1, 4), ROW)
                    for q in range(2):
                        dve.wait_ge(p2["y"].sem, s.at(1) * 2 + q + 1)
                        y = bank[2 + q][:].rearrange("p (j d) -> p j d", j=2)
                        v.tensor_tensor(o[:, 2 * q:2 * q + 2, 0:C], y[:, :, 0:C], x1[:, 2 * q:2 * q + 2, 0:C], ALU.add)
                        for i in range(2):
                            j = 2 * q + i
                            last = v.tensor_tensor(o[:, j, C:D].rearrange("p (c x) -> p c x", x=3),
                                                   y[:, i, C:D].rearrange("p (x c) -> p c x", x=3),
                                                   x1[:, j, C:D].rearrange("p (c x) -> p c x", x=3), ALU.add)
                    last.then_inc(p2["out"].sem, 1)

            run(dve, G, 1, p2_step)

            def f_step(s):
                if s.live():
                    a = s.slot(0, 2)
                    one = Chain(dve, f["chain"], 2, s.at())
                    landed(dve, f_in, s, 0, dmas=2)
                    one(v.tensor_tensor(vb[:, a], vb[:, a], scale[:].rearrange("p k c -> p (k c)").unsqueeze(1)
                                        .to_broadcast([P, 2, D]), ALU.mult))
                    landed(dve, f_out, s, 2, dmas=2)
                    for i in range(2):
                        v.tensor_tensor(hg[:, a, i, C:D].rearrange("p (c x) -> p c x", x=3),
                                        vb[:, a, i, C:D].rearrange("p (x c) -> p c x", x=3),
                                        xg[:, a, i, C:D].rearrange("p (c x) -> p c x", x=3), ALU.add)
                    one(v.tensor_tensor(hg[:, a, :, 0:C], vb[:, a, :, 0:C], xg[:, a, :, 0:C], ALU.add))
                    v.tensor_tensor(hg[:, a, :, 0:C], hg[:, a, :, 0:C], bias[:].unsqueeze(1).to_broadcast([P, 2, C]),
                                    ALU.add).then_inc(f["rows"].sem, 1)
                    one.end()

            run(dve, S, 0, f_step)


_INS = ["x", "src", "dst", "edge_attr_16", "edge_attr_4", "L0_gnn_W", "L0_gnn_b", "L1_gnn_W_up0", "L1_gnn_W_up1",
        "L1_gnn_M1", "L1_gnn_M2", "L1_gnn_M3", "L1_gnn_M4", "L1_gnn_W_lin0", "L1_gnn_W_lin1", "L1_gnn_Wsc0",
        "L1_gnn_Wsc1", "L1_gnn_Wc0", "L1_gnn_Wc1", "L1_gnn_WB0", "L1_gnn_WB1", "L1_gnn_gamma0", "L1_gnn_beta0",
        "L1_gnn_gamma1"]


def kernel(**inputs):
    import numpy as _np
    import concourse.bacc as _bacc
    from concourse import mybir as _mybir
    from concourse.bass_utils import run_bass_kernel_spmd as _run

    nc = _bacc.Bacc("TRN2", target_bir_lowering=False, num_devices=1)
    arrays, args = {}, []
    for name in _INS:
        a = _np.ascontiguousarray(inputs[name])
        arrays[f"in_{name}_dram"] = a
        args.append(nc.dram_tensor(f"in_{name}_dram", a.shape, _mybir.dt.from_np(a.dtype), kind="ExternalInput").ap())
    args.append(nc.dram_tensor("out_0_dram", (N, D), _mybir.dt.float32, kind="ExternalOutput").ap())
    build(nc, *args)
    r = _run(nc, [arrays], core_ids=[0])
    return r.results[0]["out_0_dram"]
```

```python
from contextlib import ExitStack

import concourse.bass as bass
from concourse import mybir

ALU = mybir.AluOpType
ACT = mybir.ActivationFunctionType
F32 = mybir.dt.float32
BF16 = mybir.dt.bfloat16
F16 = mybir.dt.float16
I32 = mybir.dt.int32

P = 128
N = 50000
E = 12500
D = 256
C = 64
R = 16
J = 4
NG = P * J
G = -(-N // NG)
TAIL = N - (G - 1) * NG
TAILP = TAIL // J
T = -(-E // P)
T += T % 2
S = T // 2
LASTP = E - (P - 1) * T
PAD = T - LASTP
ROW = D + 1
TRASH = N
MSG_ROWS = -(-(N + 2 * P) // P)
ZERO_ROWS = 8
EPS = 1e-5
INV3 = 3.0 ** -0.5
U = 4
NOWHERE = 1 << 20
assert TAIL == TAILP * J and 0 < LASTP < T and S * ZERO_ROWS < MSG_ROWS <= (S + 1) * ZERO_ROWS


class Step:

    def __init__(self, b, u, k, n, looped=False):
        self.b, self.u, self.k, self.n, self.looped = b, u, k, n, looped

    def at(self, d=0):
        return self.b * U + (self.u - d)

    def live(self, d=0):
        assert not self.looped or self.k >= d, "more steps have to come before the loop"
        return 0 <= self.k - d < self.n

    def slot(self, d, m):
        return (self.u - d) % m

    def uses(self, d, m):
        return self.b * (U // m) + (self.u - d) // m + 1


def run(eng, n, skew, body, first=2):
    hi = n // U - (1 if n % U == 0 else 0)
    for s in range(first * U):
        body(Step(s // U, s % U, s, n))
    with eng.Fori(first, hi, 1) as b:
        for u in range(U):
            body(Step(b, u, first * U + u, n, looped=True))
    for s in range(hi * U, n + skew):
        body(Step(s // U, s % U, s, n))


class Signal:

    def __init__(self, sem, base=0):
        self.sem, self.base = sem, base


def done(eng, sem, s, d=0, per=1):
    if s.live(d):
        eng.wait_ge(sem.sem, s.at(d) * per + (per + sem.base))


def landed(eng, slots, s, d=0, dmas=1):
    if s.live(d):
        eng.wait_ge(slots[s.slot(d, len(slots))], s.uses(d, len(slots)) * (16 * dmas))


def all_landed(eng, slots, n, dmas=1):
    for i, one in enumerate(slots):
        eng.wait_ge(one, 16 * dmas * len(range(i, n, len(slots))))


class Chain:

    def __init__(self, eng, sem, per=0, i=0):
        self.eng, self.sem, self.base, self.per, self.k = eng, sem.sem, i * per + sem.base, per, 0

    def __call__(self, instruction):
        self.k += 1
        instruction.then_inc(self.sem, 1)
        self.eng.wait_ge(self.sem, self.base + self.k)

    def end(self):
        assert self.k == self.per, self.k


def build(nc, x, src, dst, ea16, ea4, W, b, Wup0, Wup1, M1, M2, M3, M4, Wlin0, Wlin1, Wsc0, Wsc1,
          Wc0, Wc1, WB0, WB1, gamma0, beta0, gamma1, out):
    with ExitStack() as ctx:
        def sb(name, shape, dt=F32):
            return ctx.enter_context(nc.sbuf_tensor(name, shape, dt))

        def sem(name):
            return ctx.enter_context(nc.semaphore(name))

        def sems(name, n):
            return [sem(f"{name}{i}") for i in range(n)]

        def named(prefix, names):
            return {n: Signal(sem(f"{prefix}_{n}")) for n in names.split()}

        def after(signals, names):
            return {n: Signal(signals[n].sem, signals[n].base + S) for n in names.split()}

        def dram(name, shape, dt=F32):
            return nc.dram_tensor(name, shape, dt, kind="Internal").ap()

        x1_tab = dram("x1_tab", [N + 2 * P, ROW])
        msg_tab = dram("msg_tab", [P * MSG_ROWS, ROW])
        dinv_tab = dram("dinv_tab", [G * NG, 1])
        tpw_tab = dram("tpw_tab", [S, P, 2 * D])
        edge_o = dram("edge_o", [S, P, 2 * D])
        edge_x = dram("edge_x", [S, P, 2 * ROW])

        ident = sb("ident", [P, P])
        later = sb("later", [P, 2, 2 * P])
        ones = sb("ones", [P, P])
        ones_bf = sb("ones_bf", [3, P], BF16)
        eps_col = sb("eps_col", [P, 1])
        iota_h = sb("iota_h", [P, G * J], F16)
        trash_i = sb("trash_i", [P, 2], I32)
        trash = sb("trash", [P, 2])
        pair_i = sb("pair_i", [P, T], I32)
        pair_no = sb("pair_no", [P, T])
        valid = sb("valid", [P, T])
        vm1 = sb("vm1", [P, T])
        node_ok = sb("node_ok", [P, G * J])
        zeros = sb("zeros", [P, ZERO_ROWS * ROW])
        w_sb = sb("w_sb", [P, 2, D])
        b_f = sb("b_f", [3, 3, D])
        b_bf = sb("b_bf", [3, 3, D], BF16)
        b3 = sb("b3", [3, D], BF16)
        bias_f = sb("bias_f", [3, 3, C])
        bias_bf = sb("bias_bf", [3, 3, C], BF16)
        bias3 = sb("bias3", [3, C], BF16)
        up_w = sb("up_w", [P, 2, P])
        lin_w = sb("lin_w", [P, 2, P])
        sc_w = sb("sc_w", [P, 2, P])
        wb_w = sb("wb_w", [P, 2, P])
        fin_w = sb("fin_w", [P, 2, P])
        m_sb = [sb("m1_sb", [R, C]), sb("m2_sb", [C, C]), sb("m3_sb", [C, C])]
        m4_sb = sb("m4_sb", [C, 4 * C])
        sc64 = sb("sc64", [C, 2, C])
        cw = sb("cw", [P, 9 * C])
        poly = sb("poly", [P, 4, 2, C])
        poly_vv = sb("poly_vv", [P, 1, C])
        g_b = sb("g_b", [P, 3, C])

        idx3 = sb("idx3", [P, 3, T], I32)
        src_c = sb("src_c", [P, T])
        dst_c = sb("dst_c", [P, T])
        src_f = sb("src_f", [P, T])
        dst_f = sb("dst_f", [P, T])
        src_delta = sb("src_delta", [P, T])
        dst_delta = sb("dst_delta", [P, T])
        int_a = sb("int_a", [P, T], I32)
        int_b = sb("int_b", [P, T], I32)
        lo_d, hi_d, lo_s, hi_s = (sb(n, [P, T]) for n in ("lo_d", "hi_d", "lo_s", "hi_s"))
        first_in_pair = sb("first_in_pair", [P, T])
        dinv_edge = sb("dinv_edge", [P, T, 2])
        final_idx = sb("final_idx", [P, T], I32)
        ea16_sb = sb("ea16_sb", [P, T * R])
        ea4_sb = sb("ea4_sb", [P, T * 4])
        deg = sb("deg", [P, G * J])
        dinv = sb("dinv", [P, G * J])
        dinv2 = sb("dinv2", [P, G * J])
        alone = sb("alone", [P, G * J])
        no_dst = sb("no_dst", [P, G * J])
        w_src = sb("w_src", [P, G * J])

        onehot = sb("onehot", [P, 2, 2, 2, P + G * J], BF16)
        rbf = sb("rbf", [P, 2, 2 * R])
        mlp_t = sb("mlp_t", [C, 4, 2 * P])
        tpb = sb("tpb", [P, 2, 2, 4, C])
        big = sb("big", [P, 4, J * ROW])
        hb = sb("hb", [P, 2, J, D])
        ht = sb("ht", [P, 4, 4 * P])
        x1b = sb("x1b", [P, 2, J * ROW])
        h2b = sb("h2b", [P, 2, J, ROW])
        st = sb("st", [P, 2, J, 6])
        mv = sb("mv", [P, 2, 2, J, 2])
        sd = sb("sd", [P, 2, 2, J])
        rs = sb("rs", [P, 2, 2, 3, J])
        idx = sb("idx", [P, 2, 3], I32)
        idx_e = sb("idx_e", [P, 2, 2], I32)
        got = sb("got", [P, 2, 2])
        claim = sb("claim", [P, 2, ROW])
        xg = sb("xg", [P, 4, 2, ROW])
        msg_in = sb("msg_in", [P, 4, 2, ROW])
        hg = sb("hg", [P, 2, 2, D])
        h2 = sb("h2", [P, 2, 2, ROW])
        hw = sb("hw", [P, 2, 2, D])
        vb = sb("vb", [P, 2, 2, D])
        own = sb("own", [P, 2, 2])
        sidx_f = sb("sidx_f", [P, 2])
        sidx = sb("sidx", [P, 4, 2], I32)
        eq = sb("eq", [P, 4, 2, 2 * P])
        eq_junk = sb("eq_junk", [P, 2, 2 * P])
        n_later = sb("n_later", [P, 2])
        coef = sb("coef", [P, 4, 2])
        addb = sb("addb", [P, 4, 2, ROW])
        dot = sb("dot", [P, 2, C])
        scaled_w = sb("scaled_w", [P, 2, 2, C])
        tmp_a = sb("tmp_a", [P, 2, C])
        tmp_b = sb("tmp_b", [P, 2, C])
        mt, bt = (hb[:, a, 0:2, :].rearrange("p j d -> p (j d)") for a in range(2))
        asb, asq = (x1b[:, :, i * 2 * D:(i + 1) * 2 * D].rearrange("p s (a k c) -> p s a k c", a=2, k=4)
                    for i in range(2))
        vv = sb("vv", [P, 2, C])
        term = sb("term", [P, 3, 2, 2, C])
        bsb = sb("bsb", [P, 2, 2, 4, C])
        osb = sb("osb", [P, 2, 2, 2 * D])
        lead_f = sb("lead_f", [P, 2])
        lead = sb("lead", [P, T])
        g_sb = sb("g_sb", [C, 2, C + 1])
        z_sb = sb("z_sb", [C, 3, C])
        row_sb = sb("row_sb", [1, 5 * C])
        slot_sum = sb("slot_sum", [P, 5 * C])
        fin = sb("fin", [P, 8, C])
        scale = sb("scale", [P, 4, C])
        bias = sb("bias", [P, C])

        bank = [ctx.enter_context(nc.psum_tensor(f"bank{i}", [P, 512], F32)) for i in range(8)]
        gram0, gram1 = bank[4][:, 0:P], bank[4][:, P:2 * P]

        spread = (bank[6], bank[1])
        o_bank = (bank[6], bank[5])

        def xj(t, slot, width):
            return t[:, slot, 0:J * width].rearrange("p (j d) -> p j d", j=J)

        def by_component(rows):
            return rows.rearrange("p (c x) -> p x c", x=3)

        def groups(table):
            return (table[0:(G - 1) * NG, :].rearrange("(g p j) d -> g p (j d)", p=P, j=J),
                    table[(G - 1) * NG:N, :].rearrange("(p j) d -> p (j d)", j=J))

        x_groups, out_groups, x1_groups = groups(x), groups(out), groups(x1_tab)

        def group(table, s, d=0):
            return (table[1], TAILP) if s.k - d == G - 1 else (table[0][s.at(d)], P)

        def pair(t, s, d=0):
            return t[:, bass.ds(s.at(d) * 2, 2)]

        def rows_of(index):
            return bass.IndirectOffsetOnAxis(ap=index, axis=0)
        edge_loads, loads = [], []
        for col, e in ((1, dst), (2, src)):
            edge_loads += [(idx3[0:P - 16, col, :], e[0:(P - 16) * T].rearrange("(p t) -> p t", t=T)),
                      (idx3[P - 16:P - 1, col, :], e[(P - 16) * T:(P - 1) * T].rearrange("(p t) -> p t", t=T)),
                      (idx3[P - 1:P, col, 0:LASTP], e[(P - 1) * T:E].rearrange("(p t) -> p t", p=1)),
                      (idx3[P - 1:P, col, LASTP:T], e[E - PAD:E].rearrange("(p t) -> p t", p=1))]
        for to, e, w in ((ea16_sb, ea16, R), (ea4_sb, ea4, 4)):
            edge_loads += [(to[0:P - 16, :], e[0:(P - 16) * T, :].rearrange("(p t) r -> p (t r)", t=T)),
                      (to[P - 16:P - 1, :], e[(P - 16) * T:(P - 1) * T, :].rearrange("(p t) r -> p (t r)", t=T)),
                      (to[P - 1:P, 0:LASTP * w], e[(P - 1) * T:E, :].rearrange("(p t) r -> p (t r)", p=1)),
                      (to[P - 1:P, LASTP * w:T * w], e[E - PAD:E, :].rearrange("(p t) r -> p (t r)", p=1))]
        loads += [(w_sb[:, i, :], W[i * P:(i + 1) * P, :]) for i in range(2)]
        loads += [(b_f[:, 0, :], b.partition_broadcast(3))]
        for to, w0, w1 in ((up_w, Wup0, Wup1), (lin_w, Wlin0, Wlin1), (sc_w, Wsc0, Wsc1), (wb_w, WB0, WB1)):
            loads += [(to[0:C, 0, 0:C], w0), (to[C:P, 0, C:P], w1), (to[0:C, 1, 0:C], w1), (to[C:P, 1, C:P], w1)]
        loads += [(sc64[:, 0, :], Wsc0), (sc64[:, 1, :], Wsc1)]
        loads += list(zip((m_sb[0][:], m_sb[1][:], m_sb[2][:], m4_sb[:]), (M1, M2, M3, M4)))
        loads += [(cw[:, 0:5 * C], Wc0.rearrange("c k -> (c k)").partition_broadcast(P)),
                  (cw[:, 5 * C:9 * C], Wc1.rearrange("c k -> (c k)").partition_broadcast(P))]
        loads += [(g_b[:, i, :], w.partition_broadcast(P)) for i, w in enumerate((gamma0, beta0, gamma1))]
        LOADED = 16 * len(loads)
        EDGES_LOADED = 16 * len(edge_loads)
        CLEARED = 16 * (S + 2)

        pre = named("pre", "pool_chain dve_chain consts edges inputs prepared b3 cleared deg root dinv dinv_out")
        cnt = named("cnt", "rbf onehot counted turned0 act0 layer1 act1 layer2 act2 layer3 act3 layer4 weights")
        tpw_out = sems("tpw_out", 2)
        p1 = named("p1", "chain_a chain_b chain_m chain_n stats1 root1 norm1 relu1 turned ht xw x1 stats2 root2 norm2 "
                         "relu2 gram idx dinv_got")
        x_in, x1_out, claim_out, dinv_in = sems("x_in", 4), sems("x1_out", 2), sems("claim_out", 1), sems("dinv_in", 2)
        e1 = named("e1", "idx own others chain_a chain_b chain_c eq sidx coef stats root norm relu turned ht xw v "
                         "merged add")
        e1_got, e1_out = sems("e1_got", 4), sems("e1_out", 1)
        e2 = named("e2", "chain_m weighted up gram message")
        e2 |= after(e1, "idx own others eq sidx stats root norm relu turned ht merged add")
        e2_got, e2_out, tp_in = sems("e2_got", 4), sems("e2_out", 1), sems("tp_in", 2)
        e3 = named("e3", "chain_p lead m_turned mt a_done a b b_turned bt o_done o summed")
        e3 |= after(e2, "idx stats root norm relu turned ht")
        e3_got, eo_out, ex_out = sems("e3_got", 4), sems("eo_out", 2), sems("ex_out", 4)
        fs = named("fs", "chain grams grams_end products z sums var root rsqrt weights")
        p2 = named("p2", "chain_a chain_b stats root norm relu turned ht y out")
        y_in, y_out = sems("y_in", 4), sems("y_out", 2)
        f = named("f", "chain idx rows")
        f_in, f_out = sems("f_in", 2), sems("f_out", 2)

        for chain, per in (("chain_a", 1), ("chain_b", 1), ("chain_c", 3)):
            e2[chain] = Signal(e1[chain].sem, S * per)
            e3[chain] = Signal(e1[chain].sem, 2 * S * per)
        n_consts = []

        waited = {nc.gpsimd.engine: sem("waited_pool"), nc.tensor.engine: sem("waited_pe"),
                  nc.vector.engine: sem("waited_dve")}

        def settle(eng):
            eng.sem_inc(waited[eng.engine], 1)

        block = ctx.enter_context(nc.Block())

        @block.gpsimd
        def _(pool):
            g = nc.gpsimd
            n = [0]

            def const(instruction, wait=False):
                n[0] += 1
                instruction.then_inc(pre["consts"].sem, 1)
                if wait:
                    pool.wait_ge(pre["consts"].sem, n[0])

            const(g.memset(ident[:], 0.0), wait=True)
            const(g.affine_select(out=ident[:], in_=ident[:], compare_op=ALU.not_equal, fill=1.0, base=0,
                                  pattern=[[-1, P]], channel_multiplier=1))
            const(g.memset(later[:, 0, :], 1.0))
            const(g.memset(later[:, 1, 0:P], 0.0))
            const(g.memset(later[:, 1, P:2 * P], 1.0), wait=True)
            for a in range(2):
                v = later[:, a, a * P:(a + 1) * P]
                const(g.affine_select(out=v, in_=v, compare_op=ALU.is_gt, fill=0.0, base=0, pattern=[[1, P]],
                                      channel_multiplier=-1))
            const(g.memset(valid[:], 1.0))
            const(g.memset(node_ok[:], 1.0), wait=True)
            const(g.affine_select(out=valid[:], in_=valid[:], compare_op=ALU.is_gt, fill=0.0, base=E,
                                  pattern=[[-1, T]], channel_multiplier=-T))
            v = node_ok[:].rearrange("p (g j) -> p g j", j=J)
            const(g.affine_select(out=v, in_=v, compare_op=ALU.is_gt, fill=0.0, base=N, pattern=[[-NG, G], [-1, J]],
                                  channel_multiplier=-J))
            const(g.memset(ones[:], 1.0))
            const(g.memset(ones_bf[:], 1.0))
            const(g.memset(eps_col[:], EPS))
            const(g.memset(zeros[:], 0.0))
            for t in (claim, addb, up_w, lin_w, sc_w, wb_w):
                const(g.memset(t[:], 0.0))
            const(g.memset(h2b[:, :, :, 0:1], 1.0))
            const(g.memset(h2[:, :, :, 0:1], 1.0))
            const(g.iota(iota_h[:], pattern=[[1, G * J]], base=0, channel_multiplier=0,
                         allow_small_or_imprecise_dtypes=True))
            const(g.iota(trash_i[:], pattern=[[P, 2]], base=TRASH, channel_multiplier=1))
            const(g.iota(pair_i[:], pattern=[[1, S], [0, 2]], base=0, channel_multiplier=0))
            n_consts.append(n[0])

            def rbf_step(s):
                if s.live():
                    if s.k == 0:
                        pool.wait_ge(pre["edges"].sem, EDGES_LOADED)
                    done(pool, cnt["turned0"], s, 2)
                    settle(pool)
                    g.tensor_copy(rbf[:, s.slot(0, 2), :],
                                  ea16_sb[:, bass.ds(s.at() * (2 * R), 2 * R)]).then_inc(cnt["rbf"].sem, 1)

            run(pool, S, 0, rbf_step)

            def claim_step(s):
                if s.live():
                    a = s.slot(0, 2)
                    if s.k == 0:
                        pool.wait_ge(pre["prepared"].sem, 1)
                        pool.wait_ge(pre["cleared"].sem, CLEARED)
                        pool.wait_ge(pre["dinv_out"].sem, 16)
                    landed(pool, claim_out, s, 2)
                    landed(pool, dinv_in, s, 2, dmas=2)
                    settle(pool)
                    g.tensor_copy(idx[:, a, :], idx3[:, :, s.at()]).then_inc(p1["idx"].sem, 1)
                    g.tensor_copy(claim[:, a, D:ROW], pair_no[:, bass.ds(s.at(), 1)]).then_inc(p1["idx"].sem, 1)
                    done(pool, p1["idx"], s, 0, per=2)
                    done(pool, p1["dinv_got"], s, 2)
                    landed(pool, claim_out, s, 1)
                    settle(pool)
                    pool.indirect_dma_start(msg_tab, rows_of(idx[:, a, 0:1]), claim[:, a, :],
                                            None).then_inc(claim_out[0], 16)
                    for i in range(2):
                        pool.indirect_dma_start(got[:, a, i:i + 1], None, dinv_tab,
                                                rows_of(idx[:, a, i + 1:i + 2])).then_inc(dinv_in[a], 16)
                if s.live(1):
                    landed(pool, dinv_in, s, 1, dmas=2)
                    settle(pool)
                    g.tensor_copy(dinv_edge[:, bass.ds(s.at(1), 1), :],
                                  got[:, s.slot(1, 2), :].unsqueeze(1)).then_inc(p1["dinv_got"].sem, 1)

            run(pool, T, 1, claim_step)

            def gather(sm, got_sems, s, which, sources, free):
                a = s.slot(0, 2)
                landed(pool, got_sems, s, 2, dmas=2 * len(sources))
                settle(pool)
                g.tensor_copy(idx_e[:, a, :], idx3[:, which, bass.ds(s.at() * 2, 2)]).then_inc(sm["idx"].sem, 1)
                free(s)
                settle(pool)
                done(pool, sm["idx"], s, 0)
                settle(pool)
                for i in range(2):
                    for to, table in sources:
                        pool.indirect_dma_start(to[:, s.slot(0, 4), i, 0:table.shape[1]], None, table,
                                                rows_of(idx_e[:, a, i:i + 1])).then_inc(got_sems[s.slot(0, 4)], 16)

            def scatter_add(sm, out_sems, s, d, table):
                if s.live(d):
                    done(pool, sm["add"], s, d)
                    done(pool, sm["sidx"], s, d)
                    landed(pool, out_sems, s, d + 1, dmas=2)
                    settle(pool)
                    for i in range(2):
                        pool.indirect_dma_start(table, rows_of(sidx[:, s.slot(d, 4), i:i + 1]),
                                                addb[:, s.slot(d, 4), i, :], None,
                                                compute_op=ALU.add).then_inc(out_sems[0], 16)

            def e1_step(s):
                if s.live():
                    gather(e1, e1_got, s, 1, [(xg, x)], lambda s: done(pool, e1["relu"], s, 4))
                if s.k == 4:
                    all_landed(pool, x1_out, G)
                scatter_add(e1, e1_out, s, 4, x1_tab)

            run(pool, S, 4, e1_step)
            all_landed(pool, e1_out, S, dmas=2)

            def e2_step(s):
                if s.live():
                    gather(e2, e2_got, s, 2, [(xg, x1_tab)], lambda s: done(pool, e2["weighted"], s, 4))
                scatter_add(e2, e2_out, s, 5, msg_tab)

            all_landed(pool, claim_out, T)
            run(pool, S, 5, e2_step)
            all_landed(pool, e2_out, S, dmas=2)

            def e3_free(s):
                done(pool, e3["relu"], s, 4)
                landed(pool, ex_out, s, 4)
                done(pool, e3["lead"], s, 4)
                done(pool, e3["m_turned"], s, 4)
                settle(pool)

            def e3_step(s):
                if s.live():
                    gather(e3, e3_got, s, 1, [(xg, x1_tab), (msg_in, msg_tab)], e3_free)

            run(pool, S, 0, e3_step)

            def f_step(s):
                if s.live():
                    a = s.slot(0, 2)
                    landed(pool, f_out, s, 2, dmas=2)
                    settle(pool)
                    g.tensor_copy(idx_e[:, a, :], pair(final_idx, s)).then_inc(f["idx"].sem, 1)
                    done(pool, f["idx"], s, 0)
                    done(pool, f["rows"], s, 0)
                    settle(pool)
                    if s.k == 0:
                        all_landed(pool, y_out, G)
                    for i in range(2):
                        pool.indirect_dma_start(out, rows_of(idx_e[:, a, i:i + 1]), hg[:, a, i, :], None,
                                                bounds_check=N - 1, oob_is_err=False).then_inc(f_out[a], 16)

            pool.wait_ge(e3["lead"].sem, S)
            run(pool, S, 0, f_step)
            all_landed(pool, f_out, S, dmas=2)

        @block.sync
        def _(sp):
            for to, what in edge_loads:
                sp.dma_start(to, what).then_inc(pre["edges"].sem, 16)

            sp.wait_ge(pre["consts"].sem, n_consts[0])
            m = msg_tab.rearrange("(p r) d -> p (r d)", p=P)
            sp.dma_start(m[:, S * ZERO_ROWS * ROW:], zeros[:, 0:(MSG_ROWS - S * ZERO_ROWS) * ROW]
                         ).then_inc(pre["cleared"].sem, 16)
            sp.dma_start(x1_tab[N:N + 2 * P, :].rearrange("(p a) d -> p (a d)", p=P),
                         zeros[:, 0:2 * ROW]).then_inc(pre["cleared"].sem, 16)

            def tpw_step(s):
                if s.live(4):
                    done(sp, cnt["weights"], s, 4)
                    sp.dma_start(tpw_tab[s.at(4)], tpb[:, s.slot(4, 2)].rearrange("p a k c -> p (a k c)")
                                 ).then_inc(tpw_out[s.slot(4, 2)], 16)
                if s.live():
                    sp.dma_start(m[:, bass.ds(s.at() * (ZERO_ROWS * ROW), ZERO_ROWS * ROW)], zeros[:]
                                 ).then_inc(pre["cleared"].sem, 16)

            run(sp, S, 4, tpw_step)
            sp.wait_ge(pre["dinv"].sem, 1)
            sp.dma_start(dinv_tab.rearrange("(g p j) a -> p g (j a)", p=P, j=J),
                         dinv[:].rearrange("p (g j) -> p g j", j=J)).then_inc(pre["dinv_out"].sem, 16)

            def p1_step(s):
                done(sp, p1["x1"], s, 4, per=2)
                if s.live():
                    rows, n = group(x_groups, s)
                    sp.dma_start(big[0:n, s.slot(0, 4), 0:J * D], rows).then_inc(x_in[s.slot(0, 4)], 16)
                if s.live(4):
                    rows, n = group(x1_groups, s, 4)
                    sp.dma_start(rows, x1b[0:n, s.slot(4, 2), :]).then_inc(x1_out[s.slot(4, 2)], 16)

            run(sp, G, 4, p1_step)

            all_landed(sp, tpw_out, S)
            def tp_step(s):
                if s.live():
                    done(sp, e2["message"], s, 2)
                    sp.dma_start(tpb[:, s.slot(0, 2)].rearrange("p a k c -> p (a k c)"),
                                 tpw_tab[s.at()]).then_inc(tp_in[s.slot(0, 2)], 16)

            run(sp, S, 0, tp_step)

            def e3_step(s):
                if s.live():
                    landed(sp, e3_got, s, 0, dmas=4)
                    sp.dma_start(edge_x[s.at()], xg[:, s.slot(0, 4)].rearrange("p a d -> p (a d)")
                                 ).then_inc(ex_out[s.slot(0, 4)], 16)
                if s.live(4):
                    done(sp, e3["o"], s, 4)
                    sp.dma_start(edge_o[s.at(4)].rearrange("p (a d) -> p a d", a=2),
                                 osb[:, s.slot(4, 2), :, D:2 * D]).then_inc(eo_out[s.slot(4, 2)], 16)

            run(sp, S, 4, e3_step)

            def p2_step(s):
                if s.k == 0:
                    all_landed(sp, ex_out, S)
                done(sp, p2["out"], s, 4, per=2)
                if s.live():
                    rows, n = group(x1_groups, s)
                    sp.dma_start(big[0:n, s.slot(0, 4), :], rows).then_inc(y_in[s.slot(0, 4)], 16)
                if s.live(3):
                    done(sp, p2["out"], s, 3, per=2)
                    rows, n = group(out_groups, s, 3)
                    sp.dma_start(rows, x1b[0:n, s.slot(3, 2), 0:J * D]).then_inc(y_out[s.slot(3, 2)], 16)

            run(sp, G, 3, p2_step)

            all_landed(sp, eo_out, S)
            def f_step(s):
                if s.live():
                    a = s.slot(0, 2)
                    done(sp, f["rows"], s, 2)
                    sp.dma_start(vb[:, a].rearrange("p a d -> p (a d)"), edge_o[s.at()]).then_inc(f_in[a], 16)
                    sp.dma_start(xg[:, a].rearrange("p a d -> p (a d)"), edge_x[s.at()]).then_inc(f_in[a], 16)

            run(sp, S, 0, f_step)
            all_landed(sp, y_out, G)

        @block.tensor
        def _(pe):
            mm = nc.tensor.matmul

            layers = ((cnt["turned0"], bank[2]), (cnt["layer1"], bank[3]), (cnt["layer2"], bank[6]),
                      (cnt["layer3"], bank[7]))

            def count_step(s):
                if s.k == 0:
                    pe.wait_ge(pre["consts"].sem, n_consts[0])
                    pe.wait_ge(pre["inputs"].sem, LOADED)
                if s.live():
                    a = s.slot(0, 2)
                    done(pe, cnt["onehot"], s, 0)
                    for i in range(2):
                        for which in range(2):
                            o = onehot[:, a, i, which, :]
                            last = mm(bank[which][:, 0:G * J], o[:, 0:P], o[:, P:P + G * J],
                                      start=(s.k == 0 and i == 0), stop=(s.k == S - 1 and i == 1))
                    last.then_inc(cnt["counted"].sem, 1)
                    done(pe, cnt["rbf"], s, 0)
                    done(pe, cnt["act0"], s, 1)
                    for i in range(2):
                        last = nc.tensor.transpose(bank[2][0:R, i * P:(i + 1) * P], rbf[:, a, i * R:(i + 1) * R],
                                                   ident[:])
                    last.then_inc(cnt["turned0"].sem, 1)
                for i in range(3):
                    if s.live(i + 1):
                        done(pe, cnt[f"act{i}"], s, i + 1)
                        done(pe, cnt[f"act{i + 1}"], s, i + 2)
                        k = R if i == 0 else C
                        settle(pe)
                        mm(layers[i + 1][1][0:C, 0:2 * P], m_sb[i][:], mlp_t[0:k, i, :], start=True,
                           stop=True).then_inc(cnt[f"layer{i + 1}"].sem, 1)
                if s.live(4):
                    done(pe, cnt["act3"], s, 4)
                    done(pe, cnt["weights"], s, 5)
                    for i in range(2):
                        last = mm(bank[4][:, i * D:(i + 1) * D], mlp_t[:, 3, i * P:(i + 1) * P], m4_sb[:],
                                  start=True, stop=True)
                    last.then_inc(cnt["layer4"].sem, 1)

            run(pe, S, 4, count_step)

            pe.wait_ge(pre["b3"].sem, 1)
            done(pe, cnt["weights"], Step(0, S - 1, S - 1, S))
            mm(bank[4][0:C, 0:2 * P], zeros[:, 0:C], zeros[:, 0:2 * P], start=True, stop=False)

            def turn_group(sm, s):
                done(pe, sm["relu1" if sm is p1 else "relu"], s, 2)
                for q in range(2):
                    if s.live(3):
                        pe.wait_ge(sm["ht"].sem, s.at(3) * 2 + q + 1)
                    for j in range(2):
                        for k in range(2):
                            last = nc.tensor.transpose(bank[q][:, (2 * j + k) * P:(2 * j + k + 1) * P],
                                                       hb[:, s.slot(2, 2), 2 * q + j, k * P:(k + 1) * P], ident[:])
                    last.then_inc(sm["turned"].sem, 1)

            def p1_step(s):
                if s.live(2):
                    turn_group(p1, s)
                if s.live(4):
                    done(pe, p1["relu2"], s, 4)
                    settle(pe)
                    for j in range(J):
                        h = h2b[:, s.slot(4, 2), j, :]
                        mm(gram0[0:C, 0:C + 1], h[:, 1:C + 1], h[:, 0:C + 1], start=False, stop=False)
                        for c in range(3):
                            v = by_component(h[:, C + 1:ROW])[:, c, :]
                            last = mm(gram1[0:C, 0:C], v, v, start=False, stop=False)
                    last.then_inc(p1["gram"].sem, 1)
                if s.live(2):
                    for q in range(2):
                        if s.live(3):
                            pe.wait_ge(p1["x1"].sem, s.at(3) * 2 + q + 1)
                        pe.wait_ge(p1["ht"].sem, s.at(2) * 2 + q + 1)
                        for j in range(2):
                            y = bank[2 + q][:, j * D:(j + 1) * D]
                            for k in range(2):
                                mm(y, ht[:, q, (2 * j + k) * P:(2 * j + k + 1) * P], w_sb[:, k, :], start=(k == 0),
                                   stop=False)
                            last = mm(y, ones_bf[:], b3[:], start=False, stop=True)
                        last.then_inc(p1["xw"].sem, 1)

            run(pe, G, 4, p1_step)

            def spread_own(sm, s):
                done(pe, sm["own"], s, 0)
                done(pe, sm["eq"], s, 2)
                for i in range(2):
                    last = mm(spread[s.slot(0, 2)][:, i * P:(i + 1) * P], own[:, s.slot(0, 2), i:i + 1].to_broadcast([P, P]), ident[:],
                              start=True, stop=True)
                last.then_inc(sm["others"].sem, 1)

            def turn(h, to, ready):
                for i in range(2):
                    for k in range(2):
                        last = nc.tensor.transpose(to[:, (2 * i + k) * P:(2 * i + k + 1) * P],
                                                   h[:, i, k * P:(k + 1) * P], ident[:])
                last.then_inc(ready.sem, 1)

            def merge(sm, s, d, rows, to):
                for i in range(2):
                    for k in range(2):
                        last = mm(to[:, i * D:(i + 1) * D], eq[:, s.slot(d, 4), k, i * P:(i + 1) * P],
                                  rows[:, k, 0:D], start=(k == 0), stop=(k == 1))
                last.then_inc(sm["merged"].sem, 1)

            def e1_step(s):
                if s.live(2):
                    done(pe, e1["relu"], s, 2)
                    done(pe, e1["ht"], s, 3)
                    turn(hg[:, s.slot(2, 2)], bank[0], e1["turned"])
                if s.live():
                    spread_own(e1, s)
                if s.live(3):
                    done(pe, e1["v"], s, 3)
                    done(pe, e1["eq"], s, 3)
                    done(pe, e1["add"], s, 4)
                    merge(e1, s, 3, vb[:, s.slot(3, 2)], bank[3])
                if s.live(2):
                    done(pe, e1["ht"], s, 2)
                    done(pe, e1["v"], s, 3)
                    for i in range(2):
                        y = bank[2][:, i * D:(i + 1) * D]
                        for k in range(2):
                            mm(y, ht[:, 0, (2 * i + k) * P:(2 * i + k + 1) * P], w_sb[:, k, :], start=(k == 0),
                               stop=False)
                        last = mm(y, ones_bf[:], b3[:], start=False, stop=True)
                    last.then_inc(e1["xw"].sem, 1)

            run(pe, S, 3, e1_step)

            def e2_step(s):
                if s.live(2):
                    done(pe, e2["relu"], s, 2)
                    done(pe, e2["ht"], s, 3)
                    turn(h2[:, s.slot(2, 2), :, 1:ROW], bank[0], e2["turned"])
                if s.live():
                    spread_own(e2, s)
                if s.live(4):
                    done(pe, e2["message"], s, 4)
                    done(pe, e2["eq"], s, 4)
                    done(pe, e2["add"], s, 5)
                    merge(e2, s, 4, msg_in[:, s.slot(4, 4)], bank[7])
                if s.live(2):
                    done(pe, e2["ht"], s, 2)
                    done(pe, e2["message"], s, 4)
                    for i in range(2):
                        for k in range(2):
                            last = mm(bank[2 + s.slot(2, 2)][:, i * D + k * P:i * D + (k + 1) * P],
                                      ht[:, 0, (2 * i + k) * P:(2 * i + k + 1) * P], up_w[:, k, :], start=True,
                                      stop=True)
                    last.then_inc(e2["up"].sem, 1)
                    done(pe, e2["weighted"], s, 2)
                    settle(pe)
                    for i in range(2):
                        h, w = h2[:, s.slot(2, 2), i, :], hw[:, s.slot(2, 2), i, :]
                        mm(gram0[0:C, 0:C + 1], w[:, 0:C], h[:, 0:C + 1], start=False, stop=False)
                        for c in range(1, 4):
                            last = mm(gram1[0:C, 0:C], w[:, c * C:(c + 1) * C], h[:, 1 + c * C:1 + (c + 1) * C],
                                      start=False, stop=False)
                    last.then_inc(e2["gram"].sem, 1)

            run(pe, S, 4, e2_step)

            def e3_step(s):
                if s.live(2):
                    landed(pe, e3_got, s, 2, dmas=4)
                    done(pe, e3["mt"], s, 3)
                    turn(msg_in[:, s.slot(2, 4)], bank[1], e3["m_turned"])
                if s.live(4):
                    done(pe, e3["b"], s, 4)
                    done(pe, e3["bt"], s, 5)
                    turn(bsb[:, s.slot(4, 2)].rearrange("p a k c -> p a (k c)"), bank[3], e3["b_turned"])
                if s.live(2):
                    done(pe, e3["relu"], s, 2)
                    done(pe, e3["ht"], s, 3)
                    turn(h2[:, s.slot(2, 2), :, 1:ROW], bank[0], e3["turned"])
                if s.live(6):
                    done(pe, e3["o"], s, 6)
                    for i in range(2):
                        last = mm(bank[7][0:1, 0:5 * C], ones[:, 0:1], osb[:, s.slot(6, 2), i, 0:5 * C],
                                  start=(s.k == 6 and i == 0), stop=(s.k == S + 5 and i == 1))
                    last.then_inc(e3["summed"].sem, 1)
                if s.live(2):
                    done(pe, e3["mt"], s, 2)
                    done(pe, e3["a"], s, 3)
                    for i in range(2):
                        for k in range(2):
                            last = mm(bank[2][:, i * D + k * P:i * D + (k + 1) * P],
                                      mt[:, (2 * i + k) * P:(2 * i + k + 1) * P], lin_w[:, k, :], start=True, stop=True)
                    last.then_inc(e3["a_done"].sem, 1)
                if s.live(4):
                    done(pe, e3["bt"], s, 4)
                    done(pe, e3["ht"], s, 4)
                    done(pe, e3["o"], s, 6)
                    for i in range(2):
                        for k in range(2):
                            y = o_bank[s.slot(4, 2)][:, i * D + k * P:i * D + (k + 1) * P]
                            at = slice((2 * i + k) * P, (2 * i + k + 1) * P)
                            mm(y, bt[:, at], wb_w[:, k, :], start=True, stop=False)
                            last = mm(y, ht[:, s.slot(4, 4), at], sc_w[:, k, :], start=False, stop=True)
                    last.then_inc(e3["o_done"].sem, 1)

            run(pe, S, 6, e3_step)

            mm(bank[4][0:C, 0:2 * P], zeros[:, 0:C], zeros[:, 0:2 * P], start=False, stop=True
               ).then_inc(fs["grams_end"].sem, 1)
            pe.wait_ge(fs["grams"].sem, 1)
            for i in range(2):
                mm(bank[i][0:C, 0:C], g_sb[:, i, 1 - i:1 - i + C], sc64[:, i, :], start=True,
                   stop=True).then_inc(fs["products"].sem, 1)
            pe.wait_ge(fs["z"].sem, 1)
            mm(bank[2][:, 0:3 * C], ones[0:C, :], z_sb[:].rearrange("p a c -> p (a c)"), start=True, stop=True)
            mm(bank[3][:, 0:5 * C], ones[0:1, :], row_sb[:], start=True, stop=True).then_inc(fs["sums"].sem, 1)

            pe.wait_ge(fs["weights"].sem, 1)

            def p2_step(s):
                if s.live(2):
                    turn_group(p2, s)
                    for q in range(2):
                        if s.live(3):
                            pe.wait_ge(p2["out"].sem, s.at(3) * 2 + q + 1)
                        pe.wait_ge(p2["ht"].sem, s.at(2) * 2 + q + 1)
                        for j in range(2):
                            for k in range(2):
                                y = bank[2 + q][:, j * D + k * P:j * D + (k + 1) * P]
                                last = mm(y, ht[:, q, (2 * j + k) * P:(2 * j + k + 1) * P], fin_w[:, k, :], start=True,
                                          stop=(k == 1))
                                if k == 0:
                                    mm(y[:, 0:C], ones_bf[:], bias3[:], start=False, stop=True)
                        last.then_inc(p2["y"].sem, 1)

            run(pe, G, 2, p2_step)

        @block.scalar
        def _(act):
            s_act = nc.scalar.activation

            act.wait_ge(pre["consts"].sem, n_consts[0])
            for to, what in loads:
                act.dma_start(to, what).then_inc(pre["inputs"].sem, 16)

            def count_step(s):
                if s.live():
                    done(act, cnt["turned0"], s, 0)
                    done(act, cnt["layer1"], s, 1)
                    nc.scalar.copy(mlp_t[0:R, 0, :], bank[2][0:R, 0:2 * P]).then_inc(cnt["act0"].sem, 1)
                for i, from_ in ((1, bank[3]), (2, bank[6]), (3, bank[7])):
                    if s.live(i):
                        done(act, cnt[f"layer{i}"], s, i)
                        done(act, cnt[f"layer{i + 1}"], s, i + 1)
                        s_act(mlp_t[:, i, :], from_[0:C, 0:2 * P], ACT.Silu).then_inc(cnt[f"act{i}"].sem, 1)
                if s.live(4):
                    done(act, cnt["layer4"], s, 4)
                    landed(act, tpw_out, s, 6)
                    nc.scalar.copy(tpb[:, s.slot(4, 2)].rearrange("p a k c -> p (a k c)"), bank[4][:]
                                   ).then_inc(cnt["weights"].sem, 1)

            run(act, S, 4, count_step)
            act.wait_ge(pre["deg"].sem, 1)
            s_act(deg[:], deg[:], ACT.Sqrt).then_inc(pre["root"].sem, 1)

            def root(sm, which, k, a, n, s, d=0):
                done(act, sm[f"stats{which}"], s, d)
                s_act(sd[:, k, a, 0:n], mv[:, k, a, 0:n, 1], ACT.Sqrt, bias=eps_col[:]).then_inc(sm[f"root{which}"].sem, 1)

            def p1_step(s):
                if s.live(2):
                    for q in range(2):
                        act.wait_ge(p1["turned"].sem, s.at(2) * 2 + q + 1)
                        if s.live(3):
                            act.wait_ge(p1["xw"].sem, s.at(3) * 2 + q + 1)
                        nc.scalar.copy(ht[:, q, :], bank[q][:]).then_inc(p1["ht"].sem, 1)
                if s.live(1):
                    a = s.slot(1, 2)
                    done(act, p1["norm1"], s, 1)
                    done(act, p1["turned"], s, 3, per=2)
                    for j in range(J):
                        last = s_act(hb[:, a, j, :], xj(big, s.slot(1, 4), D)[:, j, :], ACT.Relu,
                                     bias=rs[:, 0, a, 1, j:j + 1], scale=rs[:, 0, a, 0, j:j + 1])
                    last.then_inc(p1["relu1"].sem, 1)
                if s.live(3):
                    a = s.slot(3, 2)
                    root(p1, "2", 1, a, J, s, 3)
                    done(act, p1["norm2"], s, 3)
                    done(act, p1["gram"], s, 5)
                    for j in range(J):
                        last = s_act(h2b[:, a, j, 1:ROW], xj(x1b, a, ROW)[:, j, 0:D], ACT.Relu,
                                     bias=rs[:, 1, a, 2, j:j + 1], scale=rs[:, 1, a, 1, j:j + 1])
                    last.then_inc(p1["relu2"].sem, 1)
                if s.live():
                    root(p1, "1", 0, s.slot(0, 2), J, s)

            run(act, G, 3, p1_step)

            def relu_by_component(h, rows, r, j):
                s_act(h[:, 0:C], rows[:, 0:C], ACT.Relu, bias=r[:, 1, j:j + 1], scale=r[:, 0, j:j + 1])
                return s_act(by_component_out(h[:, C:D]), by_component(rows[:, C:D]), ACT.Relu,
                             bias=r[:, 1, j:j + 1], scale=r[:, 0, j:j + 1])

            def by_component_out(h):
                return h.rearrange("p (x c) -> p x c", x=3)

            def merged_rows(sm, out_sems, s, d, merged):
                done(act, sm["merged"], s, d)
                landed(act, out_sems, s, d + 4, dmas=2)
                nc.scalar.copy(addb[:, s.slot(d, 4), :, 0:D], merged[:].rearrange("p (a d) -> p a d", a=2)
                               ).then_inc(sm["add"].sem, 1)

            def e1_step(s):
                if s.live(3):
                    a = s.slot(3, 2)
                    done(act, e1["xw"], s, 3)
                    done(act, e1["coef"], s, 3)
                    done(act, e1["merged"], s, 5)
                    for i in range(2):
                        last = s_act(vb[:, a, i, :], bank[2][:, i * D:(i + 1) * D], ACT.Identity,
                                     scale=coef[:, s.slot(3, 4), i:i + 1])
                    last.then_inc(e1["v"].sem, 1)
                if s.live(2):
                    done(act, e1["turned"], s, 2)
                    done(act, e1["xw"], s, 3)
                    nc.scalar.copy(ht[:, 0, :], bank[0][:]).then_inc(e1["ht"].sem, 1)
                if s.live(1):
                    a = s.slot(1, 2)
                    done(act, e1["norm"], s, 1)
                    done(act, e1["turned"], s, 3)
                    for i in range(2):
                        last = s_act(hg[:, a, i, :], xg[:, s.slot(1, 4), i, 0:D], ACT.Relu,
                                     bias=rs[:, 0, a, 1, i:i + 1], scale=rs[:, 0, a, 0, i:i + 1])
                    last.then_inc(e1["relu"].sem, 1)
                if s.live():
                    root(e1, "", 0, s.slot(0, 2), 2, s)
                if s.live(3):
                    merged_rows(e1, e1_out, s, 3, bank[3])

            run(act, S, 3, e1_step)

            def e2_step(s):
                if s.live(2):
                    done(act, e2["turned"], s, 2)
                    done(act, e2["up"], s, 3)
                    nc.scalar.copy(ht[:, 0, :], bank[0][:]).then_inc(e2["ht"].sem, 1)
                if s.live(1):
                    a = s.slot(1, 2)
                    done(act, e2["norm"], s, 1)
                    done(act, e2["gram"], s, 3)
                    for i in range(2):
                        last = relu_by_component(h2[:, a, i, 1:ROW], xg[:, s.slot(1, 4), i, :], rs[:, 0, a], i)
                    last.then_inc(e2["relu"].sem, 1)
                if s.live():
                    root(e2, "", 0, s.slot(0, 2), 2, s)
                if s.live(1):
                    done(act, e2["relu"], s, 1)
                    for i in range(2):
                        last = s_act(hw[:, a, i, :], h2[:, a, i, 1:ROW], ACT.Identity,
                                     scale=xg[:, s.slot(1, 4), i, D:ROW])
                    last.then_inc(e2["weighted"].sem, 1)
                if s.live(4):
                    merged_rows(e2, e2_out, s, 4, bank[7])

            run(act, S, 4, e2_step)

            def e3_step(s):
                if s.live(5):
                    a = s.slot(5, 2)
                    done(act, e3["o_done"], s, 5)
                    done(act, e3["summed"], s, 7)
                    landed(act, eo_out, s, 7)
                    for i in range(2):
                        o = o_bank[a][:, i * D:(i + 1) * D]
                        leads = lead[:, bass.ds(s.at(5) * 2 + i, 1)]
                        s_act(osb[:, a, i, 0:D], o, ACT.Square, scale=leads)
                        last = s_act(osb[:, a, i, D:2 * D], o, ACT.Identity, scale=leads)
                    last.then_inc(e3["o"].sem, 1)
                if s.live(3):
                    a = s.slot(3, 2)
                    done(act, e3["a_done"], s, 3)
                    done(act, e3["b"], s, 5)
                    nc.scalar.copy(asb[:, a].rearrange("p a k c -> p (a k c)"), bank[2][:])
                    s_act(asq[:, a].rearrange("p a k c -> p (a k c)"), bank[2][:], ACT.Square).then_inc(e3["a"].sem, 1)
                if s.live(2):
                    done(act, e3["m_turned"], s, 2)
                    done(act, e3["a_done"], s, 3)
                    nc.scalar.copy(mt, bank[1][:]).then_inc(e3["mt"].sem, 1)
                if s.live(4):
                    done(act, e3["b_turned"], s, 4)
                    done(act, e3["o_done"], s, 5)
                    nc.scalar.copy(bt, bank[3][:]).then_inc(e3["bt"].sem, 1)
                if s.live(2):
                    done(act, e3["turned"], s, 2)
                    done(act, e3["o_done"], s, 6)
                    nc.scalar.copy(ht[:, s.slot(2, 4), :], bank[0][:]).then_inc(e3["ht"].sem, 1)
                if s.live(1):
                    a = s.slot(1, 2)
                    done(act, e3["norm"], s, 1)
                    done(act, e3["turned"], s, 3)
                    for i in range(2):
                        last = relu_by_component(h2[:, a, i, 1:ROW], xg[:, s.slot(1, 4), i, :], rs[:, 0, a], i)
                    last.then_inc(e3["relu"].sem, 1)
                if s.live():
                    root(e3, "", 0, s.slot(0, 2), 2, s)

            run(act, S, 5, e3_step)

            for i in range(2):
                act.wait_ge(fs["var"].sem, i + 1)
                s_act(fin[:, 6 + i, :], fin[:, 4 + i, :], ACT.Sqrt, bias=eps_col[:]).then_inc(fs["root"].sem, 1)

            def p2_step(s):
                if s.live(2):
                    for q in range(2):
                        act.wait_ge(p2["turned"].sem, s.at(2) * 2 + q + 1)
                        if s.live(3):
                            act.wait_ge(p2["y"].sem, s.at(3) * 2 + q + 1)
                        nc.scalar.copy(ht[:, q, :], bank[q][:]).then_inc(p2["ht"].sem, 1)
                if s.live(1):
                    a = s.slot(1, 2)
                    done(act, p2["norm"], s, 1)
                    done(act, p2["turned"], s, 3, per=2)
                    for j in range(J):
                        last = relu_by_component(hb[:, a, j, :], xj(big, s.slot(1, 4), ROW)[:, j, :], rs[:, 0, a], j)
                    last.then_inc(p2["relu"].sem, 1)
                if s.live():
                    root(p2, "", 0, s.slot(0, 2), J, s)

            run(act, G, 2, p2_step)

        @block.vector
        def _(dve):
            v = nc.vector
            link = Chain(dve, pre["dve_chain"])

            dve.wait_ge(pre["consts"].sem, n_consts[0])
            dve.wait_ge(pre["edges"].sem, EDGES_LOADED)
            v.tensor_copy(trash[:], trash_i[:])
            v.tensor_copy(pair_no[:], pair_i[:])
            v.tensor_scalar(vm1[:], valid[:], -1.0, None, ALU.add)
            v.tensor_copy(dst_f[:], idx3[:, 1, :])
            link(v.tensor_copy(src_f[:], idx3[:, 2, :]))
            v.tensor_tensor(dst_c[:], dst_f[:], valid[:], ALU.mult)
            link(v.tensor_tensor(src_c[:], src_f[:], valid[:], ALU.mult))
            link(v.scalar_tensor_tensor(out=idx3[:, 0, :], in0=vm1[:], scalar=-float(TRASH + P - 1), in1=dst_c[:],
                                        op0=ALU.mult, op1=ALU.add))
            v.tensor_tensor(dst_c[:], dst_c[:], vm1[:], ALU.add)
            v.tensor_tensor(src_c[:], src_c[:], vm1[:], ALU.add)
            for delta, index in ((dst_delta, dst_f), (src_delta, src_f)):
                for i in range(2):
                    v.tensor_scalar(delta[:].rearrange("p (s a) -> p a s", a=2)[:, i],
                                    index[:].rearrange("p (s a) -> p a s", a=2)[:, i], trash[:, i:i + 1], None,
                                    ALU.subtract)
            for col, lo, hi in ((1, lo_d, hi_d), (2, lo_s, hi_s)):
                link(v.tensor_scalar(int_a[:], idx3[:, col, :], 2, P - 1, ALU.logical_shift_right, ALU.bitwise_and))
                link(v.tensor_copy(lo[:], int_a[:]))
                link(v.tensor_tensor(lo[:], lo[:], valid[:], ALU.mult))
                v.tensor_tensor(lo[:], lo[:], vm1[:], ALU.add)
                v.tensor_scalar(int_a[:], idx3[:, col, :], 9, 2, ALU.logical_shift_right, ALU.logical_shift_left)
                link(v.tensor_scalar(int_b[:], idx3[:, col, :], J - 1, None, ALU.bitwise_and))
                link(v.tensor_tensor(int_a[:], int_a[:], int_b[:], ALU.bitwise_or))
                link(v.tensor_copy(hi[:], int_a[:]))
            v.tensor_copy(int_b[:], int_a[:]).then_inc(pre["prepared"].sem, 1)

            def three_parts(chain, f, bf, to):
                chain(v.tensor_copy(bf[:, 0, :], f[:, 0, :]))
                chain(v.tensor_tensor(f[:, 1, :], f[:, 0, :], bf[:, 0, :], ALU.subtract))
                chain(v.tensor_copy(bf[:, 1, :], f[:, 1, :]))
                chain(v.tensor_tensor(f[:, 2, :], f[:, 1, :], bf[:, 1, :], ALU.subtract))
                chain(v.tensor_copy(bf[:, 2, :], f[:, 2, :]))
                chain(v.tensor_scalar(to[:], bf[:, 0, :], ident[0:3, 0:1], None, ALU.mult))
                chain(v.scalar_tensor_tensor(out=to[:], in0=bf[:, 1, :], scalar=ident[0:3, 1:2], in1=to[:],
                                             op0=ALU.mult, op1=ALU.add))
                return v.scalar_tensor_tensor(out=to[:], in0=bf[:, 2, :], scalar=ident[0:3, 2:3], in1=to[:],
                                              op0=ALU.mult, op1=ALU.add)

            def onehot_step(s):
                if s.live():
                    done(dve, cnt["counted"], s, 2)
                    for i in range(2):
                        for which, lo, hi in ((0, lo_d, hi_d), (1, lo_s, hi_s)):
                            o = onehot[:, s.slot(0, 2), i, which, :]
                            v.tensor_scalar(o[:, 0:P], iota_h[:, 0:P], lo[:, bass.ds(s.at() * 2 + i, 1)], None,
                                            ALU.is_equal)
                            last = v.tensor_scalar(o[:, P:P + G * J], iota_h[:], hi[:, bass.ds(s.at() * 2 + i, 1)],
                                                   None, ALU.is_equal)
                    last.then_inc(cnt["onehot"].sem, 1)

            run(dve, S, 0, onehot_step)
            dve.wait_ge(pre["inputs"].sem, LOADED)
            three_parts(link, b_f, b_bf, b3).then_inc(pre["b3"].sem, 1)

            c0 = cw[:, 0:5 * C].rearrange("p (c k) -> p k c", k=5)
            c1 = cw[:, 5 * C:9 * C].rearrange("p (c k) -> p k c", k=4)
            for i, k in enumerate((0, 1, 3, 4)):
                v.tensor_copy(poly[:, i, 0, :], c0[:, k])
                v.tensor_copy(poly[:, i, 1, :], c1[:, i])
            link(v.tensor_copy(poly_vv[:, 0, :], c0[:, 2]))

            dve.wait_ge(cnt["counted"].sem, S)
            ends, starts = bank[0][:, 0:G * J], bank[1][:, 0:G * J]
            v.tensor_scalar(deg[:], ends, 1.0, None, ALU.add).then_inc(pre["deg"].sem, 1)
            v.tensor_scalar(no_dst[:], ends, 0.0, None, ALU.is_equal)
            v.tensor_scalar(w_src[:], starts, 1.0, None, ALU.max)
            link(v.scalar_tensor_tensor(out=alone[:], in0=starts, scalar=0.0, in1=node_ok[:], op0=ALU.is_equal,
                                        op1=ALU.mult))
            v.tensor_tensor(alone[:], alone[:], no_dst[:], ALU.mult)
            link(v.reciprocal(w_src[:], w_src[:]))
            link(v.tensor_tensor(w_src[:], w_src[:], no_dst[:], ALU.mult))
            dve.wait_ge(pre["root"].sem, 1)
            link(v.reciprocal(dinv[:], deg[:]))
            v.tensor_tensor(dinv2[:], dinv[:], dinv[:], ALU.mult).then_inc(pre["dinv"].sem, 1)
            dve.wait_ge(pre["dinv"].sem, 1)

            def stats(sm, chain, signal, k, a, rows, s, d=0):
                one = Chain(dve, sm[chain], 1, s.at(d))
                for j, row in enumerate(rows):
                    last = v.bn_stats(st[:, k, j, :], row)
                one(last)
                settle(dve)
                for j in range(len(rows)):
                    last = v.bn_aggr(mv[:, k, a, j, :], st[:, k, j, :])
                last.then_inc(sm[signal].sem, 1)
                one.end()

            def norm(sm, a, n, s, d=0):
                one = Chain(dve, sm["chain_b"], 1, s.at(d))
                done(dve, sm["root1" if sm is p1 else "root"], s, d)
                one(v.reciprocal(rs[:, 0, a, 0, 0:n], sd[:, 0, a, 0:n]))
                v.scalar_tensor_tensor(out=rs[:, 0, a, 1, 0:n], in0=mv[:, 0, a, 0:n, 0], scalar=-1.0,
                                       in1=rs[:, 0, a, 0, 0:n], op0=ALU.mult, op1=ALU.mult
                                       ).then_inc(sm["norm1" if sm is p1 else "norm"].sem, 1)
                one.end()

            def p1_step(s):
                if s.live():
                    landed(dve, x_in, s)
                    stats(p1, "chain_a", "stats1", 0, s.slot(0, 2),
                          [xj(big, s.slot(0, 4), D)[:, j, :] for j in range(J)], s)
                if s.live(3):
                    a = s.slot(3, 2)
                    one = Chain(dve, p1["chain_n"], 2, s.at(3))
                    done(dve, p1["root2"], s, 3)
                    one(v.reciprocal(rs[:, 1, a, 0, :], sd[:, 1, a, :]))
                    one(v.tensor_tensor(rs[:, 1, a, 1, :], rs[:, 1, a, 0, :], alone[:, bass.ds(s.at(3) * J, J)],
                                        ALU.mult))
                    v.scalar_tensor_tensor(out=rs[:, 1, a, 2, :], in0=mv[:, 1, a, :, 0], scalar=-1.0,
                                           in1=rs[:, 1, a, 1, :], op0=ALU.mult, op1=ALU.mult
                                           ).then_inc(p1["norm2"].sem, 1)
                    one.end()
                if s.live(2):
                    x1 = xj(x1b, s.slot(2, 2), ROW)
                    landed(dve, x1_out, s, 4)
                    done(dve, p1["relu2"], s, 4)
                    v.tensor_copy(x1[:, :, D], w_src[:, bass.ds(s.at(2) * J, J)])
                    for q in range(2):
                        dve.wait_ge(p1["xw"].sem, s.at(2) * 2 + q + 1)
                        for i in range(2):
                            j = 2 * q + i
                            last = v.scalar_tensor_tensor(
                                out=x1[:, j, 0:D], in0=bank[2 + q][:, i * D:(i + 1) * D],
                                scalar=dinv2[:, bass.ds(s.at(2) * J + j, 1)], in1=xj(big, s.slot(2, 4), D)[:, j, :],
                                op0=ALU.mult, op1=ALU.add)
                        last.then_inc(p1["x1"].sem, 1)
                if s.live():
                    norm(p1, s.slot(0, 2), J, s)
                if s.live(2):
                    done(dve, p1["x1"], s, 2, per=2)
                    stats(p1, "chain_m", "stats2", 1, s.slot(2, 2), [x1[:, j, 0:D] for j in range(J)], s, 2)

            run(dve, G, 3, p1_step)

            def same_index(sm, s, d):
                done(dve, sm["others"], s, d)
                done(dve, sm["merged"], s, d + 4)
                for i in range(2):
                    last = v.tensor_scalar(eq[:, s.slot(d, 4), i, :], spread[s.slot(d, 2)][:, 0:2 * P],
                                           own[:, s.slot(d, 2), i:i + 1], None, ALU.is_equal)
                last.then_inc(sm["eq"].sem, 1)

            def scatter_to(sm, out_sems, s, d, delta):
                one = Chain(dve, sm["chain_c"], 3, s.at(d))
                done(dve, sm["eq"], s, d)
                for i in range(2):
                    last = v.tensor_tensor_reduce(out=eq_junk[:, i, :], in0=eq[:, s.slot(d, 4), i, :],
                                                  in1=later[:, i, :], scale=1.0, scalar=0.0, op0=ALU.mult,
                                                  op1=ALU.add, accum_out=n_later[:, i:i + 1])
                one(last)
                one(v.scalar_tensor_tensor(out=pair(first_in_pair, s, d), in0=n_later[:], scalar=0.0,
                                           in1=pair(valid, s, d), op0=ALU.is_equal, op1=ALU.mult))
                one(v.tensor_tensor(sidx_f[:], pair(first_in_pair, s, d), pair(delta, s, d), ALU.mult))
                landed(dve, out_sems, s, d + 4, dmas=2)
                v.tensor_tensor(sidx[:, s.slot(d, 4), :], sidx_f[:], trash[:], ALU.add).then_inc(sm["sidx"].sem, 1)
                one.end()

            def take_own(sm, s, index):
                done(dve, sm["others"], s, 2)
                v.tensor_copy(own[:, s.slot(0, 2), :], pair(index, s)).then_inc(sm["own"].sem, 1)
                done(dve, sm["own"], s, 0)

            dve.wait_ge(p1["dinv_got"].sem, T)

            def e1_step(s):
                if s.live():
                    take_own(e1, s, src_c)
                if s.live(1):
                    norm(e1, s.slot(1, 2), 2, s, 1)
                if s.live():
                    landed(dve, e1_got, s, 0, dmas=2)
                    stats(e1, "chain_a", "stats", 0, s.slot(0, 2),
                          [xg[:, s.slot(0, 4), i, 0:D] for i in range(2)], s)
                if s.live(1):
                    same_index(e1, s, 1)
                    done(dve, e1["v"], s, 5)
                    c = pair(dinv_edge, s, 1)
                    v.tensor_tensor(coef[:, s.slot(1, 4), :], c[:, :, 0], c[:, :, 1], ALU.mult
                                    ).then_inc(e1["coef"].sem, 1)
                    scatter_to(e1, e1_out, s, 1, src_delta)

            run(dve, S, 1, e1_step)

            def e2_step(s):
                if s.live():
                    take_own(e2, s, dst_c)
                if s.live(1):
                    norm(e2, s.slot(1, 2), 2, s, 1)
                if s.live():
                    landed(dve, e2_got, s, 0, dmas=2)
                    stats(e2, "chain_a", "stats", 0, s.slot(0, 2),
                          [xg[:, s.slot(0, 4), i, 0:D] for i in range(2)], s)
                if s.live(1):
                    same_index(e2, s, 1)
                    scatter_to(e2, e2_out, s, 1, dst_delta)
                if s.live(3):
                    one = Chain(dve, e2["chain_m"], 4, s.at(3))
                    done(dve, e2["up"], s, 3)
                    landed(dve, tp_in, s, 3)
                    w = tpb[:, s.slot(3, 2)]
                    up = bank[2 + s.slot(3, 2)][:].rearrange("p (a k c) -> p a k c", a=2, k=4)
                    m = msg_in[:, s.slot(3, 4), :, 0:D].rearrange("p a (k c) -> p a k c", k=4)

                    def sh(i, k):
                        return ea4_sb[:, bass.ds((s.at(3) * 2 + i) * 4 + k, 1)]

                    for i in range(2):
                        v.tensor_scalar(dot[:, i, :], up[:, i, 1, :], sh(i, 1), None, ALU.mult)
                        v.tensor_scalar(scaled_w[:, i], w[:, i, 0:4:2, :], sh(i, 0), None, ALU.mult)
                    one(v.tensor_tensor(tmp_a[:], w[:, :, 1, :], up[:, :, 0, :], ALU.mult))
                    for i in range(2):
                        v.scalar_tensor_tensor(out=dot[:, i, :], in0=up[:, i, 2, :], scalar=sh(i, 2),
                                               in1=dot[:, i, :], op0=ALU.mult, op1=ALU.add)
                        v.tensor_tensor(m[:, i, 1:4, :], scaled_w[:, i, 1:2, :].to_broadcast([P, 3, C]),
                                        up[:, i, 1:4, :], ALU.mult)
                    one(v.tensor_tensor(m[:, :, 0, :], scaled_w[:, :, 0, :], up[:, :, 0, :], ALU.mult))
                    for i in range(2):
                        last = v.scalar_tensor_tensor(out=dot[:, i, :], in0=up[:, i, 3, :], scalar=sh(i, 3),
                                                      in1=dot[:, i, :], op0=ALU.mult, op1=ALU.add)
                    one(last)
                    for i in range(2):
                        for k in range(1, 4):
                            v.scalar_tensor_tensor(out=m[:, i, k, :], in0=tmp_a[:, i, :], scalar=sh(i, k),
                                                   in1=m[:, i, k, :], op0=ALU.mult, op1=ALU.add)
                    one(v.tensor_tensor(tmp_b[:], w[:, :, 3, :], dot[:], ALU.mult))
                    v.scalar_tensor_tensor(out=m[:, :, 0, :], in0=tmp_b[:], scalar=INV3, in1=m[:, :, 0, :],
                                           op0=ALU.mult, op1=ALU.add).then_inc(e2["message"].sem, 1)
                    one.end()

            run(dve, S, 3, e2_step)

            def e3_step(s):
                if s.live(1):
                    norm(e3, s.slot(1, 2), 2, s, 1)
                if s.live():
                    landed(dve, e3_got, s, 0, dmas=4)
                    stats(e3, "chain_a", "stats", 0, s.slot(0, 2),
                          [xg[:, s.slot(0, 4), i, 0:D] for i in range(2)], s)
                    one = Chain(dve, e3["chain_c"], 3, s.at())
                    one(v.tensor_tensor(lead_f[:], msg_in[:, s.slot(0, 4), :, D], pair(pair_no, s), ALU.is_equal))
                    one(v.tensor_tensor(pair(lead, s), lead_f[:], pair(first_in_pair, s), ALU.mult))
                    one(v.scalar_tensor_tensor(out=sidx_f[:], in0=pair(dst_f, s), scalar=-float(NOWHERE),
                                               in1=pair(lead, s), op0=ALU.add, op1=ALU.mult))
                    v.tensor_scalar(pair(final_idx, s), sidx_f[:], float(NOWHERE), None, ALU.add
                                    ).then_inc(e3["lead"].sem, 1)
                    one.end()
                if s.live(3):
                    a = s.slot(3, 2)
                    one = Chain(dve, e3["chain_p"], 6, s.at(3))
                    done(dve, e3["a"], s, 3)
                    done(dve, e3["b_turned"], s, 5)
                    A, Q, B = asb[:, a], asq[:, a], bsb[:, a]

                    def coefficients(i):
                        return poly[:, i].unsqueeze(1).to_broadcast([P, 2, 2, C])

                    def both(t):
                        return t.unsqueeze(2).to_broadcast([P, 2, 2, C])

                    one(v.tensor_tensor(vv[:], Q[:, :, 1, :], Q[:, :, 2, :], ALU.add))
                    v.tensor_tensor(term[:, 0], coefficients(1), both(A[:, :, 0, :]), ALU.mult)
                    v.tensor_tensor(term[:, 1], coefficients(2), both(Q[:, :, 0, :]), ALU.mult)
                    one(v.tensor_tensor(vv[:], vv[:], Q[:, :, 3, :], ALU.add))
                    v.tensor_tensor(tmp_a[:], poly_vv[:].to_broadcast([P, 2, C]), vv[:], ALU.mult)
                    v.tensor_tensor(term[:, 0], term[:, 0], coefficients(0), ALU.add)
                    one(v.tensor_tensor(term[:, 2], coefficients(3), both(vv[:]), ALU.mult))
                    one(v.tensor_tensor(term[:, 1], term[:, 1], term[:, 2], ALU.add))
                    one(v.tensor_tensor(term[:, 0], term[:, 0], term[:, 1], ALU.add))
                    for i in range(2):
                        v.tensor_tensor(B[:, i, 1:4, :], term[:, 0, i, 1:2, :].to_broadcast([P, 3, C]),
                                        A[:, i, 1:4, :], ALU.mult)
                    one(v.tensor_tensor(tmp_b[:], term[:, 0, :, 0, :], A[:, :, 0, :], ALU.mult))
                    v.tensor_tensor(B[:, :, 0, :], tmp_a[:], tmp_b[:], ALU.add).then_inc(e3["b"].sem, 1)
                    one.end()

            run(dve, S, 3, e3_step)

            one = Chain(dve, fs["chain"])
            dve.wait_ge(fs["grams_end"].sem, 1)
            dve.wait_ge(e3["summed"].sem, S)
            v.tensor_copy(g_sb[:, 0, :], gram0[0:C, 0:C + 1])
            v.tensor_copy(row_sb[:], bank[7][0:1, 0:5 * C])
            v.tensor_copy(g_sb[:, 1, 0:C], gram1[0:C, 0:C]).then_inc(fs["grams"].sem, 1)
            dve.wait_ge(fs["grams"].sem, 1)
            dve.wait_ge(fs["products"].sem, 2)
            for i in range(2):
                v.tensor_tensor(z_sb[:, i, :], sc64[:, i, :], bank[i][0:C, 0:C], ALU.mult)
            v.tensor_scalar(z_sb[:, 2, :], sc64[:, 0, :], g_sb[:, 0, 0:1], None, ALU.mult).then_inc(fs["z"].sem, 1)
            dve.wait_ge(fs["sums"].sem, 1)
            one(v.tensor_copy(slot_sum[:], bank[3][:, 0:5 * C]))
            whole = bank[2]
            v.tensor_tensor(fin[:, 0, :], whole[:, 2 * C:3 * C], slot_sum[:, 4 * C:5 * C], ALU.add)
            v.tensor_tensor(fin[:, 1, :], whole[:, 0:C], slot_sum[:, 0:C], ALU.add)
            v.tensor_tensor(fin[:, 2, :], whole[:, C:2 * C], slot_sum[:, C:2 * C], ALU.add)
            one(v.tensor_tensor(fin[:, 3, :], slot_sum[:, 2 * C:3 * C], slot_sum[:, 3 * C:4 * C], ALU.add))
            v.tensor_scalar(fin[:, 0, :], fin[:, 0, :], 1.0 / N, None, ALU.mult)
            v.tensor_scalar(fin[:, 1, :], fin[:, 1, :], 1.0 / N, None, ALU.mult)
            one(v.tensor_tensor(fin[:, 2, :], fin[:, 2, :], fin[:, 3, :], ALU.add))
            v.tensor_scalar(fin[:, 5, :], fin[:, 2, :], 1.0 / (3 * N), None, ALU.mult)
            one(v.tensor_tensor(fin[:, 4, :], fin[:, 0, :], fin[:, 0, :], ALU.mult))
            v.tensor_tensor(fin[:, 4, :], fin[:, 1, :], fin[:, 4, :], ALU.subtract).then_inc(fs["var"].sem, 2)
            dve.wait_ge(fs["root"].sem, 2)
            one(v.reciprocal(fin[:, 6:8, :], fin[:, 6:8, :]))
            v.tensor_tensor(scale[:, 0, :], fin[:, 6, :], g_b[:, 0, :], ALU.mult)
            for k in range(1, 4):
                last = v.tensor_tensor(scale[:, k, :], fin[:, 7, :], g_b[:, 2, :], ALU.mult)
            one(last)
            one(v.tensor_tensor(bias[:], fin[:, 0, :], scale[:, 0, :], ALU.mult))
            v.tensor_tensor(fin_w[:].rearrange("p a c -> p (a c)"), sc_w[:].rearrange("p a c -> p (a c)"),
                            scale[:].rearrange("p a c -> p (a c)"), ALU.mult)
            one(v.tensor_tensor(bias[:], g_b[:, 1, :], bias[:], ALU.subtract))
            one(v.tensor_copy(bias_f[:, 0, :], bias[0:3, :]))
            three_parts(one, bias_f, bias_bf, bias3).then_inc(fs["weights"].sem, 1)

            def p2_step(s):
                if s.live(1):
                    norm(p2, s.slot(1, 2), J, s, 1)
                if s.live():
                    landed(dve, y_in, s)
                    stats(p2, "chain_a", "stats", 0, s.slot(0, 2),
                          [xj(big, s.slot(0, 4), ROW)[:, j, 0:D] for j in range(J)], s)
                if s.live(2):
                    landed(dve, y_out, s, 4)
                    o, x1 = xj(x1b, s.slot(2, 2), D), xj(big, s.slot(2, 4), ROW)
                    for q in range(2):
                        dve.wait_ge(p2["y"].sem, s.at(2) * 2 + q + 1)
                        y = bank[2 + q][:].rearrange("p (j d) -> p j d", j=2)
                        v.tensor_tensor(o[:, 2 * q:2 * q + 2, 0:C], y[:, :, 0:C], x1[:, 2 * q:2 * q + 2, 0:C], ALU.add)
                        for i in range(2):
                            j = 2 * q + i
                            last = v.tensor_tensor(o[:, j, C:D].rearrange("p (c x) -> p c x", x=3),
                                                   y[:, i, C:D].rearrange("p (x c) -> p c x", x=3),
                                                   x1[:, j, C:D].rearrange("p (c x) -> p c x", x=3), ALU.add)
                        last.then_inc(p2["out"].sem, 1)

            run(dve, G, 2, p2_step)

            def f_step(s):
                if s.live():
                    a = s.slot(0, 2)
                    one = Chain(dve, f["chain"], 2, s.at())
                    landed(dve, f_in, s, 0, dmas=2)
                    one(v.tensor_tensor(vb[:, a], vb[:, a], scale[:].rearrange("p k c -> p (k c)").unsqueeze(1)
                                        .to_broadcast([P, 2, D]), ALU.mult))
                    landed(dve, f_out, s, 2, dmas=2)
                    for i in range(2):
                        v.tensor_tensor(hg[:, a, i, C:D].rearrange("p (c x) -> p c x", x=3),
                                        vb[:, a, i, C:D].rearrange("p (x c) -> p c x", x=3),
                                        xg[:, a, i, C:D].rearrange("p (c x) -> p c x", x=3), ALU.add)
                    one(v.tensor_tensor(hg[:, a, :, 0:C], vb[:, a, :, 0:C], xg[:, a, :, 0:C], ALU.add))
                    v.tensor_tensor(hg[:, a, :, 0:C], hg[:, a, :, 0:C], bias[:].unsqueeze(1).to_broadcast([P, 2, C]),
                                    ALU.add).then_inc(f["rows"].sem, 1)
                    one.end()

            run(dve, S, 0, f_step)


_INS = ["x", "src", "dst", "edge_attr_16", "edge_attr_4", "L0_gnn_W", "L0_gnn_b", "L1_gnn_W_up0", "L1_gnn_W_up1",
        "L1_gnn_M1", "L1_gnn_M2", "L1_gnn_M3", "L1_gnn_M4", "L1_gnn_W_lin0", "L1_gnn_W_lin1", "L1_gnn_Wsc0",
        "L1_gnn_Wsc1", "L1_gnn_Wc0", "L1_gnn_Wc1", "L1_gnn_WB0", "L1_gnn_WB1", "L1_gnn_gamma0", "L1_gnn_beta0",
        "L1_gnn_gamma1"]


def kernel(**inputs):
    import numpy as _np
    import concourse.bacc as _bacc
    from concourse import mybir as _mybir
    from concourse.bass_utils import run_bass_kernel_spmd as _run

    nc = _bacc.Bacc("TRN2", target_bir_lowering=False, num_devices=1)
    arrays, args = {}, []
    for name in _INS:
        a = _np.ascontiguousarray(inputs[name])
        arrays[f"in_{name}_dram"] = a
        args.append(nc.dram_tensor(f"in_{name}_dram", a.shape, _mybir.dt.from_np(a.dtype), kind="ExternalInput").ap())
    args.append(nc.dram_tensor("out_0_dram", (N, D), _mybir.dt.float32, kind="ExternalOutput").ap())
    build(nc, *args)
    r = _run(nc, [arrays], core_ids=[0])
    return r.results[0]["out_0_dram"]
```

```python
from contextlib import ExitStack

import concourse.bass as bass
from concourse import mybir

ALU = mybir.AluOpType
ACT = mybir.ActivationFunctionType
F32 = mybir.dt.float32
BF16 = mybir.dt.bfloat16
F16 = mybir.dt.float16
I32 = mybir.dt.int32

P = 128
N = 50000
E = 12500
D = 256
C = 64
R = 16
J = 4
NG = P * J
G = -(-N // NG)
TAIL = N - (G - 1) * NG
TAILP = TAIL // J
T = -(-E // P)
T += T % 2
S = T // 2
LASTP = E - (P - 1) * T
PAD = T - LASTP
ROW = D + 1
TRASH = N
MSG_ROWS = -(-(N + 2 * P) // P)
ZERO_ROWS = 8
CLEAR_ROWS = 2
EPS = 1e-5
INV3 = 3.0 ** -0.5
XS = 8
NOWHERE = 1 << 20
assert TAIL == TAILP * J and 0 < LASTP < T and S * CLEAR_ROWS < MSG_ROWS and (MSG_ROWS - S * CLEAR_ROWS) % ZERO_ROWS


class Step:

    def __init__(self, b, u, k, n, unroll, looped=False):
        self.b, self.u, self.k, self.n, self.unroll, self.looped = b, u, k, n, unroll, looped

    def at(self, d=0):
        return self.b * self.unroll + (self.u - d)

    def live(self, d=0):
        assert not self.looped or self.k >= d, "more steps have to come before the loop"
        return 0 <= self.k - d < self.n

    def slot(self, d, m):
        return (self.u - d) % m

    def uses(self, d, m):
        return self.b * (self.unroll // m) + (self.u - d) // m + 1


def run(eng, n, skew, body, first=2, unroll=4):
    hi = n // unroll - (1 if n % unroll == 0 else 0)
    for s in range(first * unroll):
        body(Step(s // unroll, s % unroll, s, n, unroll))
    with eng.Fori(first, hi, 1) as b:
        for u in range(unroll):
            body(Step(b, u, first * unroll + u, n, unroll, looped=True))
    for s in range(hi * unroll, n + skew):
        body(Step(s // unroll, s % unroll, s, n, unroll))


def run_groups(eng, skew, body):
    run(eng, G, skew, body, first=1, unroll=XS)


class Signal:

    def __init__(self, sem, base=0):
        self.sem, self.base = sem, base


def done(eng, sem, s, d=0, per=1):
    if s.live(d):
        eng.wait_ge(sem.sem, s.at(d) * per + (per + sem.base))


def landed(eng, slots, s, d=0, dmas=1):
    if s.live(d):
        one = slots[s.slot(d, len(slots))]
        eng.wait_ge(one.sem, s.uses(d, len(slots)) * (16 * dmas) + one.base)


def all_landed(eng, slots, n, dmas=1):
    for i, one in enumerate(slots):
        eng.wait_ge(one.sem, 16 * dmas * len(range(i, n, len(slots))) + one.base)


def reused(slots, n, count):
    return [Signal(one.sem, one.base + 16 * len(range(i, n, len(slots)))) for i, one in enumerate(slots)][:count]


class Chain:

    def __init__(self, eng, sem, per=0, i=0, marked=0):
        self.eng, self.sem, self.base, self.per, self.k = eng, sem.sem, i * per + sem.base, per, marked

    def mark(self, instruction):
        self.k += 1
        instruction.then_inc(self.sem, 1)

    def wait(self):
        self.eng.wait_ge(self.sem, self.base + self.k)

    def __call__(self, instruction):
        self.mark(instruction)
        self.wait()

    def end(self):
        assert self.k == self.per, self.k


def build(nc, x, src, dst, ea16, ea4, W, b, Wup0, Wup1, M1, M2, M3, M4, Wlin0, Wlin1, Wsc0, Wsc1,
          Wc0, Wc1, WB0, WB1, gamma0, beta0, gamma1, out):
    with ExitStack() as ctx:
        def sb(name, shape, dt=F32):
            return ctx.enter_context(nc.sbuf_tensor(name, shape, dt))

        def sem(name):
            return ctx.enter_context(nc.semaphore(name))

        def sems(name, n):
            return [Signal(sem(f"{name}{i}")) for i in range(n)]

        def named(prefix, names):
            return {n: Signal(sem(f"{prefix}_{n}")) for n in names.split()}

        def after(signals, names):
            return {n: Signal(signals[n].sem, signals[n].base + S) for n in names.split()}

        def dram(name, shape, dt=F32):
            return nc.dram_tensor(name, shape, dt, kind="Internal").ap()

        x1_tab = dram("x1_tab", [N + 2 * P, ROW])
        msg_tab = dram("msg_tab", [P * MSG_ROWS, ROW])
        dinv_tab = dram("dinv_tab", [G * NG, 1])
        tpw_tab = dram("tpw_tab", [S, P, 2 * D])
        edge_o = dram("edge_o", [S, P, 2 * D])
        edge_x = dram("edge_x", [S, P, 2 * ROW])

        ident = sb("ident", [P, P])
        later = sb("later", [P, 2, 2 * P])
        ones = sb("ones", [P, P])
        ones_bf = sb("ones_bf", [3, P], BF16)
        eps_col = sb("eps_col", [P, 1])
        iota_h = sb("iota_h", [P, G * J], F16)
        trash_i = sb("trash_i", [P, 2], I32)
        trash = sb("trash", [P, 2])
        pair_i = sb("pair_i", [P, T], I32)
        pair_no = sb("pair_no", [P, T])
        valid = sb("valid", [P, T])
        vm1 = sb("vm1", [P, T])
        node_ok = sb("node_ok", [P, G * J])
        zeros = sb("zeros", [P, ZERO_ROWS * ROW])
        w_sb = sb("w_sb", [P, 2, D])
        b_f = sb("b_f", [3, 3, D])
        b_bf = sb("b_bf", [3, 3, D], BF16)
        b3 = sb("b3", [3, D], BF16)
        bias_f = sb("bias_f", [3, 3, C])
        bias_bf = sb("bias_bf", [3, 3, C], BF16)
        bias3 = sb("bias3", [3, C], BF16)
        up_w = sb("up_w", [P, 2, P])
        lin_w = sb("lin_w", [P, 2, P])
        sc_w = sb("sc_w", [P, 2, P])
        wb_w = sb("wb_w", [P, 2, P])
        fin_w = sb("fin_w", [P, 2, P])
        m_sb = sb("m_sb", [P, 3, P])
        m4_sb = sb("m4_sb", [P, 4 * C])
        sc_twice = sb("sc_twice", [P, 2, C])
        cw = sb("cw", [P, 9 * C])
        poly = sb("poly", [P, 4, 2, C])
        poly_vv = sb("poly_vv", [P, 1, C])
        g_b = sb("g_b", [P, 3, C])

        idx3 = sb("idx3", [P, 3, T], I32)
        src_c = sb("src_c", [P, T])
        dst_c = sb("dst_c", [P, T])
        src_f = sb("src_f", [P, T])
        dst_f = sb("dst_f", [P, T])
        src_delta = sb("src_delta", [P, T])
        dst_delta = sb("dst_delta", [P, T])
        int_a = sb("int_a", [P, T], I32)
        int_b = sb("int_b", [P, T], I32)
        lo_d, hi_d, lo_s, hi_s = (sb(n, [P, T]) for n in ("lo_d", "hi_d", "lo_s", "hi_s"))
        last_in_pair = sb("last_in_pair", [P, T])
        dinv_edge = sb("dinv_edge", [P, T, 2])
        final_idx = sb("final_idx", [P, T], I32)
        ea16_sb = sb("ea16_sb", [P, T * R])
        ea4_sb = sb("ea4_sb", [P, T, 4])
        deg = sb("deg", [P, G * J])
        dinv = sb("dinv", [P, G * J])
        dinv2 = sb("dinv2", [P, G * J])
        alone = sb("alone", [P, G * J])
        no_dst = sb("no_dst", [P, G * J])
        w_src = sb("w_src", [P, G * J])

        onehot = sb("onehot", [P, 2, 2, 2, P + G * J], BF16)
        rbf = sb("rbf", [P, 2, 2, C])
        mlp_t = sb("mlp_t", [P, 4, P])
        tpb = sb("tpb", [P, 2, 2, 4, C])
        big = sb("big", [P, XS, J * ROW])
        hb = sb("hb", [P, 2, J, D])
        ht = sb("ht", [P, 4, 4 * P])
        x1b = sb("x1b", [P, 2, J * ROW])
        h2b = sb("h2b", [P, 2, J, ROW])
        st = sb("st", [P, 2, J, 6])
        mv = sb("mv", [P, 2, 2, J, 2])
        sd = sb("sd", [P, 2, 2, J])
        rs = sb("rs", [P, 2, 2, 3, J])
        idx = sb("idx", [P, 2, 3], I32)
        idx_e = sb("idx_e", [P, 4, 2], I32)
        got = sb("got", [P, 2, 2])
        claim = sb("claim", [P, 2, ROW])
        xg, msg_in = (big[:, i:i + 2, :].rearrange("p b (h a d) -> p (b h) a d", h=2, a=2) for i in (4, 6))
        hg = sb("hg", [P, 2, 2, D])
        h2 = sb("h2", [P, 2, 2, ROW])
        hw = sb("hw", [P, 2, 2, D])
        vb = sb("vb", [P, 2, 2, D])
        own = sb("own", [P, 2, 4])
        sidx_f = sb("sidx_f", [P, 2])
        sidx = sb("sidx", [P, 4, 2], I32)
        eq = sb("eq", [P, 4, 2, 2 * P])
        difference = x1b[:, 0, 0:4 * P].rearrange("p (a e) -> p a e", a=2)
        eq_junk = sb("eq_junk", [P, 2, 2 * P])
        n_later = sb("n_later", [P, 2])
        coef = sb("coef", [P, 4, 2])
        addb = sb("addb", [P, 4, 2, ROW])
        dot = sb("dot", [P, 2, C])
        products = sb("products", [P, 2, 3, C])
        outer = sb("outer", [P, 2, 3, C])
        tmp_a = sb("tmp_a", [P, 2, C])
        tmp_b = sb("tmp_b", [P, 2, C])
        mt, bt = (hb[:, a, 0:2, :].rearrange("p j d -> p (j d)") for a in range(2))
        asb, asq = (x1b[:, :, i * 2 * D:(i + 1) * 2 * D].rearrange("p s (a k c) -> p s a k c", a=2, k=4)
                    for i in range(2))
        vv = sb("vv", [P, 2, C])
        term = sb("term", [P, 3, 2, 2, C])
        bsb = sb("bsb", [P, 2, 2, 4, C])
        osb = sb("osb", [P, 2, 2, 2 * D])
        lead_f = sb("lead_f", [P, 2])
        lead = sb("lead", [P, T])
        g_sb = sb("g_sb", [P, 2, C + 1])
        z_sb = sb("z_sb", [P, 3, C])
        row_sb = sb("row_sb", [1, 5 * C])
        slot_sum = sb("slot_sum", [P, 5 * C])
        fin = sb("fin", [P, 8, C])
        scale = sb("scale", [P, 4, C])
        centered = h2b[:, :, :, 0:C]
        bias = sb("bias", [P, C])

        bank = [ctx.enter_context(nc.psum_tensor(f"bank{i}", [P, 512], F32)) for i in range(8)]
        gram0, gram1 = bank[4][:, 0:P], bank[4][:, P:2 * P]

        spread = (bank[6], bank[1])
        o_bank = (bank[6], bank[5])

        f_o = big[:, 0:4, 0:2 * D].rearrange("p s (a d) -> p s a d", a=2)
        f_x = big[:, 0:4, 2 * D:2 * D + 2 * ROW].rearrange("p s (a d) -> p s a d", a=2)
        f_rows = [hb[:, a // 2, a % 2 * 2:a % 2 * 2 + 2, :] for a in range(4)]

        def xj(t, slot, width):
            return t[:, slot, 0:J * width].rearrange("p (j d) -> p j d", j=J)

        def by_component(rows):
            return rows.rearrange("p (c x) -> p x c", x=3)

        def groups(table):
            return (table[0:(G - 1) * NG, :].rearrange("(g p j) d -> g p (j d)", p=P, j=J),
                    table[(G - 1) * NG:N, :].rearrange("(p j) d -> p (j d)", j=J))

        x_groups, out_groups, x1_groups = groups(x), groups(out), groups(x1_tab)

        def group(table, s, d=0):
            return (table[1], TAILP) if s.k - d == G - 1 else (table[0][s.at(d)], P)

        def pair(t, s, d=0):
            return t[:, bass.ds(s.at(d) * 2, 2)]

        def rows_of(index):
            return bass.IndirectOffsetOnAxis(ap=index, axis=0)
        edge_loads, loads, mlp_loads = [], [], []
        for col, e in ((1, dst), (2, src)):
            edge_loads += [(idx3[0:P - 16, col, :], e[0:(P - 16) * T].rearrange("(p t) -> p t", t=T)),
                      (idx3[P - 16:P - 1, col, :], e[(P - 16) * T:(P - 1) * T].rearrange("(p t) -> p t", t=T)),
                      (idx3[P - 1:P, col, 0:LASTP], e[(P - 1) * T:E].rearrange("(p t) -> p t", p=1)),
                      (idx3[P - 1:P, col, LASTP:T], e[E - PAD:E].rearrange("(p t) -> p t", p=1))]
        for to, e, w in ((ea16_sb, ea16, R), (ea4_sb[:].rearrange("p t r -> p (t r)"), ea4, 4)):
            edge_loads += [(to[0:P - 16, :], e[0:(P - 16) * T, :].rearrange("(p t) r -> p (t r)", t=T)),
                      (to[P - 16:P - 1, :], e[(P - 16) * T:(P - 1) * T, :].rearrange("(p t) r -> p (t r)", t=T)),
                      (to[P - 1:P, 0:LASTP * w], e[(P - 1) * T:E, :].rearrange("(p t) r -> p (t r)", p=1)),
                      (to[P - 1:P, LASTP * w:T * w], e[E - PAD:E, :].rearrange("(p t) r -> p (t r)", p=1))]
        loads += [(w_sb[:, i, :], W[i * P:(i + 1) * P, :]) for i in range(2)]
        loads += [(b_f[:, 0, :], b.partition_broadcast(3))]
        for to, w0, w1 in ((up_w, Wup0, Wup1), (lin_w, Wlin0, Wlin1), (sc_w, Wsc0, Wsc1), (wb_w, WB0, WB1)):
            loads += [(to[0:C, 0, 0:C], w0), (to[C:P, 0, C:P], w1), (to[0:C, 1, 0:C], w1), (to[C:P, 1, C:P], w1)]
        loads += [(sc_twice[half, i, :], w) for half in (slice(0, C), slice(C, P)) for i, w in enumerate((Wsc0, Wsc1))]
        for half in (slice(0, C), slice(C, P)):
            mlp_loads += [(m_sb[half.start:half.start + R, 0, half], M1), (m_sb[half, 1, half], M2),
                      (m_sb[half, 2, half], M3), (m4_sb[half, :], M4)]
        loads += [(cw[:, 0:5 * C], Wc0.rearrange("c k -> (c k)").partition_broadcast(P)),
                  (cw[:, 5 * C:9 * C], Wc1.rearrange("c k -> (c k)").partition_broadcast(P))]
        loads += [(g_b[:, i, :], w.partition_broadcast(P)) for i, w in enumerate((gamma0, beta0, gamma1))]
        LOADED, MLP_LOADED = 16 * len(loads), 16 * len(mlp_loads)
        EDGES_LOADED = 16 * len(edge_loads)
        LATER_CLEARS = (MSG_ROWS - S * CLEAR_ROWS) // ZERO_ROWS
        CLEARED = 16 * (S + 2)

        pre = named("pre", "dve_chain consts edges mlp inputs prepared b3 cleared cleared_later deg root dinv dinv_out")
        cnt = named("cnt", "rbf onehot counted turned0 act0 layer1 act1 layer2 act2 layer3 act3 layer4 weights")
        tpw_out = sems("tpw_out", 2)
        p1 = named("p1", "chain_a chain_b chain_m chain_n stats1 root1 norm1 relu1 turned ht xw x1 stats2 root2 norm2 "
                         "relu2 gram idx dinv_got")
        x_in, x1_out, claim_out, dinv_in = sems("x_in", XS), sems("x1_out", 2), sems("claim_out", 1), sems("dinv_in", 2)
        e1 = named("e1", "idx own others chain_a chain_b chain_c eq sidx coef stats root norm relu turned ht xw v "
                         "merged add")
        e1_got, e1_out = sems("e1_got", 4), sems("e1_out", 1)
        e2 = named("e2", "differences chain_m weighted up gram message")
        e2 |= after(e1, "idx own others eq sidx stats root norm relu turned ht merged add")
        e2_got, e2_out, tp_in = sems("e2_got", 4), sems("e2_out", 1), sems("tp_in", 2)
        e3 = named("e3", "chain_p lead m_turned mt a_done a b b_turned bt o_done o summed")
        e3 |= after(e2, "idx stats root norm relu turned ht")
        e3_got, eo_out, ex_out = sems("e3_got", 4), sems("eo_out", 2), sems("ex_out", 4)
        fs = named("fs", "chain grams grams_end products z sums var root weights")
        p2 = named("p2", "relu0 chain_p chain_a chain_b stats root norm relu turned ht y out")
        y_in, y_out = reused(x_in, G, XS), sems("y_out", 2)
        f = named("f", "chain idx rows")
        f_in, f_out = reused(y_in, G, 4), sems("f_out", 4)

        for chain, per in (("chain_a", 1), ("chain_b", 1), ("chain_c", 3)):
            e2[chain] = Signal(e1[chain].sem, S * per)
            e3[chain] = Signal(e1[chain].sem, 2 * S * per)
        n_consts = []

        waited = {nc.gpsimd.engine: sem("waited_pool"), nc.tensor.engine: sem("waited_pe"),
                  nc.vector.engine: sem("waited_dve")}

        def settle(eng):
            eng.sem_inc(waited[eng.engine], 1)

        block = ctx.enter_context(nc.Block())

        @block.gpsimd
        def _(pool):
            g = nc.gpsimd
            n = [0]

            def const(instruction, wait=False):
                n[0] += 1
                instruction.then_inc(pre["consts"].sem, 1)
                if wait:
                    pool.wait_ge(pre["consts"].sem, n[0])

            const(g.memset(ident[:], 0.0), wait=True)
            const(g.affine_select(out=ident[:], in_=ident[:], compare_op=ALU.not_equal, fill=1.0, base=0,
                                  pattern=[[-1, P]], channel_multiplier=1))
            const(g.memset(later[:, 0, :], 1.0))
            const(g.memset(later[:, 1, 0:P], 0.0))
            const(g.memset(later[:, 1, P:2 * P], 1.0), wait=True)
            for a in range(2):
                v = later[:, a, a * P:(a + 1) * P]
                const(g.affine_select(out=v, in_=v, compare_op=ALU.is_gt, fill=0.0, base=0, pattern=[[1, P]],
                                      channel_multiplier=-1))
            const(g.memset(valid[:], 1.0))
            const(g.memset(node_ok[:], 1.0), wait=True)
            const(g.affine_select(out=valid[:], in_=valid[:], compare_op=ALU.is_gt, fill=0.0, base=E,
                                  pattern=[[-1, T]], channel_multiplier=-T))
            v = node_ok[:].rearrange("p (g j) -> p g j", j=J)
            const(g.affine_select(out=v, in_=v, compare_op=ALU.is_gt, fill=0.0, base=N, pattern=[[-NG, G], [-1, J]],
                                  channel_multiplier=-J))
            const(g.iota(iota_h[:], pattern=[[1, G * J]], base=0, channel_multiplier=0,
                         allow_small_or_imprecise_dtypes=True))
            const(g.iota(trash_i[:], pattern=[[P, 2]], base=TRASH, channel_multiplier=1))
            const(g.iota(pair_i[:], pattern=[[1, S], [0, 2]], base=0, channel_multiplier=0))
            for t in (m_sb, rbf):
                const(g.memset(t[:], 0.0))
            n_consts.append(n[0])
            for t in (up_w, lin_w, sc_w, wb_w, zeros, claim, addb):
                const(g.memset(t[:], 0.0))
            for t in (ones[:], ones_bf[:], h2b[:, :, :, 0:1], h2[:, :, :, 0:1]):
                const(g.memset(t, 1.0))
            const(g.memset(eps_col[:], EPS))
            n_consts.append(n[0])

            def rbf_step(s):
                if s.live():
                    if s.k == 0:
                        pool.wait_ge(pre["consts"].sem, n_consts[1])
                        pool.wait_ge(pre["edges"].sem, EDGES_LOADED)
                    done(pool, cnt["turned0"], s, 2)
                    settle(pool)
                    g.tensor_copy(rbf[:, s.slot(0, 2), :, 0:R],
                                  ea16_sb[:, bass.ds(s.at() * (2 * R), 2 * R)].rearrange("p (a r) -> p a r", a=2)
                                  ).then_inc(cnt["rbf"].sem, 1)

            run(pool, S, 0, rbf_step)

            m = msg_tab.rearrange("(p r) d -> p (r d)", p=P)

            def clear_step(s):
                if s.live():
                    done(pool, p1["stats1"], s, 0)
                    pool.dma_start(m[:, bass.ds(s.at() * (ZERO_ROWS * ROW) + S * CLEAR_ROWS * ROW, ZERO_ROWS * ROW)],
                                   zeros[:]).then_inc(pre["cleared_later"].sem, 16)

            run(pool, LATER_CLEARS, 0, clear_step)

            def claim_step(s):
                if s.live():
                    a = s.slot(0, 2)
                    if s.k == 0:
                        pool.wait_ge(pre["prepared"].sem, 1)
                        pool.wait_ge(pre["cleared"].sem, CLEARED)
                        pool.wait_ge(pre["cleared_later"].sem, 16 * LATER_CLEARS)
                        pool.wait_ge(pre["dinv_out"].sem, 16)
                    landed(pool, claim_out, s, 2)
                    landed(pool, dinv_in, s, 2, dmas=2)
                    settle(pool)
                    g.tensor_copy(idx[:, a, :], idx3[:, :, s.at()]).then_inc(p1["idx"].sem, 1)
                    g.tensor_copy(claim[:, a, D:ROW], pair_no[:, bass.ds(s.at(), 1)]).then_inc(p1["idx"].sem, 1)
                    done(pool, p1["idx"], s, 0, per=2)
                    done(pool, p1["dinv_got"], s, 2)
                    landed(pool, claim_out, s, 1)
                    settle(pool)
                    pool.indirect_dma_start(msg_tab, rows_of(idx[:, a, 0:1]), claim[:, a, :],
                                            None).then_inc(claim_out[0].sem, 16)
                    for i in range(2):
                        pool.indirect_dma_start(got[:, a, i:i + 1], None, dinv_tab,
                                                rows_of(idx[:, a, i + 1:i + 2])).then_inc(dinv_in[a].sem, 16)
                if s.live(1):
                    landed(pool, dinv_in, s, 1, dmas=2)
                    settle(pool)
                    g.tensor_copy(dinv_edge[:, bass.ds(s.at(1), 1), :],
                                  got[:, s.slot(1, 2), :].unsqueeze(1)).then_inc(p1["dinv_got"].sem, 1)

            run(pool, T, 1, claim_step)

            def gather(sm, got_sems, s, which, sources, free):
                a = s.slot(0, 4)
                landed(pool, got_sems, s, 4, dmas=2 * len(sources))
                settle(pool)
                g.tensor_copy(idx_e[:, a, :], idx3[:, which, bass.ds(s.at() * 2, 2)]).then_inc(sm["idx"].sem, 1)
                free(s)
                settle(pool)
                done(pool, sm["idx"], s, 0)
                settle(pool)
                for i in range(2):
                    for to, table in sources:
                        pool.indirect_dma_start(to[:, s.slot(0, 4), i, 0:table.shape[1]], None, table,
                                                rows_of(idx_e[:, a, i:i + 1])).then_inc(got_sems[s.slot(0, 4)].sem, 16)

            def scatter_add(sm, out_sems, s, d, table):
                if s.live(d):
                    done(pool, sm["add"], s, d)
                    done(pool, sm["sidx"], s, d)
                    landed(pool, out_sems, s, d + 1, dmas=2)
                    settle(pool)
                    for i in range(2):
                        pool.indirect_dma_start(table, rows_of(sidx[:, s.slot(d, 4), i:i + 1]),
                                                addb[:, s.slot(d, 4), i, :], None,
                                                compute_op=ALU.add).then_inc(out_sems[0].sem, 16)

            def e1_step(s):
                if s.live():
                    gather(e1, e1_got, s, 1, [(xg, x)], lambda s: done(pool, e1["relu"], s, 4))
                if s.k == 4:
                    all_landed(pool, x1_out, G)
                scatter_add(e1, e1_out, s, 4, x1_tab)

            pool.wait_ge(p1["x1"].sem, 2 * G)
            run(pool, S, 4, e1_step)
            all_landed(pool, e1_out, S, dmas=2)

            def e2_step(s):
                if s.live():
                    gather(e2, e2_got, s, 2, [(xg, x1_tab)], lambda s: done(pool, e2["weighted"], s, 4))
                scatter_add(e2, e2_out, s, 5, msg_tab)

            all_landed(pool, claim_out, T)
            run(pool, S, 5, e2_step)
            all_landed(pool, e2_out, S, dmas=2)

            def e3_free(s):
                done(pool, e3["relu"], s, 4)
                landed(pool, ex_out, s, 4)
                done(pool, e3["lead"], s, 4)
                done(pool, e3["m_turned"], s, 4)
                settle(pool)

            def e3_step(s):
                if s.live():
                    gather(e3, e3_got, s, 1, [(xg, x1_tab), (msg_in, msg_tab)], e3_free)

            run(pool, S, 0, e3_step)

            def p2_step(s):
                if s.live():
                    a = s.slot(0, 2)
                    one = Chain(pool, p2["chain_p"], 2, s.at())
                    done(pool, p2["norm"], s, 0)
                    done(pool, p2["turned"], s, 2, per=2)
                    settle(pool)
                    one(g.tensor_tensor(centered[:, a], xj(big, s.slot(0, XS), ROW)[:, :, 0:C],
                                        mv[:, 0, a, :, 0:1].to_broadcast([P, J, C]), ALU.subtract))
                    settle(pool)
                    one(g.tensor_scalar(centered[:, a], centered[:, a], 0.0, None, ALU.max))
                    g.tensor_tensor(hb[:, a, :, 0:C], centered[:, a],
                                    rs[:, 0, a, 0, :].unsqueeze(2).to_broadcast([P, J, C]), ALU.mult
                                    ).then_inc(p2["relu0"].sem, 1)
                    one.end()

            run_groups(pool, 0, p2_step)

            def f_step(s):
                if s.live():
                    a = s.slot(0, 4)
                    landed(pool, f_out, s, 4, dmas=2)
                    settle(pool)
                    g.tensor_copy(idx_e[:, a, :], pair(final_idx, s)).then_inc(f["idx"].sem, 1)
                if s.live(1):
                    done(pool, f["idx"], s, 1)
                    done(pool, f["rows"], s, 1)
                    settle(pool)
                    if s.k == 1:
                        all_landed(pool, y_out, G)
                    for i in range(2):
                        pool.indirect_dma_start(out, rows_of(idx_e[:, s.slot(1, 4), i:i + 1]),
                                                f_rows[s.slot(1, 4)][:, i, :], None, bounds_check=N - 1,
                                                oob_is_err=False).then_inc(f_out[s.slot(1, 4)].sem, 16)

            pool.wait_ge(e3["lead"].sem, S)
            run(pool, S, 1, f_step)
            all_landed(pool, f_out, S, dmas=2)

        @block.sync
        def _(sp):
            for to, what in edge_loads:
                sp.dma_start(to, what).then_inc(pre["edges"].sem, 16)

            sp.wait_ge(pre["consts"].sem, n_consts[1])
            for to, what in loads:
                sp.dma_start(to, what).then_inc(pre["inputs"].sem, 16)

            m = msg_tab.rearrange("(p r) d -> p (r d)", p=P)
            rest = (MSG_ROWS - S * CLEAR_ROWS) % ZERO_ROWS
            sp.dma_start(m[:, (MSG_ROWS - rest) * ROW:], zeros[:, 0:rest * ROW]).then_inc(pre["cleared"].sem, 16)
            sp.dma_start(x1_tab[N:N + 2 * P, :].rearrange("(p a) d -> p (a d)", p=P),
                         zeros[:, 0:2 * ROW]).then_inc(pre["cleared"].sem, 16)

            def tpw_step(s):
                if s.live(4):
                    done(sp, cnt["weights"], s, 4)
                    sp.dma_start(tpw_tab[s.at(4)], tpb[:, s.slot(4, 2)].rearrange("p a k c -> p (a k c)")
                                 ).then_inc(tpw_out[s.slot(4, 2)].sem, 16)
                if s.live():
                    n = CLEAR_ROWS * ROW
                    sp.dma_start(m[:, bass.ds(s.at() * n, n)], zeros[:, 0:n]).then_inc(pre["cleared"].sem, 16)

            run(sp, S, 4, tpw_step)

            def p1_step(s):
                if s.live():
                    done(sp, p1["x1"], s, XS, per=2)
                    rows, n = group(x_groups, s)
                    sp.dma_start(big[0:n, s.slot(0, XS), 0:J * D], rows).then_inc(x_in[s.slot(0, XS)].sem, 16)
                if s.live(4):
                    done(sp, p1["x1"], s, 4, per=2)
                    rows, n = group(x1_groups, s, 4)
                    sp.dma_start(rows, x1b[0:n, s.slot(4, 2), :]).then_inc(x1_out[s.slot(4, 2)].sem, 16)

            run_groups(sp, 4, p1_step)

            all_landed(sp, tpw_out, S)
            def tp_step(s):
                if s.live():
                    done(sp, e2["message"], s, 2)
                    sp.dma_start(tpb[:, s.slot(0, 2)].rearrange("p a k c -> p (a k c)"),
                                 tpw_tab[s.at()]).then_inc(tp_in[s.slot(0, 2)].sem, 16)

            run(sp, S, 0, tp_step)

            def e3_step(s):
                if s.live():
                    landed(sp, e3_got, s, 0, dmas=4)
                    sp.dma_start(edge_x[s.at()], xg[:, s.slot(0, 4)].rearrange("p a d -> p (a d)")
                                 ).then_inc(ex_out[s.slot(0, 4)].sem, 16)
                if s.live(4):
                    done(sp, e3["o"], s, 4)
                    sp.dma_start(edge_o[s.at(4)].rearrange("p (a d) -> p a d", a=2),
                                 osb[:, s.slot(4, 2), :, D:2 * D]).then_inc(eo_out[s.slot(4, 2)].sem, 16)

            run(sp, S, 4, e3_step)

            def p2_step(s):
                if s.k == 0:
                    all_landed(sp, ex_out, S)
                if s.k == 4:
                    for name in ("relu", "m_turned", "lead"):
                        sp.wait_ge(e3[name].sem, e3[name].base + S)
                if s.live():
                    done(sp, p2["out"], s, XS, per=2)
                    rows, n = group(x1_groups, s)
                    sp.dma_start(big[0:n, s.slot(0, XS), :], rows).then_inc(y_in[s.slot(0, XS)].sem, 16)
                if s.live(4):
                    done(sp, p2["out"], s, 4, per=2)
                    rows, n = group(out_groups, s, 4)
                    sp.dma_start(rows, x1b[0:n, s.slot(4, 2), 0:J * D]).then_inc(y_out[s.slot(4, 2)].sem, 16)

            run_groups(sp, 4, p2_step)

            all_landed(sp, eo_out, S)
            def f_step(s):
                if s.live():
                    a = s.slot(0, 4)
                    done(sp, f["rows"], s, 4)
                    sp.dma_start(big[:, a, 0:2 * D], edge_o[s.at()]).then_inc(f_in[a].sem, 16)
                    sp.dma_start(big[:, a, 2 * D:2 * D + 2 * ROW], edge_x[s.at()]).then_inc(f_in[a].sem, 16)

            run(sp, S, 0, f_step)
            all_landed(sp, y_out, G)

        @block.tensor
        def _(pe):
            mm = nc.tensor.matmul

            layers = ((cnt["turned0"], bank[2]), (cnt["layer1"], bank[3]), (cnt["layer2"], bank[6]),
                      (cnt["layer3"], bank[7]))

            def count_step(s):
                if s.k == 0:
                    pe.wait_ge(pre["consts"].sem, n_consts[0])
                    pe.wait_ge(pre["mlp"].sem, MLP_LOADED)
                if s.live():
                    a = s.slot(0, 2)
                    done(pe, cnt["onehot"], s, 0)
                    for i in range(2):
                        for which in range(2):
                            o = onehot[:, a, i, which, :]
                            last = mm(bank[which][:, 0:G * J], o[:, 0:P], o[:, P:P + G * J],
                                      start=(s.k == 0 and i == 0), stop=(s.k == S - 1 and i == 1))
                    last.then_inc(cnt["counted"].sem, 1)
                    done(pe, cnt["rbf"], s, 0)
                    done(pe, cnt["act0"], s, 1)
                    nc.tensor.transpose(bank[2][:, 0:P], rbf[:, a].rearrange("p a r -> p (a r)"), ident[:]
                                        ).then_inc(cnt["turned0"].sem, 1)
                for i in range(3):
                    if s.live(i + 1):
                        done(pe, cnt[f"act{i}"], s, i + 1)
                        done(pe, cnt[f"act{i + 1}"], s, i + 2)
                        mm(layers[i + 1][1][:, 0:P], m_sb[:, i, :], mlp_t[:, i, :], start=True, stop=True
                           ).then_inc(cnt[f"layer{i + 1}"].sem, 1)
                if s.live(4):
                    done(pe, cnt["act3"], s, 4)
                    done(pe, cnt["weights"], s, 5)
                    for i in range(2):
                        half = slice(i * C, (i + 1) * C)
                        last = mm(bank[4 + i][:, 0:D], mlp_t[half, 3, :], m4_sb[half, :], start=True, stop=True)
                    last.then_inc(cnt["layer4"].sem, 1)

            run(pe, S, 4, count_step)

            pe.wait_ge(pre["consts"].sem, n_consts[1])
            pe.wait_ge(pre["inputs"].sem, LOADED)
            pe.wait_ge(pre["b3"].sem, 1)
            done(pe, cnt["weights"], Step(0, S - 1, S - 1, S, 4))
            mm(bank[4][:, 0:2 * P], zeros[:, 0:P], zeros[:, 0:2 * P], start=True, stop=False)

            def add_product(gram, n, a, b):
                half = n % 2 * C
                return mm(gram[half:half + C, 0:b.shape[-1]], a, b, start=False, stop=False)


            def turn_group(sm, s):
                done(pe, sm["relu1" if sm is p1 else "relu"], s, 2)
                if sm is p2:
                    done(pe, p2["relu0"], s, 2)
                for q in range(2):
                    if s.live(3):
                        pe.wait_ge(sm["ht"].sem, s.at(3) * 2 + q + 1)
                    for j in range(2):
                        for k in range(2):
                            last = nc.tensor.transpose(bank[q][:, (2 * j + k) * P:(2 * j + k + 1) * P],
                                                       hb[:, s.slot(2, 2), 2 * q + j, k * P:(k + 1) * P], ident[:])
                    last.then_inc(sm["turned"].sem, 1)

            def p1_step(s):
                if s.live(2):
                    turn_group(p1, s)
                if s.live(5):
                    done(pe, p1["relu2"], s, 5)
                    settle(pe)
                    for j in range(J):
                        h = h2b[:, s.slot(5, 2), j, :]
                        add_product(gram0, j, h[:, 1:C + 1], h[:, 0:C + 1])
                        for c in range(3):
                            v = by_component(h[:, C + 1:ROW])[:, c, :]
                            last = add_product(gram1, j + c + 1, v, v)
                    last.then_inc(p1["gram"].sem, 1)
                if s.live(2):
                    for q in range(2):
                        if s.live(3):
                            pe.wait_ge(p1["x1"].sem, s.at(3) * 2 + q + 1)
                        pe.wait_ge(p1["ht"].sem, s.at(2) * 2 + q + 1)
                        for j in range(2):
                            y = bank[2 + q][:, j * D:(j + 1) * D]
                            for k in range(2):
                                mm(y, ht[:, q, (2 * j + k) * P:(2 * j + k + 1) * P], w_sb[:, k, :], start=(k == 0),
                                   stop=False)
                            last = mm(y, ones_bf[:], b3[:], start=False, stop=True)
                        last.then_inc(p1["xw"].sem, 1)

            run_groups(pe, 5, p1_step)

            def spread_own(sm, s):
                done(pe, sm["own"], s, 0)
                done(pe, sm["eq"], s, 2)
                for i in range(2):
                    last = mm(spread[s.slot(0, 2)][:, i * P:(i + 1) * P], 
                              own[:, s.slot(0, 2), i:i + 1].to_broadcast([P, P]), ident[:],
                              start=True, stop=True)
                last.then_inc(sm["others"].sem, 1)

            def turn(h, to, ready):
                for i in range(2):
                    for k in range(2):
                        last = nc.tensor.transpose(to[:, (2 * i + k) * P:(2 * i + k + 1) * P],
                                                   h[:, i, k * P:(k + 1) * P], ident[:])
                last.then_inc(ready.sem, 1)

            def merge(sm, s, d, rows, to):
                for i in range(2):
                    for k in range(2):
                        last = mm(to[:, i * D:(i + 1) * D], eq[:, s.slot(d, 4), k, i * P:(i + 1) * P],
                                  rows[:, k, 0:D], start=(k == 0), stop=(k == 1))
                last.then_inc(sm["merged"].sem, 1)

            def e1_step(s):
                if s.live(2):
                    done(pe, e1["relu"], s, 2)
                    done(pe, e1["ht"], s, 3)
                    turn(hg[:, s.slot(2, 2)], bank[0], e1["turned"])
                if s.live():
                    spread_own(e1, s)
                if s.live(3):
                    done(pe, e1["v"], s, 3)
                    done(pe, e1["eq"], s, 3)
                    done(pe, e1["add"], s, 4)
                    merge(e1, s, 3, vb[:, s.slot(3, 2)], bank[3])
                if s.live(2):
                    done(pe, e1["ht"], s, 2)
                    done(pe, e1["v"], s, 3)
                    for i in range(2):
                        y = bank[2][:, i * D:(i + 1) * D]
                        for k in range(2):
                            mm(y, ht[:, 0, (2 * i + k) * P:(2 * i + k + 1) * P], w_sb[:, k, :], start=(k == 0),
                               stop=False)
                        last = mm(y, ones_bf[:], b3[:], start=False, stop=True)
                    last.then_inc(e1["xw"].sem, 1)

            run(pe, S, 3, e1_step)

            def e2_step(s):
                if s.live(2):
                    done(pe, e2["relu"], s, 2)
                    done(pe, e2["ht"], s, 3)
                    turn(h2[:, s.slot(2, 2), :, 1:ROW], bank[0], e2["turned"])
                if s.live():
                    spread_own(e2, s)
                if s.live(4):
                    done(pe, e2["message"], s, 4)
                    done(pe, e2["eq"], s, 4)
                    done(pe, e2["add"], s, 5)
                    merge(e2, s, 4, msg_in[:, s.slot(4, 4)], bank[7])
                if s.live(2):
                    done(pe, e2["ht"], s, 2)
                    done(pe, e2["message"], s, 4)
                    for i in range(2):
                        for k in range(2):
                            last = mm(bank[2 + s.slot(2, 2)][:, i * D + k * P:i * D + (k + 1) * P],
                                      ht[:, 0, (2 * i + k) * P:(2 * i + k + 1) * P], up_w[:, k, :], start=True,
                                      stop=True)
                    last.then_inc(e2["up"].sem, 1)
                    done(pe, e2["weighted"], s, 2)
                    settle(pe)
                    for i in range(2):
                        h, w = h2[:, s.slot(2, 2), i, :], hw[:, s.slot(2, 2), i, :]
                        add_product(gram0, i, w[:, 0:C], h[:, 0:C + 1])
                        for c in range(1, 4):
                            last = add_product(gram1, i + c, w[:, c * C:(c + 1) * C], h[:, 1 + c * C:1 + (c + 1) * C])
                    last.then_inc(e2["gram"].sem, 1)

            run(pe, S, 4, e2_step)

            def e3_step(s):
                if s.live(2):
                    landed(pe, e3_got, s, 2, dmas=4)
                    done(pe, e3["mt"], s, 3)
                    turn(msg_in[:, s.slot(2, 4)], bank[1], e3["m_turned"])
                if s.live(2):
                    done(pe, e3["relu"], s, 2)
                    done(pe, e3["ht"], s, 3)
                    turn(h2[:, s.slot(2, 2), :, 1:ROW], bank[0], e3["turned"])
                if s.live(6):
                    done(pe, e3["o"], s, 6)
                    for i in range(2):
                        last = mm(bank[7][0:1, 0:5 * C], ones[:, 0:1], osb[:, s.slot(6, 2), i, 0:5 * C],
                                  start=(s.k == 6 and i == 0), stop=(s.k == S + 5 and i == 1))
                    last.then_inc(e3["summed"].sem, 1)
                if s.live(4):
                    done(pe, e3["b"], s, 4)
                    done(pe, e3["bt"], s, 5)
                    turn(bsb[:, s.slot(4, 2)].rearrange("p a k c -> p a (k c)"), bank[3], e3["b_turned"])
                if s.live(2):
                    done(pe, e3["mt"], s, 2)
                    done(pe, e3["a"], s, 3)
                    for i in range(2):
                        for k in range(2):
                            last = mm(bank[2][:, i * D + k * P:i * D + (k + 1) * P],
                                      mt[:, (2 * i + k) * P:(2 * i + k + 1) * P], lin_w[:, k, :], start=True, stop=True)
                    last.then_inc(e3["a_done"].sem, 1)
                if s.live(4):
                    done(pe, e3["bt"], s, 4)
                    done(pe, e3["ht"], s, 4)
                    done(pe, e3["o"], s, 6)
                    for i in range(2):
                        for k in range(2):
                            y = o_bank[s.slot(4, 2)][:, i * D + k * P:i * D + (k + 1) * P]
                            at = slice((2 * i + k) * P, (2 * i + k + 1) * P)
                            mm(y, bt[:, at], wb_w[:, k, :], start=True, stop=False)
                            last = mm(y, ht[:, s.slot(4, 4), at], sc_w[:, k, :], start=False, stop=True)
                    last.then_inc(e3["o_done"].sem, 1)

            run(pe, S, 6, e3_step)

            mm(bank[4][:, 0:2 * P], zeros[:, 0:P], zeros[:, 0:2 * P], start=False, stop=True
               ).then_inc(fs["grams_end"].sem, 1)
            pe.wait_ge(fs["grams"].sem, 1)
            for i in range(2):
                mm(bank[i][0:C, 0:C], g_sb[:, i, 1 - i:1 - i + C], sc_twice[:, i, :], start=True,
                   stop=True).then_inc(fs["products"].sem, 1)
            pe.wait_ge(fs["z"].sem, 1)
            mm(bank[2][:, 0:2 * C], ones[0:C, :], z_sb[0:C, 0:2].rearrange("p a c -> p (a c)"), start=True, stop=True)
            mm(bank[2][:, 2 * C:3 * C], ones[:], z_sb[:, 2], start=True, stop=True)
            mm(bank[3][:, 0:5 * C], ones[0:1, :], row_sb[:], start=True, stop=True).then_inc(fs["sums"].sem, 1)

            pe.wait_ge(fs["weights"].sem, 1)

            def p2_step(s):
                if s.live(2):
                    turn_group(p2, s)
                    for q in range(2):
                        if s.live(3):
                            pe.wait_ge(p2["out"].sem, s.at(3) * 2 + q + 1)
                        pe.wait_ge(p2["ht"].sem, s.at(2) * 2 + q + 1)
                        for j in range(2):
                            for k in range(2):
                                y = bank[2 + q][:, j * D + k * P:j * D + (k + 1) * P]
                                last = mm(y, ht[:, q, (2 * j + k) * P:(2 * j + k + 1) * P], fin_w[:, k, :], start=True,
                                          stop=(k == 1))
                                if k == 0:
                                    mm(y[:, 0:C], ones_bf[:], bias3[:], start=False, stop=True)
                        last.then_inc(p2["y"].sem, 1)

            run_groups(pe, 2, p2_step)

        @block.scalar
        def _(act):
            s_act = nc.scalar.activation

            act.wait_ge(pre["consts"].sem, n_consts[0])
            for to, what in mlp_loads:
                act.dma_start(to, what).then_inc(pre["mlp"].sem, 16)

            def count_step(s):
                if s.live():
                    done(act, cnt["turned0"], s, 0)
                    done(act, cnt["layer1"], s, 1)
                    nc.scalar.copy(mlp_t[:, 0, :], bank[2][:, 0:P]).then_inc(cnt["act0"].sem, 1)
                for i, from_ in ((1, bank[3]), (2, bank[6]), (3, bank[7])):
                    if s.live(i):
                        done(act, cnt[f"layer{i}"], s, i)
                        done(act, cnt[f"layer{i + 1}"], s, i + 1)
                        s_act(mlp_t[:, i, :], from_[:, 0:P], ACT.Silu).then_inc(cnt[f"act{i}"].sem, 1)
                if s.live(4):
                    done(act, cnt["layer4"], s, 4)
                    landed(act, tpw_out, s, 6)
                    for i in range(2):
                        last = nc.scalar.copy(tpb[:, s.slot(4, 2), i].rearrange("p k c -> p (k c)"),
                                              bank[4 + i][:, 0:D])
                    last.then_inc(cnt["weights"].sem, 1)

            run(act, S, 4, count_step)
            act.wait_ge(pre["consts"].sem, n_consts[1])
            act.wait_ge(pre["deg"].sem, 1)
            s_act(deg[:], deg[:], ACT.Sqrt).then_inc(pre["root"].sem, 1)
            act.wait_ge(pre["dinv"].sem, 1)
            act.dma_start(dinv_tab.rearrange("(g p j) a -> p g (j a)", p=P, j=J),
                          dinv[:].rearrange("p (g j) -> p g j", j=J)).then_inc(pre["dinv_out"].sem, 16)

            def root(sm, which, k, a, n, s, d=0):
                done(act, sm[f"stats{which}"], s, d)
                s_act(sd[:, k, a, 0:n], mv[:, k, a, 0:n, 1], ACT.Sqrt, bias=eps_col[:]
                      ).then_inc(sm[f"root{which}"].sem, 1)

            def p1_step(s):
                def relu1(j):
                    a = s.slot(1, 2)
                    return s_act(hb[:, a, j, :], xj(big, s.slot(1, XS), D)[:, j, :], ACT.Relu,
                                 bias=rs[:, 0, a, 1, j:j + 1], scale=rs[:, 0, a, 0, j:j + 1])

                def relu2(d, j):
                    a = s.slot(d, 2)
                    return s_act(h2b[:, a, j, 1:ROW], xj(x1b, a, ROW)[:, j, 0:D], ACT.Relu,
                                 bias=rs[:, 1, a, 2, j:j + 1], scale=rs[:, 1, a, 1, j:j + 1])

                if s.live(2):
                    for q in range(2):
                        act.wait_ge(p1["turned"].sem, s.at(2) * 2 + q + 1)
                        if s.live(3):
                            act.wait_ge(p1["xw"].sem, s.at(3) * 2 + q + 1)
                        nc.scalar.copy(ht[:, q, :], bank[q][:]).then_inc(p1["ht"].sem, 1)
                if s.live(4):
                    relu2(4, 2)
                    relu2(4, 3).then_inc(p1["relu2"].sem, 1)
                if s.live(1):
                    done(act, p1["norm1"], s, 1)
                    done(act, p1["turned"], s, 3, per=2)
                    relu1(0)
                    relu1(1)
                if s.live(3):
                    root(p1, "2", 1, s.slot(3, 2), J, s, 3)
                if s.live(1):
                    relu1(2)
                    relu1(3).then_inc(p1["relu1"].sem, 1)
                if s.live(3):
                    done(act, p1["norm2"], s, 3)
                    done(act, p1["gram"], s, 5)
                    relu2(3, 0)
                    relu2(3, 1)
                if s.live():
                    root(p1, "1", 0, s.slot(0, 2), J, s)

            run_groups(act, 4, p1_step)

            def relu_by_component(h, rows, r, j):
                s_act(h[:, 0:C], rows[:, 0:C], ACT.Relu, bias=r[:, 1, j:j + 1], scale=r[:, 0, j:j + 1])
                return relu_vectors(h, rows, r, j)

            def relu_vectors(h, rows, r, j):
                return s_act(by_component_out(h[:, C:D]), by_component(rows[:, C:D]), ACT.Relu,
                             bias=r[:, 1, j:j + 1], scale=r[:, 0, j:j + 1])

            def by_component_out(h):
                return h.rearrange("p (x c) -> p x c", x=3)

            def merged_rows(sm, out_sems, s, d, merged):
                done(act, sm["merged"], s, d)
                landed(act, out_sems, s, d + 4, dmas=2)
                nc.scalar.copy(addb[:, s.slot(d, 4), :, 0:D], merged[:].rearrange("p (a d) -> p a d", a=2)
                               ).then_inc(sm["add"].sem, 1)

            def e1_step(s):
                if s.live(3):
                    a = s.slot(3, 2)
                    done(act, e1["xw"], s, 3)
                    done(act, e1["coef"], s, 3)
                    done(act, e1["merged"], s, 5)
                    for i in range(2):
                        last = s_act(vb[:, a, i, :], bank[2][:, i * D:(i + 1) * D], ACT.Identity,
                                     scale=coef[:, s.slot(3, 4), i:i + 1])
                    last.then_inc(e1["v"].sem, 1)
                if s.live(2):
                    done(act, e1["turned"], s, 2)
                    done(act, e1["xw"], s, 3)
                    nc.scalar.copy(ht[:, 0, :], bank[0][:]).then_inc(e1["ht"].sem, 1)
                if s.live(1):
                    a = s.slot(1, 2)
                    done(act, e1["norm"], s, 1)
                    done(act, e1["turned"], s, 3)
                    for i in range(2):
                        last = s_act(hg[:, a, i, :], xg[:, s.slot(1, 4), i, 0:D], ACT.Relu,
                                     bias=rs[:, 0, a, 1, i:i + 1], scale=rs[:, 0, a, 0, i:i + 1])
                    last.then_inc(e1["relu"].sem, 1)
                if s.live():
                    root(e1, "", 0, s.slot(0, 2), 2, s)
                if s.live(3):
                    merged_rows(e1, e1_out, s, 3, bank[3])

            run(act, S, 3, e1_step)

            def e2_step(s):
                if s.live(2):
                    done(act, e2["turned"], s, 2)
                    done(act, e2["up"], s, 3)
                    nc.scalar.copy(ht[:, 0, :], bank[0][:]).then_inc(e2["ht"].sem, 1)
                if s.live(1):
                    a = s.slot(1, 2)
                    done(act, e2["norm"], s, 1)
                    done(act, e2["gram"], s, 3)
                    for i in range(2):
                        last = relu_by_component(h2[:, a, i, 1:ROW], xg[:, s.slot(1, 4), i, :], rs[:, 0, a], i)
                    last.then_inc(e2["relu"].sem, 1)
                if s.live():
                    root(e2, "", 0, s.slot(0, 2), 2, s)
                if s.live(1):
                    done(act, e2["others"], s, 1)
                    done(act, e2["own"], s, 1)
                    done(act, e2["eq"], s, 2)
                    done(act, e2["merged"], s, 5)
                    for i in range(2):
                        last = s_act(difference[:, i, :], spread[s.slot(1, 2)][:, 0:2 * P], ACT.Square,
                                     bias=own[:, s.slot(1, 2), 2 + i:3 + i])
                    last.then_inc(e2["differences"].sem, 1)
                if s.live(1):
                    done(act, e2["relu"], s, 1)
                    for i in range(2):
                        last = s_act(hw[:, a, i, :], h2[:, a, i, 1:ROW], ACT.Identity,
                                     scale=xg[:, s.slot(1, 4), i, D:ROW])
                    last.then_inc(e2["weighted"].sem, 1)
                    done(act, e2["differences"], s, 1)
                    s_act(eq[:, s.slot(1, 4)], difference, ACT.Relu, bias=ones[:, 0:1], scale=-1.0
                          ).then_inc(e2["eq"].sem, 1)
                if s.live(4):
                    merged_rows(e2, e2_out, s, 4, bank[7])

            run(act, S, 4, e2_step)

            def e3_step(s):
                if s.live(3):
                    a = s.slot(3, 2)
                    done(act, e3["a_done"], s, 3)
                    done(act, e3["b"], s, 5)
                    nc.scalar.copy(asb[:, a].rearrange("p a k c -> p (a k c)"), bank[2][:])
                    s_act(asq[:, a].rearrange("p a k c -> p (a k c)"), bank[2][:], ACT.Square).then_inc(e3["a"].sem, 1)
                if s.live(2):
                    done(act, e3["m_turned"], s, 2)
                    done(act, e3["a_done"], s, 3)
                    nc.scalar.copy(mt, bank[1][:]).then_inc(e3["mt"].sem, 1)
                if s.live(2):
                    done(act, e3["turned"], s, 2)
                    done(act, e3["o_done"], s, 6)
                    nc.scalar.copy(ht[:, s.slot(2, 4), :], bank[0][:]).then_inc(e3["ht"].sem, 1)
                if s.live(4):
                    done(act, e3["b_turned"], s, 4)
                    done(act, e3["o_done"], s, 5)
                    nc.scalar.copy(bt, bank[3][:]).then_inc(e3["bt"].sem, 1)
                if s.live(5):
                    a = s.slot(5, 2)
                    done(act, e3["o_done"], s, 5)
                    done(act, e3["summed"], s, 7)
                    landed(act, eo_out, s, 7)
                    for i in range(2):
                        o = o_bank[a][:, i * D:(i + 1) * D]
                        leads = lead[:, bass.ds(s.at(5) * 2 + i, 1)]
                        s_act(osb[:, a, i, 0:D], o, ACT.Square, scale=leads)
                        last = s_act(osb[:, a, i, D:2 * D], o, ACT.Identity, scale=leads)
                    last.then_inc(e3["o"].sem, 1)
                if s.live(1):
                    a = s.slot(1, 2)
                    done(act, e3["norm"], s, 1)
                    done(act, e3["turned"], s, 3)
                    for i in range(2):
                        last = relu_by_component(h2[:, a, i, 1:ROW], xg[:, s.slot(1, 4), i, :], rs[:, 0, a], i)
                    last.then_inc(e3["relu"].sem, 1)
                if s.live():
                    root(e3, "", 0, s.slot(0, 2), 2, s)

            run(act, S, 5, e3_step)

            for i in range(2):
                act.wait_ge(fs["var"].sem, i + 1)
                s_act(fin[:, 6 + i, :], fin[:, 4 + i, :], ACT.Sqrt, bias=eps_col[:]).then_inc(fs["root"].sem, 1)

            def p2_step(s):
                a = s.slot(1, 2)
                if s.live(1):
                    done(act, p2["norm"], s, 1)
                    done(act, p2["turned"], s, 3, per=2)
                for q in range(2):
                    if s.live(1):
                        relu_vectors(hb[:, a, q, :], xj(big, s.slot(1, XS), ROW)[:, q, :], rs[:, 0, a], q)
                    if s.live(2):
                        act.wait_ge(p2["turned"].sem, s.at(2) * 2 + q + 1)
                        if s.live(3):
                            act.wait_ge(p2["y"].sem, s.at(3) * 2 + q + 1)
                        nc.scalar.copy(ht[:, q, :], bank[q][:]).then_inc(p2["ht"].sem, 1)
                if s.live():
                    root(p2, "", 0, s.slot(0, 2), J, s)
                if s.live(1):
                    for j in range(2, J):
                        last = relu_vectors(hb[:, a, j, :], xj(big, s.slot(1, XS), ROW)[:, j, :], rs[:, 0, a], j)
                    last.then_inc(p2["relu"].sem, 1)

            run_groups(act, 2, p2_step)

        @block.vector
        def _(dve):
            v = nc.vector
            link = Chain(dve, pre["dve_chain"])

            dve.wait_ge(pre["consts"].sem, n_consts[0])
            dve.wait_ge(pre["edges"].sem, EDGES_LOADED)
            v.tensor_copy(trash[:], trash_i[:])
            v.tensor_copy(pair_no[:], pair_i[:])
            v.tensor_scalar(vm1[:], valid[:], -1.0, None, ALU.add)
            v.tensor_copy(dst_f[:], idx3[:, 1, :])
            link(v.tensor_copy(src_f[:], idx3[:, 2, :]))
            v.tensor_tensor(dst_c[:], dst_f[:], valid[:], ALU.mult)
            link(v.tensor_tensor(src_c[:], src_f[:], valid[:], ALU.mult))
            link(v.scalar_tensor_tensor(out=idx3[:, 0, :], in0=vm1[:], scalar=-float(TRASH + P - 1), in1=dst_c[:],
                                        op0=ALU.mult, op1=ALU.add))
            v.tensor_tensor(dst_c[:], dst_c[:], vm1[:], ALU.add)
            v.tensor_tensor(src_c[:], src_c[:], vm1[:], ALU.add)
            for delta, index in ((dst_delta, dst_f), (src_delta, src_f)):
                for i in range(2):
                    v.tensor_scalar(delta[:].rearrange("p (s a) -> p a s", a=2)[:, i],
                                    index[:].rearrange("p (s a) -> p a s", a=2)[:, i], trash[:, i:i + 1], None,
                                    ALU.subtract)
            for col, lo, hi in ((1, lo_d, hi_d), (2, lo_s, hi_s)):
                link(v.tensor_scalar(int_a[:], idx3[:, col, :], 2, P - 1, ALU.logical_shift_right, ALU.bitwise_and))
                link(v.tensor_copy(lo[:], int_a[:]))
                link(v.tensor_tensor(lo[:], lo[:], valid[:], ALU.mult))
                v.tensor_tensor(lo[:], lo[:], vm1[:], ALU.add)
                v.tensor_scalar(int_a[:], idx3[:, col, :], 9, 2, ALU.logical_shift_right, ALU.logical_shift_left)
                link(v.tensor_scalar(int_b[:], idx3[:, col, :], J - 1, None, ALU.bitwise_and))
                link(v.tensor_tensor(int_a[:], int_a[:], int_b[:], ALU.bitwise_or))
                link(v.tensor_copy(hi[:], int_a[:]))
            v.tensor_copy(int_b[:], int_a[:]).then_inc(pre["prepared"].sem, 1)

            def three_parts(chain, f, bf, to):
                chain(v.tensor_copy(bf[:, 0, :], f[:, 0, :]))
                chain(v.tensor_tensor(f[:, 1, :], f[:, 0, :], bf[:, 0, :], ALU.subtract))
                chain(v.tensor_copy(bf[:, 1, :], f[:, 1, :]))
                chain(v.tensor_tensor(f[:, 2, :], f[:, 1, :], bf[:, 1, :], ALU.subtract))
                chain(v.tensor_copy(bf[:, 2, :], f[:, 2, :]))
                chain(v.tensor_scalar(to[:], bf[:, 0, :], ident[0:3, 0:1], None, ALU.mult))
                chain(v.scalar_tensor_tensor(out=to[:], in0=bf[:, 1, :], scalar=ident[0:3, 1:2], in1=to[:],
                                             op0=ALU.mult, op1=ALU.add))
                return v.scalar_tensor_tensor(out=to[:], in0=bf[:, 2, :], scalar=ident[0:3, 2:3], in1=to[:],
                                              op0=ALU.mult, op1=ALU.add)

            def onehot_step(s):
                if s.live():
                    done(dve, cnt["counted"], s, 2)
                    for i in range(2):
                        for which, lo, hi in ((0, lo_d, hi_d), (1, lo_s, hi_s)):
                            o = onehot[:, s.slot(0, 2), i, which, :]
                            v.tensor_scalar(o[:, 0:P], iota_h[:, 0:P], lo[:, bass.ds(s.at() * 2 + i, 1)], None,
                                            ALU.is_equal)
                            last = v.tensor_scalar(o[:, P:P + G * J], iota_h[:], hi[:, bass.ds(s.at() * 2 + i, 1)],
                                                   None, ALU.is_equal)
                    last.then_inc(cnt["onehot"].sem, 1)

            run(dve, S, 0, onehot_step)
            dve.wait_ge(pre["inputs"].sem, LOADED)
            dve.wait_ge(pre["consts"].sem, n_consts[1])
            three_parts(link, b_f, b_bf, b3).then_inc(pre["b3"].sem, 1)

            c0 = cw[:, 0:5 * C].rearrange("p (c k) -> p k c", k=5)
            c1 = cw[:, 5 * C:9 * C].rearrange("p (c k) -> p k c", k=4)
            for i, k in enumerate((0, 1, 3, 4)):
                v.tensor_copy(poly[:, i, 0, :], c0[:, k])
                v.tensor_copy(poly[:, i, 1, :], c1[:, i])
            link(v.tensor_copy(poly_vv[:, 0, :], c0[:, 2]))

            dve.wait_ge(cnt["counted"].sem, S)
            ends, starts = bank[0][:, 0:G * J], bank[1][:, 0:G * J]
            v.tensor_scalar(deg[:], ends, 1.0, None, ALU.add).then_inc(pre["deg"].sem, 1)
            v.tensor_scalar(no_dst[:], ends, 0.0, None, ALU.is_equal)
            v.tensor_scalar(w_src[:], starts, 1.0, None, ALU.max)
            link(v.scalar_tensor_tensor(out=alone[:], in0=starts, scalar=0.0, in1=node_ok[:], op0=ALU.is_equal,
                                        op1=ALU.mult))
            v.tensor_tensor(alone[:], alone[:], no_dst[:], ALU.mult)
            link(v.reciprocal(w_src[:], w_src[:]))
            link(v.tensor_tensor(w_src[:], w_src[:], no_dst[:], ALU.mult))
            dve.wait_ge(pre["root"].sem, 1)
            link(v.reciprocal(dinv[:], deg[:]))
            v.tensor_tensor(dinv2[:], dinv[:], dinv[:], ALU.mult).then_inc(pre["dinv"].sem, 1)
            dve.wait_ge(pre["dinv"].sem, 1)

            def moments(sm, chain, k, rows, s, d=0):
                one = Chain(dve, sm[chain], 1, s.at(d))
                for j, row in enumerate(rows):
                    last = v.bn_stats(st[:, k, j, :], row)
                one.mark(last)
                return one

            def mean_variance(sm, one, signal, k, a, n):
                one.wait()
                settle(dve)
                for j in range(n):
                    last = v.bn_aggr(mv[:, k, a, j, :], st[:, k, j, :])
                last.then_inc(sm[signal].sem, 1)
                one.end()

            def one_over(sm, a, n, s, d):
                one = Chain(dve, sm["chain_b"], 1, s.at(d))
                done(dve, sm["root1" if sm is p1 else "root"], s, d)
                one.mark(v.reciprocal(rs[:, 0, a, 0, 0:n], sd[:, 0, a, 0:n]))
                return one

            def minus_mean(sm, one, a, n):
                one.wait()
                v.scalar_tensor_tensor(out=rs[:, 0, a, 1, 0:n], in0=mv[:, 0, a, 0:n, 0], scalar=-1.0,
                                       in1=rs[:, 0, a, 0, 0:n], op0=ALU.mult, op1=ALU.mult
                                       ).then_inc(sm["norm1" if sm is p1 else "norm"].sem, 1)
                one.end()

            def p1_step(s):
                def own_moments(js):
                    for j in js:
                        last = v.bn_stats(st[:, 0, j, :], xj(big, s.slot(0, XS), D)[:, j, :])
                    return last

                a = s.slot(3, 2)
                if s.live():
                    landed(dve, x_in, s)
                    own_moments((0,))
                if s.live(3):
                    mean_variance(p1, Chain(dve, p1["chain_m"], 1, s.at(3), marked=1), "stats2", 1, a, J)
                if s.live():
                    own_moments((1, 2))
                if s.live(3):
                    one = Chain(dve, p1["chain_n"], 2, s.at(3))
                    done(dve, p1["root2"], s, 3)
                    one.mark(v.reciprocal(rs[:, 1, a, 0, :], sd[:, 1, a, :]))
                if s.live():
                    sums = Chain(dve, p1["chain_a"], 1, s.at())
                    sums.mark(own_moments((3,)))
                if s.live(3):
                    one.wait()
                    one.mark(v.tensor_tensor(rs[:, 1, a, 1, :], rs[:, 1, a, 0, :], alone[:, bass.ds(s.at(3) * J, J)],
                                             ALU.mult))
                if s.live(2):
                    x1 = xj(x1b, s.slot(2, 2), ROW)
                    landed(dve, x1_out, s, 4)
                    done(dve, p1["relu2"], s, 4)
                    v.tensor_copy(x1[:, :, D], w_src[:, bass.ds(s.at(2) * J, J)])
                if s.live(3):
                    one.wait()
                    v.scalar_tensor_tensor(out=rs[:, 1, a, 2, :], in0=mv[:, 1, a, :, 0], scalar=-1.0,
                                           in1=rs[:, 1, a, 1, :], op0=ALU.mult, op1=ALU.mult
                                           ).then_inc(p1["norm2"].sem, 1)
                    one.end()
                if s.live():
                    mean_variance(p1, sums, "stats1", 0, s.slot(0, 2), J)
                if s.live(2):
                    for q in range(2):
                        dve.wait_ge(p1["xw"].sem, s.at(2) * 2 + q + 1)
                        for i in range(2):
                            j = 2 * q + i
                            last = v.scalar_tensor_tensor(
                                out=x1[:, j, 0:D], in0=bank[2 + q][:, i * D:(i + 1) * D],
                                scalar=dinv2[:, bass.ds(s.at(2) * J + j, 1)], in1=xj(big, s.slot(2, XS), D)[:, j, :],
                                op0=ALU.mult, op1=ALU.add)
                        last.then_inc(p1["x1"].sem, 1)
                if s.live():
                    norm = one_over(p1, s.slot(0, 2), J, s, 0)
                if s.live(2):
                    done(dve, p1["x1"], s, 2, per=2)
                    v.bn_stats(st[:, 1, 0, :], x1[:, 0, 0:D])
                if s.live():
                    minus_mean(p1, norm, s.slot(0, 2), J)
                if s.live(2):
                    for j in range(1, J):
                        last = v.bn_stats(st[:, 1, j, :], x1[:, j, 0:D])
                    Chain(dve, p1["chain_m"], 1, s.at(2)).mark(last)

            run_groups(dve, 3, p1_step)

            def same_index(sm, s, d):
                done(dve, sm["others"], s, d)
                done(dve, sm["merged"], s, d + 4)
                for i in range(2):
                    last = v.tensor_scalar(eq[:, s.slot(d, 4), i, :], spread[s.slot(d, 2)][:, 0:2 * P],
                                           own[:, s.slot(d, 2), i:i + 1], None, ALU.is_equal)
                last.then_inc(sm["eq"].sem, 1)

            def count_later(sm, s, d):
                one = Chain(dve, sm["chain_c"], 3, s.at(d))
                done(dve, sm["eq"], s, d)
                for i in range(2):
                    last = v.tensor_tensor_reduce(out=eq_junk[:, i, :], in0=eq[:, s.slot(d, 4), i, :],
                                                  in1=later[:, i, :], scale=1.0, scalar=0.0, op0=ALU.mult,
                                                  op1=ALU.add, accum_out=n_later[:, i:i + 1])
                one.mark(last)
                return one

            def find_last(one, s, d):
                one.wait()
                one.mark(v.scalar_tensor_tensor(out=pair(last_in_pair, s, d), in0=n_later[:], scalar=0.0,
                                                in1=pair(valid, s, d), op0=ALU.is_equal, op1=ALU.mult))

            def offset(one, s, d, delta):
                one.wait()
                one.mark(v.tensor_tensor(sidx_f[:], pair(last_in_pair, s, d), pair(delta, s, d), ALU.mult))

            def scatter_to(sm, one, out_sems, s, d):
                one.wait()
                landed(dve, out_sems, s, d + 4, dmas=2)
                v.tensor_tensor(sidx[:, s.slot(d, 4), :], sidx_f[:], trash[:], ALU.add).then_inc(sm["sidx"].sem, 1)
                one.end()

            def edge_moments(sm, got_sems, s, dmas):
                landed(dve, got_sems, s, 0, dmas=dmas)
                return moments(sm, "chain_a", 0, [xg[:, s.slot(0, 4), i, 0:D] for i in range(2)], s)

            def take_own(sm, s, index):
                done(dve, sm["others"], s, 2)
                if sm is e2:
                    done(dve, e2["differences"], s, 2)
                    v.tensor_scalar(own[:, s.slot(0, 2), 2:4], pair(index, s), -1.0, None, ALU.mult)
                v.tensor_copy(own[:, s.slot(0, 2), 0:2], pair(index, s)).then_inc(sm["own"].sem, 1)
                done(dve, sm["own"], s, 0)

            dve.wait_ge(p1["dinv_got"].sem, T)

            def e1_step(s):
                if s.live():
                    take_own(e1, s, src_c)
                if s.live(1):
                    norm = one_over(e1, s.slot(1, 2), 2, s, 1)
                if s.live():
                    sums = edge_moments(e1, e1_got, s, 2)
                if s.live(1):
                    minus_mean(e1, norm, s.slot(1, 2), 2)
                    same_index(e1, s, 1)
                if s.live():
                    mean_variance(e1, sums, "stats", 0, s.slot(0, 2), 2)
                if s.live(1):
                    last_ones = count_later(e1, s, 1)
                    done(dve, e1["v"], s, 5)
                    c = pair(dinv_edge, s, 1)
                    v.tensor_tensor(coef[:, s.slot(1, 4), :], c[:, :, 0], c[:, :, 1], ALU.mult
                                    ).then_inc(e1["coef"].sem, 1)
                    find_last(last_ones, s, 1)
                    offset(last_ones, s, 1, src_delta)
                    scatter_to(e1, last_ones, e1_out, s, 1)

            run(dve, S, 1, e1_step)

            def e2_step(s):
                message = s.live(3)
                if s.live():
                    take_own(e2, s, dst_c)
                if s.live(1):
                    norm = one_over(e2, s.slot(1, 2), 2, s, 1)
                if message:
                    one = Chain(dve, e2["chain_m"], 4, s.at(3))
                    done(dve, e2["up"], s, 3)
                    landed(dve, tp_in, s, 3)
                    w = tpb[:, s.slot(3, 2)]
                    up = bank[2 + s.slot(3, 2)][:].rearrange("p (a k c) -> p a k c", a=2, k=4)
                    m = msg_in[:, s.slot(3, 4), :, 0:D].rearrange("p a (k c) -> p a k c", k=4)
                    s1 = pair(ea4_sb, s, 3)[:, :, 1:4].unsqueeze(3).to_broadcast([P, 2, 3, C])
                    s0 = [ea4_sb[:, bass.ds(s.at(3) * 2 + i, 1), 0] for i in range(2)]
                    one.mark(v.tensor_tensor(products[:], up[:, :, 1:4, :], s1, ALU.mult))
                if s.live(1):
                    minus_mean(e2, norm, s.slot(1, 2), 2)
                if s.live():
                    sums = edge_moments(e2, e2_got, s, 2)
                if s.live(2):
                    last_ones = count_later(e2, s, 2)
                if s.live():
                    mean_variance(e2, sums, "stats", 0, s.slot(0, 2), 2)
                if message:
                    one.wait()
                    v.tensor_tensor(tmp_a[:], w[:, :, 1, :], up[:, :, 0, :], ALU.mult)
                    one.mark(v.tensor_tensor(dot[:], products[:, :, 0, :], products[:, :, 1, :], ALU.add))
                if s.live(2):
                    find_last(last_ones, s, 2)
                if message:
                    for i in range(2):
                        v.scalar_tensor_tensor(out=m[:, i, 1:4, :], in0=up[:, i, 1:4, :], scalar=s0[i],
                                               in1=w[:, i, 2:3, :].to_broadcast([P, 3, C]), op0=ALU.mult,
                                               op1=ALU.mult)
                if s.live(2):
                    offset(last_ones, s, 2, dst_delta)
                if message:
                    one.wait()
                    v.tensor_tensor(dot[:], dot[:], products[:, :, 2, :], ALU.add)
                    one.mark(v.tensor_tensor(outer[:], tmp_a[:].unsqueeze(2).to_broadcast([P, 2, 3, C]), s1, ALU.mult))
                if s.live(2):
                    scatter_to(e2, last_ones, e2_out, s, 2)
                if message:
                    one.wait()
                    v.tensor_tensor(tmp_b[:], w[:, :, 3, :], dot[:], ALU.mult)
                    for i in range(2):
                        last = v.scalar_tensor_tensor(out=m[:, i, 0, :], in0=up[:, i, 0, :], scalar=s0[i],
                                                      in1=w[:, i, 0, :], op0=ALU.mult, op1=ALU.mult)
                    one.mark(last)
                    v.tensor_tensor(m[:, :, 1:4, :], m[:, :, 1:4, :], outer[:], ALU.add)
                    one.wait()
                    v.scalar_tensor_tensor(out=m[:, :, 0, :], in0=tmp_b[:], scalar=INV3, in1=m[:, :, 0, :],
                                           op0=ALU.mult, op1=ALU.add).then_inc(e2["message"].sem, 1)
                    one.end()

            run(dve, S, 3, e2_step)

            def coefficients(i):
                return poly[:, i].unsqueeze(1).to_broadcast([P, 2, 2, C])

            def both(t):
                return t.unsqueeze(2).to_broadcast([P, 2, 2, C])

            def e3_step(s):
                if s.live(1):
                    norm = one_over(e3, s.slot(1, 2), 2, s, 1)
                if s.live():
                    sums = edge_moments(e3, e3_got, s, 4)
                if s.live(1):
                    minus_mean(e3, norm, s.slot(1, 2), 2)
                if s.live():
                    leads = Chain(dve, e3["chain_c"], 3, s.at())
                    leads.mark(v.tensor_tensor(lead_f[:], msg_in[:, s.slot(0, 4), :, D], pair(pair_no, s),
                                               ALU.is_equal))
                    mean_variance(e3, sums, "stats", 0, s.slot(0, 2), 2)
                if s.live(3):
                    a = s.slot(3, 2)
                    one = Chain(dve, e3["chain_p"], 6, s.at(3))
                    done(dve, e3["a"], s, 3)
                    done(dve, e3["b_turned"], s, 5)
                    A, Q, B = asb[:, a], asq[:, a], bsb[:, a]
                    one.mark(v.tensor_tensor(vv[:], Q[:, :, 1, :], Q[:, :, 2, :], ALU.add))
                if s.live():
                    leads.wait()
                    leads.mark(v.tensor_tensor(pair(lead, s), lead_f[:], pair(last_in_pair, s), ALU.mult))
                if s.live(3):
                    v.tensor_tensor(term[:, 0], coefficients(1), both(A[:, :, 0, :]), ALU.mult)
                    one.wait()
                    one.mark(v.tensor_tensor(vv[:], vv[:], Q[:, :, 3, :], ALU.add))
                if s.live():
                    leads.wait()
                    leads.mark(v.scalar_tensor_tensor(out=sidx_f[:], in0=pair(dst_f, s), scalar=-float(NOWHERE),
                                                      in1=pair(lead, s), op0=ALU.add, op1=ALU.mult))
                if s.live(3):
                    v.tensor_tensor(term[:, 1], coefficients(2), both(Q[:, :, 0, :]), ALU.mult)
                if s.live():
                    leads.wait()
                    v.tensor_scalar(pair(final_idx, s), sidx_f[:], float(NOWHERE), None, ALU.add
                                    ).then_inc(e3["lead"].sem, 1)
                    leads.end()
                if s.live(3):
                    one.wait()
                    one.mark(v.tensor_tensor(term[:, 2], coefficients(3), both(vv[:]), ALU.mult))
                    v.tensor_tensor(tmp_a[:], poly_vv[:].to_broadcast([P, 2, C]), vv[:], ALU.mult)
                    v.tensor_tensor(term[:, 0], term[:, 0], coefficients(0), ALU.add)
                    one.wait()
                    one.mark(v.tensor_tensor(term[:, 1], term[:, 1], term[:, 2], ALU.add))
                    one.wait()
                    one(v.tensor_tensor(term[:, 0], term[:, 0], term[:, 1], ALU.add))
                    v.tensor_tensor(B[:, :, 1:4, :], term[:, 0, :, 1:2, :].to_broadcast([P, 2, 3, C]),
                                    A[:, :, 1:4, :], ALU.mult)
                    one.mark(v.tensor_tensor(tmp_b[:], term[:, 0, :, 0, :], A[:, :, 0, :], ALU.mult))
                    one.wait()
                    v.tensor_tensor(B[:, :, 0, :], tmp_a[:], tmp_b[:], ALU.add).then_inc(e3["b"].sem, 1)
                    one.end()

            run(dve, S, 3, e3_step)

            one = Chain(dve, fs["chain"])
            dve.wait_ge(fs["grams_end"].sem, 1)
            dve.wait_ge(e3["summed"].sem, S)
            v.tensor_copy(g_sb[:, 0, :], gram0[:, 0:C + 1])
            v.tensor_copy(row_sb[:], bank[7][0:1, 0:5 * C])
            v.tensor_copy(g_sb[:, 1, 0:C], gram1[:, 0:C]).then_inc(fs["grams"].sem, 1)
            dve.wait_ge(fs["grams"].sem, 1)
            dve.wait_ge(fs["products"].sem, 2)
            for i in range(2):
                v.tensor_tensor(z_sb[0:C, i, :], sc_twice[0:C, i, :], bank[i][0:C, 0:C], ALU.mult)
            v.tensor_scalar(z_sb[:, 2, :], sc_twice[:, 0, :], g_sb[:, 0, 0:1], None, ALU.mult).then_inc(fs["z"].sem, 1)
            dve.wait_ge(fs["sums"].sem, 1)
            one(v.tensor_copy(slot_sum[:], bank[3][:, 0:5 * C]))
            whole = bank[2]
            v.tensor_tensor(fin[:, 0, :], whole[:, 2 * C:3 * C], slot_sum[:, 4 * C:5 * C], ALU.add)
            v.tensor_tensor(fin[:, 1, :], whole[:, 0:C], slot_sum[:, 0:C], ALU.add)
            v.tensor_tensor(fin[:, 2, :], whole[:, C:2 * C], slot_sum[:, C:2 * C], ALU.add)
            one(v.tensor_tensor(fin[:, 3, :], slot_sum[:, 2 * C:3 * C], slot_sum[:, 3 * C:4 * C], ALU.add))
            v.tensor_scalar(fin[:, 0, :], fin[:, 0, :], 1.0 / N, None, ALU.mult)
            v.tensor_scalar(fin[:, 1, :], fin[:, 1, :], 1.0 / N, None, ALU.mult)
            one(v.tensor_tensor(fin[:, 2, :], fin[:, 2, :], fin[:, 3, :], ALU.add))
            v.tensor_scalar(fin[:, 5, :], fin[:, 2, :], 1.0 / (3 * N), None, ALU.mult)
            one(v.tensor_tensor(fin[:, 4, :], fin[:, 0, :], fin[:, 0, :], ALU.mult))
            v.tensor_tensor(fin[:, 4, :], fin[:, 1, :], fin[:, 4, :], ALU.subtract).then_inc(fs["var"].sem, 2)
            dve.wait_ge(fs["root"].sem, 2)
            one(v.reciprocal(fin[:, 6:8, :], fin[:, 6:8, :]))
            v.tensor_tensor(scale[:, 0, :], fin[:, 6, :], g_b[:, 0, :], ALU.mult)
            for k in range(1, 4):
                last = v.tensor_tensor(scale[:, k, :], fin[:, 7, :], g_b[:, 2, :], ALU.mult)
            one(last)
            one(v.tensor_tensor(bias[:], fin[:, 0, :], scale[:, 0, :], ALU.mult))
            v.tensor_tensor(fin_w[:].rearrange("p a c -> p (a c)"), sc_w[:].rearrange("p a c -> p (a c)"),
                            scale[:].rearrange("p a c -> p (a c)"), ALU.mult)
            one(v.tensor_tensor(bias[:], g_b[:, 1, :], bias[:], ALU.subtract))
            one(v.tensor_copy(bias_f[:, 0, :], bias[0:3, :]))
            three_parts(one, bias_f, bias_bf, bias3).then_inc(fs["weights"].sem, 1)

            def p2_step(s):
                if s.live():
                    landed(dve, y_in, s)
                    done(dve, p2["relu0"], s, 2)
                    sums = moments(p2, "chain_a", 0, [xj(big, s.slot(0, XS), ROW)[:, j, 0:D] for j in range(J)], s)
                    mean_variance(p2, sums, "stats", 0, s.slot(0, 2), J)
                o, x1 = xj(x1b, s.slot(2, 2), D), xj(big, s.slot(2, XS), ROW)

                def add_scalars(q):
                    dve.wait_ge(p2["y"].sem, s.at(2) * 2 + q + 1)
                    y = bank[2 + q][:].rearrange("p (j d) -> p j d", j=2)
                    v.tensor_tensor(o[:, 2 * q:2 * q + 2, 0:C], y[:, :, 0:C], x1[:, 2 * q:2 * q + 2, 0:C], ALU.add)

                def add_vectors(q):
                    y = bank[2 + q][:].rearrange("p (j d) -> p j d", j=2)
                    v.tensor_tensor(o[:, 2 * q:2 * q + 2, C:D].rearrange("p j (c x) -> p j c x", x=3),
                                    y[:, :, C:D].rearrange("p j (x c) -> p j c x", x=3),
                                    x1[:, 2 * q:2 * q + 2, C:D].rearrange("p j (c x) -> p j c x", x=3), ALU.add
                                    ).then_inc(p2["out"].sem, 1)

                if s.live(2):
                    landed(dve, y_out, s, 4)
                    add_scalars(0)
                if s.live():
                    norm = one_over(p2, s.slot(0, 2), J, s, 0)
                if s.live(2):
                    add_vectors(0)
                if s.live():
                    minus_mean(p2, norm, s.slot(0, 2), J)
                if s.live(2):
                    add_scalars(1)
                    add_vectors(1)

            run_groups(dve, 2, p2_step)

            def f_step(s):
                if s.live():
                    a = s.slot(0, 4)
                    one = Chain(dve, f["chain"], 2, s.at())
                    landed(dve, f_in, s, 0, dmas=2)
                    o, x1, result = f_o[:, a], f_x[:, a], f_rows[a]
                    one.mark(v.tensor_tensor(o, o, scale[:].rearrange("p k c -> p (k c)").unsqueeze(1)
                                             .to_broadcast([P, 2, D]), ALU.mult))
                    landed(dve, f_out, s, 4, dmas=2)
                    v.tensor_tensor(x1[:, :, 0:C], x1[:, :, 0:C], bias[:].unsqueeze(1).to_broadcast([P, 2, C]), ALU.add)
                    one.wait()
                    for i in range(2):
                        last = v.tensor_tensor(result[:, i, C:D].rearrange("p (c x) -> p c x", x=3),
                                               o[:, i, C:D].rearrange("p (x c) -> p c x", x=3),
                                               x1[:, i, C:D].rearrange("p (c x) -> p c x", x=3), ALU.add)
                    one(last)
                    v.tensor_tensor(result[:, :, 0:C], o[:, :, 0:C], x1[:, :, 0:C], ALU.add).then_inc(f["rows"].sem, 1)
                    one.end()

            run(dve, S, 0, f_step)


_INS = ["x", "src", "dst", "edge_attr_16", "edge_attr_4", "L0_gnn_W", "L0_gnn_b", "L1_gnn_W_up0", "L1_gnn_W_up1",
        "L1_gnn_M1", "L1_gnn_M2", "L1_gnn_M3", "L1_gnn_M4", "L1_gnn_W_lin0", "L1_gnn_W_lin1", "L1_gnn_Wsc0",
        "L1_gnn_Wsc1", "L1_gnn_Wc0", "L1_gnn_Wc1", "L1_gnn_WB0", "L1_gnn_WB1", "L1_gnn_gamma0", "L1_gnn_beta0",
        "L1_gnn_gamma1"]


def kernel(**inputs):
    import numpy as _np
    import concourse.bacc as _bacc
    from concourse import mybir as _mybir
    from concourse.bass_utils import run_bass_kernel_spmd as _run

    nc = _bacc.Bacc("TRN2", target_bir_lowering=False, num_devices=1)
    arrays, args = {}, []
    for name in _INS:
        a = _np.ascontiguousarray(inputs[name])
        arrays[f"in_{name}_dram"] = a
        args.append(nc.dram_tensor(f"in_{name}_dram", a.shape, _mybir.dt.from_np(a.dtype), kind="ExternalInput").ap())
    args.append(nc.dram_tensor("out_0_dram", (N, D), _mybir.dt.float32, kind="ExternalOutput").ap())
    build(nc, *args)
    r = _run(nc, [arrays], core_ids=[0])
    return r.results[0]["out_0_dram"]
```
